# Optimizing a Trainium2 kernel written in Bass

```python
import numpy as np
import jax
import jax.numpy as jnp

def _softmax(x, axis=-1):
    return jax.nn.softmax(x, axis=axis)

def _gelu(x):
    return jax.nn.gelu(x, approximate=True)

def _silu(x):
    return jax.nn.silu(x)

def _sigmoid(x):
    return jax.nn.sigmoid(x)

def _layernorm(x, axis=-1, eps=1e-05):
    m = jnp.mean(x, axis=axis, keepdims=True)
    v = jnp.var(x, axis=axis, keepdims=True)
    return (x - m) / jnp.sqrt(v + eps)

def _scatter_add(tgt, idx, src, axis=0):
    return tgt.at[idx].add(src)

def _segment_sum(src, seg, n):
    return jax.ops.segment_sum(src, seg, n)
kernel_name = 'mk_adaln_d1_jaxref_r8_43ea11'

def setup_inputs(seed: int=0):
    np.random.seed(seed)
    _w = jnp.asarray

    def _L0_attn_setup():
        import math
        import jax, jax.numpy as jnp
        import numpy as np
        B, T, D = (2, 256, 256)
        NH, NKV = (32, 8)
        HD = D // NH
        key = jax.random.key(seed)
        kx, kq, kk, kv, ko = jax.random.split(key, 5)
        s = 1.0 / math.sqrt(D)
        return {'x': jax.random.normal(kx, (B, T, D), dtype=jnp.float32), 'wq': jax.random.normal(kq, (D, NH * HD), dtype=jnp.float32) * s, 'wk': jax.random.normal(kk, (D, NKV * HD), dtype=jnp.float32) * s, 'wv': jax.random.normal(kv, (D, NKV * HD), dtype=jnp.float32) * s, 'wo': jax.random.normal(ko, (NH * HD, D), dtype=jnp.float32) * s}
    _L0_attn_in = _L0_attn_setup()

    def _L0_ffn_setup():
        import jax, jax.numpy as jnp
        import numpy as np
        H = 256
        I = 176
        E = 16
        G = 4
        TOPK_GROUP = 2
        K = 4
        SI = 2 * I
        SCALE = 1.0
        NORM = True
        B, S = (4, 64)

        def _swiglu(h):
            g, u = jnp.split(h, 2, axis=-1)
            return jax.nn.silu(g) * u

        def _combine_weights(xt, gate_w):
            T = xt.shape[0]
            scores = jax.nn.softmax(xt @ gate_w.T, axis=-1)
            group_scores = scores.reshape(T, G, E // G).max(axis=-1)
            _, gidx = jax.lax.top_k(group_scores, TOPK_GROUP)
            gmask = jnp.zeros((T, G), bool).at[jnp.arange(T)[:, None], gidx].set(True)
            emask = jnp.repeat(gmask, E // G, axis=1)
            masked = jnp.where(emask, scores, 0.0)
            w, eidx = jax.lax.top_k(masked, K)
            if NORM:
                w = w / (w.sum(-1, keepdims=True) + 1e-20)
            w = w * SCALE
            return jnp.zeros((T, E), xt.dtype).at[jnp.arange(T)[:, None], eidx].add(w)
        key = jax.random.key(seed)
        ks = jax.random.split(key, 6)
        sc = lambda fan_in: 1.0 / np.sqrt(fan_in)
        return {'x': jax.random.normal(ks[0], (B, S, H), jnp.float32), 'gate_w': jax.random.normal(ks[1], (E, H), jnp.float32) * sc(H), 'expert_up_w': jax.random.normal(ks[2], (E, 2 * I, H), jnp.float32) * sc(H), 'expert_down_w': jax.random.normal(ks[3], (E, H, I), jnp.float32) * sc(I), 'shared_up_w': jax.random.normal(ks[4], (2 * SI, H), jnp.float32) * sc(H), 'shared_down_w': jax.random.normal(ks[5], (H, SI), jnp.float32) * sc(SI)}
    _L0_ffn_in = _L0_ffn_setup()
    _L0_c = _w((lambda *s: np.random.randn(*s).astype(np.float32) * 0.05)(4, 256))
    _L0_wmod = _w((lambda *s: np.random.randn(*s).astype(np.float32) * 0.05)(256, 6 * 256) * 256 ** (-0.5))
    _d = {'L0_attn_x': _L0_attn_in['x'], 'L0_attn_wq': _L0_attn_in['wq'], 'L0_attn_wk': _L0_attn_in['wk'], 'L0_attn_wv': _L0_attn_in['wv'], 'L0_attn_wo': _L0_attn_in['wo'], 'L0_ffn_gate_w': _L0_ffn_in['gate_w'], 'L0_ffn_expert_up_w': _L0_ffn_in['expert_up_w'], 'L0_ffn_expert_down_w': _L0_ffn_in['expert_down_w'], 'L0_ffn_shared_up_w': _L0_ffn_in['shared_up_w'], 'L0_ffn_shared_down_w': _L0_ffn_in['shared_down_w'], 'L0_c': _L0_c, 'L0_wmod': _L0_wmod}
    _x0 = _d['L0_attn_x']
    _d['L0_attn_x'] = jax.random.normal(jax.random.fold_in(jax.random.key(seed), 1), (4, 512, 256), dtype=_x0.dtype)
    del _x0
    return _d

def reference(L0_attn_x, L0_attn_wq, L0_attn_wk, L0_attn_wv, L0_attn_wo, L0_ffn_gate_w, L0_ffn_expert_up_w, L0_ffn_expert_down_w, L0_ffn_shared_up_w, L0_ffn_shared_down_w, L0_c, L0_wmod):

    def _L0_attn_ref(x, wq, wk, wv, wo):
        import math
        import jax, jax.numpy as jnp
        import numpy as np
        B, T, D = (2, 256, 256)
        NH, NKV = (32, 8)
        HD = D // NH
        bsz, seqlen, _ = x.shape
        q = (x @ wq).reshape(bsz, seqlen, NH, HD).transpose(0, 2, 1, 3)
        k = (x @ wk).reshape(bsz, seqlen, NKV, HD).transpose(0, 2, 1, 3)
        v = (x @ wv).reshape(bsz, seqlen, NKV, HD).transpose(0, 2, 1, 3)
        rep = NH // NKV
        k = jnp.repeat(k, rep, axis=1)
        v = jnp.repeat(v, rep, axis=1)
        att = jnp.einsum('bhqd,bhkd->bhqk', q.astype(jnp.float32), k.astype(jnp.float32)) / math.sqrt(HD)
        mask = jnp.triu(jnp.ones((seqlen, seqlen), dtype=bool), k=1)
        att = jnp.where(mask[None, None, :, :], -jnp.inf, att)
        att = jax.nn.softmax(att, axis=-1)
        y = jnp.einsum('bhqk,bhkd->bhqd', att, v.astype(jnp.float32)).astype(q.dtype)
        y = y.transpose(0, 2, 1, 3).reshape(bsz, seqlen, NH * HD)
        return y @ wo

    def _L0_ffn_ref(x, gate_w, expert_up_w, expert_down_w, shared_up_w, shared_down_w):
        import jax, jax.numpy as jnp
        import numpy as np
        H = 256
        I = 176
        E = 16
        G = 4
        TOPK_GROUP = 2
        K = 4
        SI = 2 * I
        SCALE = 1.0
        NORM = True
        B, S = (4, 64)

        def _swiglu(h):
            g, u = jnp.split(h, 2, axis=-1)
            return jax.nn.silu(g) * u

        def _combine_weights(xt, gate_w):
            T = xt.shape[0]
            scores = jax.nn.softmax(xt @ gate_w.T, axis=-1)
            group_scores = scores.reshape(T, G, E // G).max(axis=-1)
            _, gidx = jax.lax.top_k(group_scores, TOPK_GROUP)
            gmask = jnp.zeros((T, G), bool).at[jnp.arange(T)[:, None], gidx].set(True)
            emask = jnp.repeat(gmask, E // G, axis=1)
            masked = jnp.where(emask, scores, 0.0)
            w, eidx = jax.lax.top_k(masked, K)
            if NORM:
                w = w / (w.sum(-1, keepdims=True) + 1e-20)
            w = w * SCALE
            return jnp.zeros((T, E), xt.dtype).at[jnp.arange(T)[:, None], eidx].add(w)
        Bq, Sq, _ = x.shape
        xt = x.reshape(-1, H)
        cw = _combine_weights(xt, gate_w)
        out = jnp.zeros_like(xt)
        for e in range(E):
            a = _swiglu(xt @ expert_up_w[e].T)
            out = out + cw[:, e:e + 1] * (a @ expert_down_w[e].T)
        out = out + _swiglu(xt @ shared_up_w.T) @ shared_down_w.T
        return out.reshape(Bq, Sq, H)
    x = L0_attn_x
    mod = (_silu(L0_c) @ L0_wmod).reshape(L0_c.shape[0], 6, 1, -1)
    sa, ca, ga, sb, cb, gb = (mod[:, 0], mod[:, 1], mod[:, 2], mod[:, 3], mod[:, 4], mod[:, 5])
    ga = (2 * (ga >= 0) - 1) * jnp.maximum(jnp.abs(ga), 0.25)
    gb = (2 * (gb >= 0) - 1) * jnp.maximum(jnp.abs(gb), 0.25)
    h = _layernorm(x, axis=-1) * (1 + ca) + sa
    x = x + ga * _L0_attn_ref(h, L0_attn_wq, L0_attn_wk, L0_attn_wv, L0_attn_wo)
    h = _layernorm(x, axis=-1) * (1 + cb) + sb
    x = x + gb * _L0_ffn_ref(h, L0_ffn_gate_w, L0_ffn_expert_up_w, L0_ffn_expert_down_w, L0_ffn_shared_up_w, L0_ffn_shared_down_w)
    return x

_drawn_inputs = setup_inputs


def setup_inputs(seed=0):
    import zlib

    import numpy as np

    out = dict(_drawn_inputs(seed))
    spreads = {}
    factors = {}
    for name, (base, spread) in spreads.items():
        noise = np.random.default_rng([zlib.crc32(name.encode()), seed]).standard_normal(out[name].shape)
        drawn = base * np.exp(spread * noise) if base else spread * noise
        out[name] = jnp.asarray(drawn.astype(out[name].dtype))
    for name, factor in factors.items():
        out[name] = (out[name] * factor).astype(out[name].dtype)
    return out
```

```python
from contextlib import ExitStack

import concourse.bass as bass
from concourse import mybir

P = 128
ALU = mybir.AluOpType
ACT = mybir.ActivationFunctionType
AX = mybir.AxisListType
F32 = mybir.dt.float32
BF16 = mybir.dt.bfloat16

B, T, D = 4, 512, 256
NH, NKV, HD = 32, 8, 8
REP = NH // NKV
DC = D // P
QT = T // P
NT = B * QT
GH = NKV // 2
HH = NH // 2
E, I = 16, 176
NE = E + 2
G, TOPG, TOPK = 4, 2, 4
I1 = I - P
LO = 64
PARTS = 3
KR = 96
MROW = 24
EPS = 1e-5
NEG = -1e30
SCALE = float(HD) ** -0.5

S_UNITS = [GH * n for n in (1, 2, 4, 4)]
E_UNITS = [GH * n for n in (1, 1, 2, 2)]
SA, CA, GA, SB, CB, GB = (DC * n for n in range(6))


def adaln_block(nc, x, wq, wk, wv, wo, gate_t, up_t, down_t, c_t, wmod, out):
    q_parts = nc.dram_tensor("q_parts", (B, 2, PARTS, QT, HD, HH, P), BF16, kind="Internal").ap()
    k_parts = nc.dram_tensor("k_parts", (B, 2, PARTS, HD, GH, T), BF16, kind="Internal").ap()

    with ExitStack() as ctx:
        def sb(name, shape, dt=F32):
            return ctx.enter_context(nc.sbuf_tensor(name, shape, dt))

        def sem(name):
            return ctx.enter_context(nc.semaphore(name))

        bank = ctx.enter_context(nc.psum_tensor("bank", [P, 8, 512], F32))

        ident = sb("ident", [P, P])
        ident_bf = sb("ident_bf", [P, P], BF16)
        mask_qk = sb("mask_qk", [P, REP, P], BF16)
        mask_kq = sb("mask_kq", [P, REP, P], BF16)
        earlier = sb("earlier", [P, E, E])
        eps = sb("eps", [P, 1])
        X = sb("X", [P, NT, D])
        gate_bc = sb("gate_bc", [P, B, 2, D])
        mod = sb("mod", [P, 6 * DC, B])
        V = sb("V", [P, NT, NKV, 32])
        wo_sb = sb("wo_sb", [P, 2, REP, D])
        ln_st = sb("ln_st", [P, QT, 6])
        ln_mv = sb("ln_mv", [P, QT, 2])
        ln_sd = sb("ln_sd", [P, QT])
        ln_rs = sb("ln_rs", [P, QT])
        xn = sb("xn", [P, QT, D])
        pool = sb("pool", [P, 2, 4 * GH, T])

        Q = [sb(f"Q{s}", [P, QT, HH, P], BF16) for s in range(2)]
        K = [sb(f"K{s}", [P, GH, T], BF16) for s in range(2)]
        K0 = [sb(f"K0{s}", [P, GH, T], BF16) for s in range(2)]
        Vc = [sb(f"Vc{s}", [P, QT, GH, 32]) for s in range(2)]
        negm = [sb(f"negm{s}", [P, QT, HH]) for s in range(2)]
        nm_row = sb("nm_row", [HH, P])
        nm_row2 = sb("nm_row2", [HH, P])
        nm_res = sb("nm_res", [HH, P])
        nm_parts = [sb(f"nm_parts{i}", [HH, PARTS, P], BF16) for i in range(2)]
        den = sb("den", [P, REP * P])
        rden = sb("rden", [P, REP * P])
        Y = [sb(f"Y{s}", [P, REP, T]) for s in range(2)]
        prod = sb("prod", [P, D])

        flat = pool[:, :, :, :].rearrange("p a b c -> p (a b c)")

        def carve(at, n):
            return flat[:, at:at + n]
        wmod_sb = carve(0, DC * 6 * D).rearrange("p (c n) -> p c n", c=DC)
        wq_sb = carve(3072, DC * D).rearrange("p (c n) -> p c n", c=DC)
        wk_sb = carve(3584, DC * 64).rearrange("p (c n) -> p c n", c=DC)
        wv_sb = carve(3712, DC * 64).rearrange("p (c n) -> p c n", c=DC)
        c_sb = carve(3840, DC * B).rearrange("p (c b) -> p c b", c=DC)
        sc_sb = carve(3848, DC * B).rearrange("p (c b) -> p c b", c=DC)
        sc_bc = carve(3856, DC * B * P).rearrange("p (c b n) -> p c b n", c=DC, b=B)
        gtmp = carve(4880, 2 * D).rearrange("p (a n) -> p a n", a=2)
        gsgn = carve(5392, 2 * D).rearrange("p (a n) -> p a n", a=2)
        hT = carve(5904, DC * T).rearrange("p (c n) -> p c n", c=DC)
        res = carve(6928, 3 * T).rearrange("p (a n) -> p a n", a=3)
        parts = carve(8464, 3 * PARTS * T // 2).bitcast(BF16).rearrange("p (a j n) -> p a j n", a=3, j=PARTS)

        h2T = carve(0, DC * B * T).rearrange("p (c n) -> p c n", c=DC)
        acc = carve(4096, NT * D).rearrange("p (t n) -> p t n", t=NT)
        wu_sb = [carve(8192 + i * 704, 704).rearrange("p (c n) -> p c n", c=DC) for i in range(2)]
        wd_sb = [carve(9600 + i * 512, 512).rearrange("p (c n) -> p c n", c=2) for i in range(2)]
        sg = [carve(10624 + i * 1024, 1024).rearrange("p (c n) -> p c n", c=2) for i in range(2)]
        aT = [carve(12672 + i * 1024, 1024).rearrange("p (c n) -> p c n", c=2) for i in range(2)]
        gate_sb = carve(14720, DC * E).rearrange("p (c n) -> p c n", c=DC)
        lgT = carve(14752, T)
        logit = sb("logit", [P, NT, E])
        score = sb("score", [P, NT, E])
        cw = sb("cw", [P, NT, NE])
        small = sb("small", [P, 8, NT, E])
        cmp = Y[0][:, :, :].rearrange("p a b -> p (a b)").rearrange("p (t i j) -> p t i j", i=E, j=E)
        cmp2 = Y[1][:, :, :].rearrange("p a b -> p (a b)").rearrange("p (t i j) -> p t i j", i=E, j=E)

        def at(t, i):
            if isinstance(i, int):
                return t[i]
            a, *rest = "abcdefgh"[:len(t.shape) - 1]
            rest = " ".join(rest)
            return t[bass.ds(i, 1)].rearrange(f"o {a} {rest} -> (o {a}) {rest}")

        names = """x_in w_in c_in wo_in const_done silu_c sc_bcast mod_done mod_used gate_mm gate_used v_ones
            ln_stats ln_sdev xn_ready tr_done h_ready qkv_done qkv_high v_done res1 mid_done res2 low_done
            q_out qkv_free
            q_in0 q_in1 k_in0 k_in1 k0_in0 k0_in1 nm_in s_ready s_free st_ready st_free av_done o_free
            misc_ready misc_free nm_copy nm_res_done nm_split den_ready rden_ready y_ready prod_ready x2_ready
            lg_done lg_sb lgt_done lg_ready soft exp_l route wu_in0 wu_in1 up_done silu_done a_ready down_done
            acc_done w_free out_done fin chain pchain achain zero_done""".split()
        s = {n: sem(n) for n in names}

        credits = sb("credits", [P, 16])
        given = [0]

        def credit():
            given[0] += 1
            return credits[:, given[0]:given[0] + 1]

        chained = [0]

        def link(eng, ins):
            chained[0] += 1
            ins.then_inc(s["chain"], 1)
            eng.wait_ge(s["chain"], chained[0])

        def layer_norm(dve, b, base=0):
            for i in range(QT):
                st = nc.vector.bn_stats(ln_st[:, i, :], X[:, bass.ds(b * QT + i, 1), :].rearrange("p o d -> p (o d)"))
            st.then_inc(s["soft"], 1)
            dve.wait_ge(s["soft"], 3 * (b + base) + 1)
            dve.nop(nofuse=True)
            for i in range(QT):
                ag = nc.vector.bn_aggr(ln_mv[:, i, :], ln_st[:, i, :])
            ag.then_inc(s["ln_stats"], 1)
            dve.wait_ge(s["ln_sdev"], b + base + 1)
            nc.vector.reciprocal(ln_rs[:, :], ln_sd[:, :]).then_inc(s["soft"], 2)
            dve.wait_ge(s["soft"], 3 * (b + base) + 3)
            for i in range(QT):
                last = nc.vector.tensor_scalar(xn[:, i, :], X[:, bass.ds(b * QT + i, 1), :].rearrange("p o d -> p (o d)"),
                                               ln_mv[:, i, 0:1], ln_rs[:, i:i + 1], ALU.subtract, ALU.mult)
            last.then_inc(s["xn_ready"], 1)

        with nc.Block() as block:
            @block.sync
            def _(sp):
                sp.dma_start(c_sb, c_t.rearrange("(c p) b -> p c b", p=P)).then_inc(s["c_in"], 16)
                sp.dma_start(wmod_sb, wmod.rearrange("(c p) n -> p c n", p=P)).then_inc(s["c_in"], 16)
                sp.dma_start(X[:, :, :], x.rearrange("b (t p) d -> p (b t) d", p=P)).then_inc(s["x_in"], 16)
                sp.dma_start(wq_sb, wq.rearrange("(c p) n -> p c n", p=P)).then_inc(s["w_in"], 16)
                sp.dma_start(wk_sb, wk.rearrange("(c p) n -> p c n", p=P)).then_inc(s["w_in"], 16)
                sp.dma_start(wv_sb, wv.rearrange("(c p) n -> p c n", p=P)).then_inc(s["w_in"], 16)
                sp.wait_ge(s["zero_done"], 1)
                wo_v = wo.rearrange("(s g h d) n -> g d s h n", s=2, g=GH, h=REP)
                for g in range(GH):
                    for h in range(2):
                        sp.dma_start(wo_sb[32 * g:32 * g + HD, h, :, :], wo_v[g, :, h]).then_inc(s["wo_in"], 16)

                def store(b):
                    sp.wait_ge(s["low_done"], 1 * b + 1)
                    sp.nop(nofuse=True)
                    for h in range(2):
                        for j in range(PARTS):
                            sp.dma_start(at(q_parts, b)[h, j].rearrange("q d h t -> (d h) q t"),
                                         parts[:, h, j, :].rearrange("p (q t) -> p q t", q=QT)
                                         ).then_inc(s["q_out"], 16)
                        sp.dma_start(at(k_parts, b)[h].rearrange("j d g t -> (d g) j t"),
                                     parts[32 * h:32 * h + 32, 2, :, :]).then_inc(s["q_out"], 16)
                with sp.Fori(0, B) as b:
                    store(b)
                    sp.wait_ge(s["q_out"], 16 * 8 * b + 16 * 9)
                    sp.nop(nofuse=True)

            @block.gpsimd
            def _(gp):
                n = [0]

                def step(ins):
                    n[0] += 1
                    ins.then_inc(s["pchain"], 1)
                    gp.wait_ge(s["pchain"], n[0])
                step(nc.gpsimd.memset(ident[:, :], 0.0))
                step(nc.gpsimd.memset(mask_qk[:, :, :], 0.0))
                step(nc.gpsimd.memset(mask_kq[:, :, :], 0.0))
                step(nc.gpsimd.memset(earlier[:, :, :], 1.0))
                step(nc.gpsimd.affine_select(out=ident[:, :], in_=ident[:, :], compare_op=ALU.not_equal, fill=1.0,
                                             base=0, pattern=[[-1, P]], channel_multiplier=1))
                step(nc.gpsimd.tensor_copy(ident_bf[:, :], ident[:, :]))
                step(nc.gpsimd.affine_select(out=mask_qk[:, :, :], in_=mask_qk[:, :, :], compare_op=ALU.is_ge,
                                             fill=NEG, base=0, pattern=[[0, REP], [-1, P]], channel_multiplier=1))
                step(nc.gpsimd.affine_select(out=mask_kq[:, :, :], in_=mask_kq[:, :, :], compare_op=ALU.is_ge,
                                             fill=NEG, base=0, pattern=[[0, REP], [1, P]], channel_multiplier=-1))
                nc.gpsimd.affine_select(out=earlier[:, :, :], in_=earlier[:, :, :], compare_op=ALU.is_gt,
                                        fill=0.0, base=0, pattern=[[1, E], [-1, E]],
                                        channel_multiplier=0).then_inc(s["const_done"], 1)

                with gp.Fori(0, B) as b:
                    gp.wait_ge(s["res1"], b + 1)
                    gp.nop(nofuse=True)
                    nc.gpsimd.tensor_copy(parts[:, :, 1, :], res).then_inc(s["mid_done"], 1)
                    gp.wait_ge(s["mid_done"], b + 1)
                    nc.gpsimd.tensor_tensor(parts[:, :, 2, :], res, parts[:, :, 1, :],
                                            ALU.subtract).then_inc(s["low_done"], 1)

            @block.scalar
            def _(act):
                act.wait_ge(s["c_in"], 32)
                nc.scalar.activation(sc_sb, c_sb, ACT.Silu).then_inc(s["silu_c"], 1)
                with act.Fori(0, B) as b:
                    act.wait_ge(s["ln_stats"], b + 1)
                    nc.scalar.activation(ln_sd[:, :], ln_mv[:, :, 1], ACT.Sqrt,
                                         bias=eps[:, :]).then_inc(s["ln_sdev"], 1)
                    act.wait_ge(s["tr_done"], b + 1)
                    for c in range(DC):
                        nc.scalar.activation(hT[:, c, :], bank[:, c, :], ACT.Identity,
                                             bias=mod[:, SA + c, bass.ds(b, 1)],
                                             scale=mod[:, CA + c, bass.ds(b, 1)]).then_inc(s["h_ready"], 1)
                    act.wait_ge(s["qkv_done"], b + 1)
                    act.wait_ge(s["q_out"], 16 * 8 * b + 16)
                    nc.scalar.activation(parts[:, 0:2, 0, :], bank[:, 2:4, :], ACT.Copy).then_inc(s["qkv_high"], 1)
                    nc.scalar.activation(parts[0:64, 2, 0, :], bank[0:64, 4, :], ACT.Copy).then_inc(s["qkv_high"], 1)
                    nc.scalar.activation(V[:, bass.ds(b * QT, QT), :, 0:HD],
                                         bank[:, 5, 0:QT * 64].rearrange("p (t g d) -> p t g d", t=QT, g=NKV),
                                         ACT.Copy).then_inc(s["v_done"], 1)

            @block.vector
            def _(dve):
                nc.vector.memset(wo_sb[:, :, :, :], 0.0).then_inc(s["zero_done"], 1)
                nc.vector.memset(eps[:, :], EPS).then_inc(s["q_out"], 16)
                dve.wait_ge(s["q_out"], 16)
                link(dve, nc.vector.memset(V[:, :, :, :], 1.0))
                link(dve, nc.vector.memset(res, 0.0))
                for h in range(2):
                    link(dve, nc.vector.memset(Q[h][:, :, :, :], 0.0))
                    link(dve, nc.vector.memset(K[h][:, :, :], 1.0))
                    link(dve, nc.vector.memset(K0[h][:, :, :], 0.0))
                dve.wait_ge(s["silu_c"], 1)
                nc.vector.tensor_copy(sc_bc, sc_sb.unsqueeze(3).to_broadcast([P, DC, B, P])).then_inc(s["sc_bcast"], 1)
                dve.wait_ge(s["mod_done"], 1)
                mod_ps = bank[:, 7, 0:6 * DC * B].rearrange("p (m b) -> p m b", b=B)
                link(dve, nc.vector.tensor_copy(mod[:, :, :], mod_ps))
                for m in (CA, CB):
                    link(dve, nc.vector.tensor_scalar(mod[:, m:m + DC, :], mod[:, m:m + DC, :], 1.0, None, ALU.add))
                for b in range(B):
                    dve.wait_ge(s["gate_mm"], b + 1)
                    g_ps = bank[:, b, :].rearrange("p (a n) -> p a n", a=2)
                    link(dve, nc.vector.tensor_scalar(gtmp, g_ps, -1.0, 0.25, ALU.mult, ALU.max))
                    link(dve, nc.vector.tensor_tensor(gtmp, g_ps, gtmp, ALU.max))
                    link(dve, nc.vector.tensor_scalar(gsgn, g_ps, 0.0, 2.0, ALU.is_ge, ALU.mult))
                    nc.vector.scalar_tensor_tensor(out=gate_bc[:, b], in0=gsgn, scalar=-1.0, in1=gtmp,
                                                   op0=ALU.add, op1=ALU.mult).then_inc(s["gate_used"], 1)
                    dve.wait_ge(s["gate_used"], b + 1)
                dve.wait_ge(s["x_in"], 16)
                with dve.Fori(0, B) as b:
                    layer_norm(dve, b)
                    dve.wait_ge(s["qkv_high"], 2 * b + 2)
                    nc.vector.tensor_tensor(res[:, 0:2, :], bank[:, 2:4, :], parts[:, 0:2, 0, :], ALU.subtract)
                    nc.vector.tensor_tensor(res[0:64, 2, :], bank[0:64, 4, :], parts[0:64, 2, 0, :],
                                            ALU.subtract).then_inc(s["res1"], 1)

            @block.tensor
            def _(pe):
                pe.wait_ge(s["c_in"], 32)
                pe.wait_ge(s["silu_c"], 1)
                for m in range(6 * DC):
                    for c in range(DC):
                        last = nc.tensor.matmul(bank[:, 7, m * B:m * B + B], wmod_sb[:, c, m * P:m * P + P],
                                                sc_sb[:, c, :], start=(c == 0), stop=(c == DC - 1),
                                                skip_group_check=True)
                last.then_inc(s["mod_done"], 1)
                pe.wait_ge(s["sc_bcast"], 1)
                for b in range(B):
                    for a, m in enumerate((GA, GB)):
                        for c in range(DC):
                            last = nc.tensor.matmul(bank[:, b, a * D:a * D + D], sc_bc[:, c, b, :],
                                                    wmod_sb[:, c, m * P:m * P + D], start=(c == 0),
                                                    stop=(c == DC - 1), skip_group_check=True)
                    last.then_inc(s["gate_mm"], 1)
                pe.wait_ge(s["const_done"], 1)
                pe.wait_ge(s["w_in"], 48)
                pe.wait_ge(s["gate_used"], B)
                with pe.Fori(0, B) as b:
                    pe.wait_ge(s["xn_ready"], b + 1)
                    for c in range(DC):
                        for i in range(QT):
                            last = nc.tensor.transpose(bank[:, c, i * P:i * P + P], xn[:, i, c * P:c * P + P], ident[:, :])
                    last.then_inc(s["tr_done"], 1)
                    pe.wait_ge(s["h_ready"], DC * b + DC)
                    for m in range(2):
                        for c in range(DC):
                            nc.tensor.matmul(bank[:, 2 + m, :], wq_sb[:, c, m * P:m * P + P], hT[:, c, :],
                                             start=(c == 0), stop=(c == DC - 1))
                    for c in range(DC):
                        nc.tensor.matmul(bank[0:64, 4, :], wk_sb[:, c, :], hT[:, c, :],
                                         start=(c == 0), stop=(c == DC - 1))
                    for i in range(QT):
                        for c in range(DC):
                            last = nc.tensor.matmul(bank[:, 5, i * 64:i * 64 + 64], hT[:, c, i * P:i * P + P],
                                                    wv_sb[:, c, :], start=(c == 0), stop=(c == DC - 1),
                                                    skip_group_check=True)
                    last.then_inc(s["qkv_done"], 1)
                    pe.wait_ge(s["v_done"], b + 1)
                    pe.wait_ge(s["res1"], b + 1)

        E_END = [sum(E_UNITS[:q + 1]) for q in range(QT)]
        E_TOT, S_TOT = sum(E_UNITS), sum(S_UNITS)
        S_AT = {(q, g): sum(S_UNITS[:q]) + g * S_UNITS[q] // GH for q in range(QT) for g in range(GH)}
        E_AT = {(q, g): sum(E_UNITS[:q]) + g * E_UNITS[q] // GH for q in range(QT) for g in range(GH)}
        T_USE = {0: {0: 0, 1: 1, 2: 2, 3: 3}, 1: {0: 4, 1: 5, 2: 7, 3: 9}}
        WO_USE = {0: 6, 1: 8, 2: 10, 3: 11}
        WO_USE_LAST = {0: 4, 1: 5, 2: 6, 3: 7}
        MISC, OBANK = 7, 6
        q_in = [[sem(f"q_in{h}_{q}") for q in range(QT)] for h in range(2)]
        k_in = [s["k_in0"], s["k_in1"]]
        k0_in = [s["k0_in0"], s["k0_in1"]]
        nm_in = [sem("nm_in_even"), sem("nm_in_odd")]
        nm_rows = [nm_row, nm_row2]

        def s_banks(q):
            n = (q + 1) * P
            return {0: 4, 1: 2, 2: 1, 3: 1}[q], n

        with nc.Block() as block:
            @block.sync
            def _(sp):
                def load_q(b, h, q):
                    for j in range(PARTS):
                        for r in range(PARTS):
                            row = 32 * j + HD * r
                            sp.dma_start(Q[h][row:row + HD, q, :, :],
                                         at(q_parts, b)[h, j, q]).then_inc(q_in[h][q], 16)

                def load_k0(b, h):
                    for j in range(PARTS):
                        sp.dma_start(K0[h][32 * j:32 * j + MROW, :, :],
                                     at(k_parts, b)[h].rearrange("j d g t -> (j d) g t")).then_inc(k0_in[h], 16)

                def load_kv(b, h):
                    for j in range(PARTS):
                        sp.dma_start(K[h][32 * j:32 * j + MROW, :, :],
                                     at(k_parts, b)[h].rearrange("j d g t -> (j d) g t")).then_inc(k_in[h], 16)
                    sp.dma_start(Vc[h][:, :, :, :],
                                 V[:, bass.ds(b * QT, QT), h * GH:h * GH + GH, :]).then_inc(k_in[h], 16)

                def put_negm(u, h, q):
                    sp.wait_ge(s["nm_split"], 8 + 16 * u + 4 * q + 4)
                    sp.nop(nofuse=True)
                    for j in range(PARTS):
                        sp.dma_start(Q[h][32 * j + MROW:32 * j + MROW + 1, q, :, :],
                                     nm_parts[q % 2][:, j, :]).then_inc(nm_in[q % 2], 16)

                def half(b, h, loads, nxt):
                    u = 2 * b + h
                    if loads:
                        sp.wait_ge(s["s_ready"], S_TOT * u + S_TOT)
                        sp.nop(nofuse=True)
                        load_k0(b + 1, h)
                    if nxt:
                        sp.wait_ge(s["av_done"], 2 + 4 * u)
                        sp.nop(nofuse=True)
                        load_kv(b + h, 1 - h)
                    for q in range(QT):
                        if nxt and q > 0:
                            put_negm(u + 1, 1 - h, q - 1)
                        if loads:
                            sp.wait_ge(s["st_ready"], E_TOT * u + E_END[q])
                            sp.nop(nofuse=True)
                            load_q(b + 1, h, q)
                    if nxt:
                        put_negm(u + 1, 1 - h, QT - 1)

                for q in range(QT):
                    load_q(0, 0, q)
                load_k0(0, 0)
                load_kv(0, 0)
                load_k0(0, 1)
                for q in range(QT):
                    load_q(0, 1, q)
                for q in range(QT):
                    put_negm(0, 0, q)
                with sp.Fori(0, B - 1) as b:
                    half(b, 0, True, True)
                    half(b, 1, True, True)
                half(B - 1, 0, False, True)

            @block.tensor
            def _(pe):
                def scores_for_max(b, h, q, g):
                    u = 2 * b + h
                    if g == 0:
                        pe.wait_ge(q_in[h][q], 16 * 9 * b + 16 * 9)
                        if q == 0:
                            pe.wait_ge(k0_in[h], 16 * 3 * b + 16 * 3)
                    heads, n = s_banks(q)
                    for k in range(REP // heads):
                        unit = S_TOT * u + S_AT[q, g] + k
                        buf = (S_AT[q, g] + k) % 2
                        pe.wait_ge(s["s_free"], unit + 1)
                        for i in range(heads):
                            nc.tensor.matmul(bank[:, buf, i * n:i * n + n],
                                             Q[h][0:KR, q, g * REP + k * heads + i, :], K0[h][0:KR, g, 0:n],
                                             start=(i == 0), stop=False, skip_group_check=True)
                        view = bank[:, buf, 0:heads * n].rearrange("p (i n) -> p i n", i=heads)
                        nc.tensor.matmul(view[:, :, n - P:n], ident_bf[:, :], mask_qk[:, 0:heads, :],
                                         start=False, stop=True, skip_group_check=True).then_inc(s["s_ready"], 1)

                def scores(b, h, q, g):
                    u = 2 * b + h
                    if g == 0:
                        pe.wait_ge(nm_in[q % 2], 16 + 48 * (2 * u + q // 2) + 48)
                        if q == 0:
                            pe.wait_ge(k_in[h], 16 * 4 * b + 16 * 4)
                    for k, kt in enumerate(range(0, q + 1, 2)):
                        unit = E_TOT * u + E_AT[q, g] + k
                        buf = 2 + 2 * ((E_AT[q, g] + k) % 2)
                        pe.wait_ge(s["st_free"], unit + 1)
                        for i in range(min(2, q + 1 - kt)):
                            last = nc.tensor.matmul(bank[:, buf + i, :], K[h][0:KR, g, (kt + i) * P:(kt + i + 1) * P],
                                                    Q[h][0:KR, q, g * REP:g * REP + REP, :],
                                                    start=True, stop=(kt + i < q), skip_group_check=True)
                            if kt + i == q:
                                last = nc.tensor.matmul(bank[:, buf + i, :], ident_bf[:, :], mask_kq[:, :, :],
                                                        start=False, stop=True, skip_group_check=True)
                        last.then_inc(s["st_ready"], 1)

                def weigh_values(b, h, q):
                    u = 2 * b + h
                    m = 4 * u + q
                    pe.wait_ge(s["st_free"], 2 + E_TOT * u + E_END[q])
                    pe.wait_ge(s["o_free"], m + 1)
                    for kt in range(q + 1):
                        for g in range(GH):
                            last = nc.tensor.matmul(bank[32 * g:32 * g + 32, OBANK, :], Vc[h][:, kt, g, :],
                                                    pool[:, q % 2, g * QT + kt, :], start=(kt == 0), stop=(kt == q),
                                                    skip_group_check=True)
                    last.then_inc(s["av_done"], 1)

                def turn_max(b, h, q, use):
                    u = 2 * b + h
                    pe.wait_ge(s["s_free"], 2 + S_TOT * u + sum(S_UNITS[:q + 1]))
                    pe.wait_ge(s["misc_free"], use + 1)
                    nc.tensor.transpose(bank[0:HH, MISC, 0:P], negm[h][:, q, :], ident[:, :]).then_inc(s["misc_ready"], 1)

                def project(b, q, use):
                    pe.wait_ge(s["o_free"], 1 + 4 * (2 * b + 1) + q + 1)
                    pe.wait_ge(s["misc_free"], use + 1)
                    for h in range(2):
                        for r in range(REP):
                            last = nc.tensor.matmul(bank[:, MISC, 0:D], Y[h][:, r, q * P:q * P + P],
                                                    wo_sb[:, h, r, :], start=(h == 0 and r == 0),
                                                    stop=(h == 1 and r == REP - 1))
                    last.then_inc(s["misc_ready"], 1)

                def half(b, h, nxt, wo_use):
                    b1, h1 = b + h, 1 - h
                    base = 4 + 12 * b
                    for q in range(QT):
                        for g in range(GH):
                            scores(b, h, q, g)
                            if nxt:
                                scores_for_max(b1, h1, q, g)
                            if g == 1 and q > 0:
                                weigh_values(b, h, q - 1)
                            if g == 2 and q > 0 and nxt:
                                turn_max(b1, h1, q - 1, base + T_USE[h][q - 1])
                            if g == 3 and h == 1 and q >= 2:
                                project(b, q - 2, base + wo_use[q - 2])
                    weigh_values(b, h, QT - 1)
                    if nxt:
                        turn_max(b1, h1, QT - 1, base + T_USE[h][QT - 1])
                    if h == 1:
                        for q in range(QT - 2, QT):
                            project(b, q, base + wo_use[q])

                for q in range(QT):
                    for g in range(GH):
                        scores_for_max(0, 0, q, g)
                    turn_max(0, 0, q, q)
                with pe.Fori(0, B - 1) as b:
                    half(b, 0, True, WO_USE)
                    half(b, 1, True, WO_USE)
                half(B - 1, 0, True, WO_USE)
                half(B - 1, 1, False, WO_USE_LAST)

            @block.scalar
            def _(act):
                def half(b, h):
                    u = 2 * b + h
                    for q in range(QT):
                        act.wait_ge(s["av_done"], 4 * u + q + 1)
                        for g in range(GH):
                            for k, kt in enumerate(range(0, q + 1, 2)):
                                unit = E_TOT * u + E_AT[q, g] + k
                                buf = 2 + 2 * ((E_AT[q, g] + k) % 2)
                                n = min(2, q + 1 - kt)
                                act.wait_ge(s["st_ready"], unit + 1)
                                nc.scalar.activation(pool[:, q % 2, g * QT + kt:g * QT + kt + n, :],
                                                     bank[:, buf:buf + n, :], ACT.Exp,
                                                     scale=SCALE).then_inc(s["st_free"], 1)
                with act.Fori(0, B) as b:
                    half(b, 0)
                    half(b, 1)

            @block.gpsimd
            def _(gp):
                def split(u, q, use):
                    t8 = 8 + 16 * u + 4 * q
                    row, to = nm_rows[q % 2], nm_parts[q % 2]
                    gp.wait_ge(s["misc_free"], 1 + use + 1)
                    gp.wait_ge(nm_in[q % 2], 16 + 48 * (2 * u + q // 2))
                    gp.nop(nofuse=True)
                    nc.gpsimd.tensor_copy(to[:, 0, :], row[:, :]).then_inc(s["nm_split"], 1)
                    gp.wait_ge(s["nm_split"], t8 + 1)
                    nc.gpsimd.tensor_tensor(nm_res[:, :], row[:, :], to[:, 0, :], ALU.subtract).then_inc(s["nm_split"], 1)
                    gp.wait_ge(s["nm_split"], t8 + 2)
                    gp.nop(nofuse=True)
                    nc.gpsimd.tensor_copy(to[:, 1, :], nm_res[:, :]).then_inc(s["nm_split"], 1)
                    gp.wait_ge(s["nm_split"], t8 + 3)
                    nc.gpsimd.tensor_tensor(to[:, 2, :], nm_res[:, :], to[:, 1, :], ALU.subtract).then_inc(s["nm_split"], 1)
                    gp.wait_ge(s["nm_split"], t8 + 4)
                for q in range(QT):
                    split(0, q, q)
                with gp.Fori(0, B - 1) as b:
                    for h in range(2):
                        for q in range(QT):
                            split(2 * b + h + 1, q, 4 + 12 * b + T_USE[h][q])
                for q in range(QT):
                    split(2 * B - 1, q, 4 + 12 * (B - 1) + T_USE[0][q])

            @block.vector
            def _(dve):
                for name, n in (("s_free", 2), ("st_free", 2), ("av_done", 2), ("o_free", 1), ("misc_free", 1),
                                ("x2_ready", 1),
                                ("nm_split", 8)):
                    nc.vector.memset(credit(), 0.0).then_inc(s[name], n)
                for one in nm_in:
                    nc.vector.memset(credit(), 0.0).then_inc(one, 16)

                def maxima(b, h, q, g):
                    u = 2 * b + h
                    heads, n = s_banks(q)
                    for k in range(REP // heads):
                        unit = S_TOT * u + S_AT[q, g] + k
                        dve.wait_ge(s["s_ready"], unit + 1)
                        at_ = g * REP + k * heads
                        view = bank[:, (S_AT[q, g] + k) % 2, 0:heads * n].rearrange("p (i n) -> p i n", i=heads)
                        nc.vector.tensor_reduce(negm[h][:, q, at_:at_ + heads], view, AX.X, ALU.max,
                                                negate=True).then_inc(s["s_free"], 1)

                def take_max(b, h, q, use):
                    u = 2 * b + h
                    dve.wait_ge(s["misc_ready"], use + 1)
                    dve.wait_ge(s["nm_split"], 16 * u + 4 * q + 4)
                    nc.vector.tensor_copy(nm_rows[q % 2][:, :], bank[0:HH, MISC, 0:P]).then_inc(s["misc_free"], 1)

                def normalise(b, h, q):
                    m = 4 * (2 * b + h) + q
                    dve.wait_ge(s["av_done"], 2 + m + 1)
                    dve.nop(nofuse=True)
                    nc.vector.stream_shuffle(den[:, :], bank[:, OBANK, :], [HD] * 32).then_inc(s["den_ready"], 1)
                    dve.wait_ge(s["den_ready"], m + 1)
                    nc.vector.reciprocal(rden[:, :], den[:, :]).then_inc(s["rden_ready"], 1)
                    dve.wait_ge(s["rden_ready"], m + 1)
                    nc.vector.tensor_tensor(Y[h][:, :, q * P:q * P + P],
                                            bank[:, OBANK, :].rearrange("p (r t) -> p r t", r=REP),
                                            rden[:, :].rearrange("p (r t) -> p r t", r=REP),
                                            ALU.mult).then_inc(s["o_free"], 1)

                def residual(b, q, use):
                    dve.wait_ge(s["misc_ready"], use + 1)
                    dve.wait_ge(s["x2_ready"], 4 * b + q + 1)
                    g1 = gate_bc[:, bass.ds(b, 1), 0, :].rearrange("p o d -> p (o d)")
                    xt = X[:, bass.ds(b * QT + q, 1), :].rearrange("p o d -> p (o d)")
                    nc.vector.tensor_tensor(prod[:, :], bank[:, MISC, 0:D], g1, ALU.mult).then_inc(s["misc_free"], 1)
                    dve.wait_ge(s["misc_free"], 1 + use + 1)
                    nc.vector.tensor_tensor(xt, xt, prod[:, :], ALU.add).then_inc(s["x2_ready"], 1)

                def half(b, h, nxt, wo_use):
                    b1, h1 = b + h, 1 - h
                    base = 4 + 12 * b
                    for q in range(QT):
                        for g in range(GH):
                            if nxt:
                                maxima(b1, h1, q, g)
                            if g == 1 and q > 0:
                                normalise(b, h, q - 1)
                            if g == 2 and q > 0 and nxt:
                                take_max(b1, h1, q - 1, base + T_USE[h][q - 1])
                            if g == 3 and h == 1 and q >= 2:
                                residual(b, q - 2, base + wo_use[q - 2])
                    normalise(b, h, QT - 1)
                    if nxt:
                        take_max(b1, h1, QT - 1, base + T_USE[h][QT - 1])
                    if h == 1:
                        for q in range(QT - 2, QT):
                            residual(b, q, base + wo_use[q])

                for q in range(QT):
                    for g in range(GH):
                        maxima(0, 0, q, g)
                    take_max(0, 0, q, q)
                with dve.Fori(0, B - 1) as b:
                    half(b, 0, True, WO_USE)
                    half(b, 1, True, WO_USE)
                half(B - 1, 0, True, WO_USE)
                half(B - 1, 1, False, WO_USE_LAST)

        with nc.Block() as block:
            @block.sync
            def _(sp):
                sp.dma_start(gate_sb, gate_t.rearrange("(c p) e -> p c e", p=P)).then_inc(s["wo_in"], 16)

            @block.scalar
            def _(act):
                with act.Fori(0, B) as b:
                    act.wait_ge(s["ln_stats"], B + b + 1)
                    nc.scalar.activation(ln_sd[:, :], ln_mv[:, :, 1], ACT.Sqrt,
                                         bias=eps[:, :]).then_inc(s["ln_sdev"], 1)
                    act.wait_ge(s["tr_done"], B + b + 1)
                    for c in range(DC):
                        nc.scalar.activation(h2T[:, c, bass.ds(b * T, T)], bank[:, c, :], ACT.Identity,
                                             bias=mod[:, SB + c, bass.ds(b, 1)],
                                             scale=mod[:, CB + c, bass.ds(b, 1)]).then_inc(s["h_ready"], 1)
                    act.wait_ge(s["lg_done"], b + 1)
                    nc.scalar.activation(lgT[0:E, :], bank[0:E, 2, :], ACT.Copy).then_inc(s["lg_sb"], 1)
                act.wait_ge(s["soft"], 6 * B + 2)
                nc.scalar.activation(small[:, 1], small[:, 1], ACT.Exp).then_inc(s["exp_l"], 1)

            @block.tensor
            def _(pe):
                pe.wait_ge(s["wo_in"], 16 * 9)
                with pe.Fori(0, B) as b:
                    pe.wait_ge(s["xn_ready"], B + b + 1)
                    for c in range(DC):
                        for i in range(QT):
                            last = nc.tensor.transpose(bank[:, c, i * P:i * P + P], xn[:, i, c * P:c * P + P], ident[:, :])
                    last.then_inc(s["tr_done"], 1)
                    pe.wait_ge(s["h_ready"], DC * (B + b) + DC)
                    for c in range(DC):
                        last = nc.tensor.matmul(bank[0:E, 2, :], gate_sb[:, c, :], h2T[:, c, bass.ds(b * T, T)],
                                                start=(c == 0), stop=(c == DC - 1))
                    last.then_inc(s["lg_done"], 1)
                    pe.wait_ge(s["lg_sb"], b + 1)
                    pe.nop(nofuse=True)
                    for i in range(QT):
                        last = nc.tensor.transpose(bank[:, 3, i * E:i * E + E], lgT[0:E, i * P:i * P + P],
                                                   ident[0:E, 0:E])
                    last.then_inc(s["lgt_done"], 1)
                    pe.wait_ge(s["lg_ready"], b + 1)

            @block.vector
            def _(dve):
                with dve.Fori(0, B) as b:
                    layer_norm(dve, b, B)
                    dve.wait_ge(s["lgt_done"], b + 1)
                    nc.vector.tensor_copy(logit[:, bass.ds(b * QT, QT), :],
                                          bank[:, 3, 0:QT * E].rearrange("p (i e) -> p i e", i=QT)
                                          ).then_inc(s["lg_ready"], 1)
                dve.wait_ge(s["lg_ready"], B)

                n = [0]

                def step(ins):
                    n[0] += 1
                    ins.then_inc(s["route"], 1)
                    dve.wait_ge(s["route"], n[0])

                def over(a, k):
                    return a.unsqueeze(2).to_broadcast([P, NT, k])

                mx, ex, gm, gsel, msk, rank, tot, rec = (small[:, i] for i in range(8))
                step(nc.vector.tensor_reduce(tot[:, :, 0], logit[:, :, :], AX.X, ALU.max))
                nc.vector.tensor_tensor(ex, logit[:, :, :], over(tot[:, :, 0], E),
                                        ALU.subtract).then_inc(s["soft"], 2)
                dve.wait_ge(s["exp_l"], 1)
                step(nc.vector.tensor_reduce(tot[:, :, 1], ex, AX.X, ALU.add))
                step(nc.vector.reciprocal(tot[:, :, 2], tot[:, :, 1]))
                step(nc.vector.tensor_tensor(score[:, :, :], ex, over(tot[:, :, 2], E), ALU.mult))

                def before(v, t0, nt, k, to, gt, eq):
                    mine = v[:, t0:t0 + nt, 0:k].unsqueeze(3).to_broadcast([P, nt, k, k])
                    other = v[:, t0:t0 + nt, 0:k].unsqueeze(2).to_broadcast([P, nt, k, k])
                    tri = earlier[:, 0:k, 0:k].unsqueeze(1).to_broadcast([P, nt, k, k])
                    g_, e_ = gt[:, 0:nt, 0:k, 0:k], eq[:, 0:nt, 0:k, 0:k]
                    step(nc.vector.tensor_tensor(g_, other, mine, ALU.is_gt))
                    step(nc.vector.tensor_tensor(e_, other, mine, ALU.is_equal))
                    step(nc.vector.tensor_tensor(e_, e_, tri, ALU.mult))
                    step(nc.vector.tensor_tensor(g_, g_, e_, ALU.add))
                    step(nc.vector.tensor_reduce(to[:, t0:t0 + nt, 0:k], g_, AX.X, ALU.add))

                step(nc.vector.tensor_reduce(gm[:, :, 0:G], score[:, :, :].rearrange("p t (g e) -> p t g e", g=G),
                                             AX.X, ALU.max))
                for t0 in range(0, NT, 8):
                    before(gm, t0, 8, G, rank, cmp, cmp2)
                step(nc.vector.tensor_scalar(gsel[:, :, 0:G], rank[:, :, 0:G], float(TOPG), None, ALU.is_lt))
                for g in range(G):
                    w = E // G
                    step(nc.vector.tensor_tensor(msk[:, :, g * w:g * w + w], score[:, :, g * w:g * w + w],
                                                 over(gsel[:, :, g], w), ALU.mult))
                for t0 in range(0, NT, 8):
                    before(msk, t0, 8, E, rank, cmp, cmp2)
                step(nc.vector.tensor_scalar(rank, rank, float(TOPK), None, ALU.is_lt))
                step(nc.vector.tensor_tensor(msk, msk, rank, ALU.mult))
                step(nc.vector.tensor_reduce(tot[:, :, 3], msk, AX.X, ALU.add))
                step(nc.vector.tensor_scalar(tot[:, :, 4], tot[:, :, 3], 1e-20, None, ALU.add))
                step(nc.vector.reciprocal(tot[:, :, 5], tot[:, :, 4]))
                step(nc.vector.memset(cw[:, :, E:NE], 1.0))
                step(nc.vector.tensor_tensor(cw[:, :, 0:E], msk, over(tot[:, :, 5], E), ALU.mult))
                step(nc.vector.memset(acc, 0.0))

        wu_in = [s["wu_in0"], s["wu_in1"]]
        with nc.Block() as block:
            @block.sync
            def _(sp):
                def load(e, i):
                    sp.dma_start(wu_sb[i], at(up_t, e).rearrange("(c p) n -> p c n", p=P)).then_inc(wu_in[i], 16)
                    sp.dma_start(wd_sb[i][:, 0, :], at(down_t, e)[0:P, :]).then_inc(wu_in[i], 16)
                    sp.dma_start(wd_sb[i][LO:LO + I1, 1, :], at(down_t, e)[P:I, :]).then_inc(wu_in[i], 16)
                load(0, 0)
                load(1, 1)
                with sp.Fori(0, NE // 2 - 1) as e2:
                    for i in range(2):
                        sp.wait_ge(s["down_done"], 16 * e2 + 8 * i + 8)
                        sp.nop(nofuse=True)
                        load(2 * e2 + i + 2, i)

            @block.tensor
            def _(pe):
                def up(e2, i, ch):
                    n = 8 * e2 + 4 * i + ch
                    if ch == 0:
                        pe.wait_ge(wu_in[i], 48 * e2 + 48)
                    pe.wait_ge(s["a_ready"], n + 1)
                    b0 = 3 * (ch % 2)
                    for k, (c0, m, at_) in enumerate(((0, P, 0), (I, P, 0), (P, I1, 0), (I + P, I1, LO))):
                        for c in range(DC):
                            last = nc.tensor.matmul(bank[at_:at_ + m, b0 + min(k, 2), :], wu_sb[i][:, c, c0:c0 + m],
                                                    h2T[:, c, ch * T:ch * T + T], start=(c == 0),
                                                    stop=(c == DC - 1), skip_group_check=True)
                    last.then_inc(s["up_done"], 1)

                def down(e2, i, ch):
                    n = 8 * e2 + 4 * i + ch
                    pe.wait_ge(s["a_ready"], 2 + n + 1)
                    for k in range(2):
                        pe.wait_ge(s["acc_done"], 2 * n + k + 1)
                        for j in range(2):
                            tok = (2 * k + j) * P
                            nc.tensor.matmul(bank[:, 6 + k, j * D:j * D + D], aT[ch % 2][:, 0, tok:tok + P],
                                             wd_sb[i][:, 0, :], start=(j == 0), stop=False, skip_group_check=True)
                            last = nc.tensor.matmul(bank[:, 6 + k, j * D:j * D + D],
                                                    aT[ch % 2][LO:LO + I1, 1, tok:tok + P],
                                                    wd_sb[i][LO:LO + I1, 1, :], start=False, stop=True,
                                                    skip_group_check=True)
                        last.then_inc(s["down_done"], 1)

                up(0, 0, 0)
                with pe.Fori(0, NE // 2 - 1) as e2:
                    for n in range(8):
                        up(e2 + (n + 1) // 8, (n + 1) // 4 % 2, (n + 1) % 4)
                        down(e2, n // 4, n % 4)
                for n in range(8):
                    if n < 7:
                        up(NE // 2 - 1, (n + 1) // 4, (n + 1) % 4)
                    down(NE // 2 - 1, n // 4, n % 4)

            @block.scalar
            def _(act):
                with act.Fori(0, NE // 2) as e2:
                    for k in range(8):
                        ch = k % 4
                        n = 8 * e2 + k
                        b0 = 3 * (ch % 2)
                        act.wait_ge(s["up_done"], n + 1)
                        act.wait_ge(s["a_ready"], n + 1)
                        nc.scalar.activation(sg[ch % 2][:, 0, :], bank[:, b0, :], ACT.Silu).then_inc(s["silu_done"], 1)
                        nc.scalar.activation(sg[ch % 2][LO:LO + I1, 1, :], bank[0:I1, b0 + 2, :],
                                             ACT.Silu).then_inc(s["silu_done"], 1)

            @block.vector
            def _(dve):
                nc.vector.memset(credit(), 0.0).then_inc(s["a_ready"], 2)
                nc.vector.memset(credit(), 0.0).then_inc(s["acc_done"], 2)

                def gated(e2, k):
                    n = 8 * e2 + k
                    ch = k % 4
                    b0 = 3 * (ch % 2)
                    dve.wait_ge(s["silu_done"], 2 * n + 2)
                    nc.vector.tensor_tensor(aT[ch % 2][:, 0, :], bank[:, b0 + 1, :], sg[ch % 2][:, 0, :], ALU.mult)
                    nc.vector.tensor_tensor(aT[ch % 2][LO:LO + I1, 1, :], bank[LO:LO + I1, b0 + 2, :],
                                            sg[ch % 2][LO:LO + I1, 1, :], ALU.mult).then_inc(s["a_ready"], 1)

                def add(e2, k):
                    n = 8 * e2 + k
                    ch = k % 4
                    for h in range(2):
                        dve.wait_ge(s["down_done"], 2 * n + h + 1)
                        for j in range(2):
                            t = ch * QT + 2 * h + j
                            last = nc.vector.scalar_tensor_tensor(
                                out=acc[:, t, :], in0=bank[:, 6 + h, j * D:j * D + D],
                                scalar=cw[:, t, bass.ds(2 * e2 + k // 4, 1)], in1=acc[:, t, :],
                                op0=ALU.mult, op1=ALU.add)
                        last.then_inc(s["acc_done"], 1)

                gated(0, 0)
                with dve.Fori(0, NE // 2 - 1) as e2:
                    for k in range(8):
                        gated(e2 + (k + 1) // 8, (k + 1) % 8)
                        add(e2, k)
                for k in range(8):
                    if k < 7:
                        gated(NE // 2 - 1, k + 1)
                    add(NE // 2 - 1, k)
                dve.wait_ge(s["acc_done"], 2 + 8 * NE)
                for b in range(B):
                    a_b, x_b = acc[:, b * QT:b * QT + QT, :], X[:, b * QT:b * QT + QT, :]
                    g2 = gate_bc[:, b, 1, :].unsqueeze(1).to_broadcast([P, QT, D])
                    nc.vector.tensor_tensor(a_b, a_b, g2, ALU.mult).then_inc(s["fin"], 1)
                    dve.wait_ge(s["fin"], 2 * b + 1)
                    nc.vector.tensor_tensor(x_b, x_b, a_b, ALU.add).then_inc(s["fin"], 1)

            @block.gpsimd
            def _(gp):
                for b in range(B):
                    gp.wait_ge(s["fin"], 2 * b + 2)
                    gp.dma_start(out[b].rearrange("(t p) d -> p t d", p=P),
                                 X[:, b * QT:b * QT + QT, :]).then_inc(s["out_done"], 16)
                gp.wait_ge(s["out_done"], 16 * B)


def kernel(L0_attn_x, L0_attn_wq, L0_attn_wk, L0_attn_wv, L0_attn_wo, L0_ffn_gate_w, L0_ffn_expert_up_w,
           L0_ffn_expert_down_w, L0_ffn_shared_up_w, L0_ffn_shared_down_w, L0_c, L0_wmod):
    import numpy as np
    import concourse.bacc as bacc
    from concourse.bass_utils import run_bass_kernel_spmd

    def cols(w, *dims, order):
        a = np.asarray(w)
        n = a.shape[0]
        return a.reshape(n, *dims).transpose(0, *(1 + i for i in order)).reshape(n, -1)

    a = np.asarray
    wq = cols(L0_attn_wq, 2, HH, HD, order=(0, 2, 1))
    wk = cols(L0_attn_wk, 2, GH, HD, order=(0, 2, 1))
    sh = a(L0_ffn_shared_up_w).reshape(2, 2, I, D).transpose(1, 0, 2, 3).reshape(2, 2 * I, D)
    up = np.concatenate([a(L0_ffn_expert_up_w), sh]).transpose(0, 2, 1)
    sd = a(L0_ffn_shared_down_w).reshape(D, 2, I).transpose(1, 2, 0)
    down = np.concatenate([a(L0_ffn_expert_down_w).transpose(0, 2, 1), sd])
    arrays = {
        "x": a(L0_attn_x), "wq": wq, "wk": wk, "wv": a(L0_attn_wv), "wo": a(L0_attn_wo),
        "gate_t": a(L0_ffn_gate_w).T, "up_t": up, "down_t": down, "c_t": a(L0_c).T, "wmod": a(L0_wmod),
    }
    arrays = {k: np.ascontiguousarray(v) for k, v in arrays.items()}
    nc = bacc.Bacc("TRN2", target_bir_lowering=False, num_devices=1)
    args = [nc.dram_tensor(k, v.shape, mybir.dt.from_np(v.dtype), kind="ExternalInput").ap() for k, v in arrays.items()]
    out = nc.dram_tensor("out", (B, T, D), F32, kind="ExternalOutput").ap()
    adaln_block(nc, *args, out)
    r = run_bass_kernel_spmd(nc, [arrays], core_ids=[0])
    return r.results[0]["out"]
```

```python
from contextlib import ExitStack

import numpy as np

import concourse.bass as bass
from concourse import mybir

P = 128
ALU = mybir.AluOpType
ACT = mybir.ActivationFunctionType
AX = mybir.AxisListType
F32 = mybir.dt.float32
I32 = mybir.dt.int32
U32 = mybir.dt.uint32
BF16 = mybir.dt.bfloat16

B, T, D = 4, 512, 256
NH, NKV, HD = 32, 8, 8
REP = NH // NKV
DC = D // P
QT = T // P
NT = B * QT
GH = NKV // 2
HH = NH // 2
E, I = 16, 176
NE = E + 2
G, TOPG, TOPK = 4, 2, 4
I1 = I - P
LO = 64
PARTS = 3
PR = PARTS * PARTS * HD
KR = 96
EPS = 1e-5
NEG = -1e30
REGION = B * T + P
TILES = B * T * TOPK // P + E - 1
ROW = D + 1 + E
DUMMY = E * REGION
ARENA = 40448
SCALE = float(HD) ** -0.5

S_UNITS = [GH * n for n in (1, 2, 4, 4)]
E_UNITS = [GH * n for n in (1, 1, 2, 2)]
SA, CA, GA, SB, CB, GB = (DC * n for n in range(6))


def adaln_block(nc, x, wq, wk, wv, wo, gate_t, up_t, down_t, c_t, wmod, out):
    q_parts = nc.dram_tensor("q_parts", (B, 2, PARTS, PARTS, HD, HH, T), BF16, kind="Internal").ap()
    k_parts = nc.dram_tensor("k_parts", (B, 2, PARTS, PARTS, HD, GH, T), BF16, kind="Internal").ap()
    x_rows = nc.dram_tensor("x_rows", (DUMMY + P, ROW), F32, kind="Internal").ap()
    y_sum = [nc.dram_tensor(f"y_sum{i}", (B * T + P, D), F32, kind="Internal").ap() for i in range(2)]
    y_parts = nc.dram_tensor("y_parts", (2, 2, GH, REP, HD, T), F32, kind="Internal").ap()

    with ExitStack() as ctx:
        def sb(name, shape, dt=F32):
            return ctx.enter_context(nc.sbuf_tensor(name, shape, dt))

        def sem(name):
            return ctx.enter_context(nc.semaphore(name))

        bank = ctx.enter_context(nc.psum_tensor("bank", [P, 8, 512], F32))

        ident = sb("ident", [P, P])
        ident_bf = sb("ident_bf", [P, P], BF16)
        mask_qk = sb("mask_qk", [P, REP, P], BF16)
        earlier = sb("earlier", [P, E, E], BF16)
        before_bf = sb("before_bf", [P, P], BF16)
        ones_bf = sb("ones_bf", [P, P], BF16)
        counts = sb("counts", [P, 3 * E + TOPK + 2 * TILES + 1])
        counts_i = sb("counts_i", [P, 3 * E + TOPK + 2 * TILES + 1], I32)
        eps = sb("eps", [P, 1])
        X = sb("X", [P, NT, D])
        gate_bc = sb("gate_bc", [P, B, 4, D])
        mod = sb("mod", [P, 2 * DC, B])
        wo_sb = sb("wo_sb", [P, 2, D])
        ln_st = sb("ln_st", [P, QT, 6])
        ln_mv = sb("ln_mv", [P, QT, 2])
        ln_sd = sb("ln_sd", [P, QT])
        ln_rs = sb("ln_rs", [P, QT])

        arena = sb("arena", [P, ARENA])

        def region(start):
            place = [start]

            def take(*dims, dt=F32):
                n = int(np.prod(dims))
                words = n // 2 if dt == BF16 else n
                piece = arena[:, place[0]:place[0] + words]
                place[0] += words
                assert place[0] <= arena.shape[1]
                if dt != F32:
                    piece = piece.bitcast(dt)
                names = "abcd"[:len(dims)]
                return piece.rearrange(f"p ({' '.join(names)}) -> p {' '.join(names)}", **dict(zip(names, dims)))
            return take

        take = region(0)
        pool = take(2, 4 * GH, T)
        Q = [take(QT, HH, P, dt=BF16) for s in range(2)]
        K = [take(GH, T, dt=BF16) for s in range(2)]
        K0 = [take(GH, T, dt=BF16) for s in range(2)]
        V = take(NT, NKV, 32)
        Vc = [take(QT, GH, 32) for s in range(2)]
        O = [take(REP, T) for s in range(2)]
        Yp = [take(T) for k in range(2)]
        Y = [take(T) for s in range(2)]
        prod = take(2, D)
        negm = [sb(f"negm{s}", [P, QT, HH]) for s in range(2)]
        nm_row = sb("nm_row", [HH, P])
        nm_row2 = sb("nm_row2", [HH, P])
        nm_res = sb("nm_res", [HH, P])
        nm_parts = [sb(f"nm_parts{i}", [HH, PARTS, P], BF16) for i in range(2)]

        take = region(0)
        wmod_sb = take(DC, 6 * D)
        wq_sb = take(DC, D)
        wk_sb = take(DC, NKV * HD)
        wv_sb = take(DC, NKV * HD)
        c_sb = take(DC, B)
        sc_sb = take(DC, B)
        sc_bc = take(DC, B, P)
        gtmp = take(2, D)
        gsgn = take(2, D)
        hT = take(DC, T)
        res = take(3, T)
        parts = [take(3, PARTS, T, dt=BF16) for i in range(2)]
        xn = take(QT, D)

        take = region(0)
        y_back = take(B, 2, QT, D)
        take = region(0)
        w_up = take(E, DC, 2 * I)
        h2T = take(DC, B * T)
        gate_sb = take(DC, E)
        lgT = take(T)
        w_down = [take(E, D) for c in range(2)]
        rows = take(NT, ROW)
        fill = take(ROW)
        ws_up = take(2, DC, 2 * I)
        ws_down = take(2, 2, D)
        y_shared = take(2, 2, D)
        cmp = [take(TILES + 1, E, dt=BF16) for i in range(2)]
        sg = [take(2, T) for i in range(2)]
        tail = region(ARENA - 4096)
        aT = [tail(2, 2, T) for i in range(2)]
        tail = region(ARENA - 4096)
        xt = [tail(ROW) for i in range(4)]
        xT = [tail(DC, P) for i in range(2)]
        act_g = [tail(I) for i in range(2)]
        actT = [tail(2, P) for i in range(2)]
        yo = [tail(D) for i in range(4)]

        logit = sb("logit", [P, NT, E])
        rt = sb("rt", [P, 8, QT, E])
        sel_bf = sb("sel_bf", [P, QT, E], BF16)
        taken = sb("taken", [P, E])
        slot_f = sb("slot_f", [P, QT, TOPK])
        slots = sb("slots", [P, NT, TOPK], U32)
        few = sb("few", [P, 8, E])
        big = sb("big", [P, QT, TOPK, E])
        pad_row = sb("pad_row", [1, E], I32)
        tile_row = sb("tile_row", [1, TILES], I32)
        tile_expert = sb("tile_expert", [1, TILES], I32)
        tab = sb("tab", [1, 3, TILES])
        token_no = [sb(f"token_no{i}", [P, 1], U32) for i in range(4)]
        weight = [sb(f"weight{i}", [P, 1]) for i in range(4)]

        def at(t, i):
            if isinstance(i, int):
                return t[i]
            a, *rest = "abcdefgh"[:len(t.shape) - 1]
            rest = " ".join(rest)
            return t[bass.ds(i, 1)].rearrange(f"o {a} {rest} -> (o {a}) {rest}")

        names = """w_in wm_in wg_in cleared_q c_in wo_in const_done silu_c sc_bcast mod_done mod_used gate_mm gate_used v_ones
            ln_stats ln_sdev xn_ready tr_done h_ready qkv_done qkv_high v_done res1 mid_done res2 low_done
            q_out qkv_free
            q_in0 q_in1 k_in0 k_in1 k0_in0 k0_in1 nm_in s_ready s_free st_ready st_free av_done o_free
            misc_ready misc_free nm_copy nm_res_done nm_split den_ready rden_ready y_ready prod_ready x2_ready
            lg_done lg_sb lgt_done lg_ready soft exp_l route chain pchain inverted
            p_ready zero_done h2_ready numbered gate_in wu_in wd_in wd_zero ws_in filled sh_up sh_silu sh_a sh_down ys_ready
            ys_out0 ys_out1 y_zero subtracted sel_ready pos_done pos_used routed run_done table rows_out pad_out
            cleared tx_done xT_ready up_done silu_done a_ready ta_done aT_ready dn_done yo_ready extra scat0 scat1
            fin out_done""".split()
        s = {n: sem(n) for n in names}

        credits = sb("credits", [P, 32])
        given = [0]

        def credit():
            given[0] += 1
            return credits[:, given[0]:given[0] + 1]

        chained = [0]

        def link(eng, ins):
            chained[0] += 1
            ins.then_inc(s["chain"], 1)
            eng.wait_ge(s["chain"], chained[0])

        def layer_norm(dve, b, to, base=0, turned=0):
            for i in range(QT):
                st = nc.vector.bn_stats(ln_st[:, i, :], X[:, bass.ds(b * QT + i, 1), :].rearrange("p o d -> p (o d)"))
            st.then_inc(s["soft"], 1)
            dve.wait_ge(s["soft"], 3 * (b + base) + 1)
            dve.nop(nofuse=True)
            for i in range(QT):
                ag = nc.vector.bn_aggr(ln_mv[:, i, :], ln_st[:, i, :])
            ag.then_inc(s["ln_stats"], 1)
            dve.wait_ge(s["ln_sdev"], b + base + 1)
            nc.vector.reciprocal(ln_rs[:, :], ln_sd[:, :]).then_inc(s["soft"], 2)
            dve.wait_ge(s["soft"], 3 * (b + base) + 3)
            if turned:
                dve.wait_ge(s["tr_done"], turned)
            for i in range(QT):
                last = nc.vector.tensor_scalar(to(i), X[:, bass.ds(b * QT + i, 1), :].rearrange("p o d -> p (o d)"),
                                               ln_mv[:, i, 0:1], ln_rs[:, i:i + 1], ALU.subtract, ALU.mult)
            last.then_inc(s["xn_ready"], 1)

        x_in = [sem(f"x_in{b}") for b in range(B)]
        q_out = [sem(f"q_out{i}") for i in range(2)]
        q_in = [[sem(f"q_in{h}_{q}") for q in range(QT)] for h in range(2)]
        k_in = [s["k_in0"], s["k_in1"]]
        k0_in = [s["k0_in0"], s["k0_in1"]]
        STORES = 4 * PARTS

        def load_q(sp, b, h, q):
            sp.dma_start(Q[h][0:PR, q, :, :],
                         at(q_parts, b)[h].rearrange("j n d h t -> (j n d) h t")[:, :, q * P:q * P + P]
                         ).then_inc(q_in[h][q], 16)

        def load_k(sp, b, h, to, signal):
            sp.dma_start(to[h][0:PR, :, :], at(k_parts, b)[h].rearrange("n j d g t -> (n j d) g t")).then_inc(signal, 16)

        with nc.Block() as block:
            @block.sync
            def _(sp):
                def load_x(b):
                    sp.dma_start(X[:, b * QT:b * QT + QT, :], x[b].rearrange("(t p) d -> p t d", p=P)).then_inc(x_in[b], 16)
                sp.dma_start(c_sb, c_t.rearrange("(c p) b -> p c b", p=P)).then_inc(s["c_in"], 16)
                load_x(0)
                wm = wmod.rearrange("(c p) n -> p c n", p=P)
                sp.dma_start(wmod_sb[:, :, 0:GA * P], wm[:, :, 0:GA * P]).then_inc(s["wm_in"], 16)
                sp.dma_start(wq_sb, wq.rearrange("(c p) n -> p c n", p=P)).then_inc(s["w_in"], 16)
                sp.dma_start(wk_sb, wk.rearrange("(c p) n -> p c n", p=P)).then_inc(s["w_in"], 16)
                sp.dma_start(wv_sb, wv.rearrange("(c p) n -> p c n", p=P)).then_inc(s["w_in"], 16)
                load_x(1)
                sp.dma_start(wmod_sb[:, :, GA * P:], wm[:, :, GA * P:]).then_inc(s["wg_in"], 16)
                load_x(2)
                load_x(3)
                sp.dma_start(wo_sb[:, :, :], wo.rearrange("(s p) n -> p s n", p=P)).then_inc(s["wo_in"], 16)

                for b in range(B):
                    i = b % 2
                    sp.wait_ge(s["low_done"], b + 1)
                    for h in range(2):
                        for j in range(PARTS):
                            mine = parts[i][:, h, j, :].unsqueeze(1).to_broadcast([P, PARTS, T])
                            sp.dma_start(q_parts[b, h, j].rearrange("n d h t -> (d h) n t"), mine).then_inc(q_out[i], 16)
                        for n in range(PARTS):
                            sp.dma_start(k_parts[b, h, n].rearrange("j d g t -> (d g) j t"),
                                         parts[i][32 * h:32 * h + 32, 2, :, :]).then_inc(q_out[i], 16)
                    if b == 1:
                        sp.wait_ge(q_out[0], 16 * STORES)
                        sp.wait_ge(s["cleared_q"], 1)
                        for q in range(QT):
                            load_q(sp, 0, 0, q)
                            if q == 0:
                                load_k(sp, 0, 0, K0, k0_in[0])
                        load_k(sp, 0, 0, K, k_in[0])
                        load_k(sp, 0, 1, K0, k0_in[1])
                        for q in range(QT):
                            load_q(sp, 0, 1, q)

            @block.gpsimd
            def _(gp):
                n = [0]

                def step(ins):
                    n[0] += 1
                    ins.then_inc(s["pchain"], 1)
                    gp.wait_ge(s["pchain"], n[0])

                def low(b):
                    mid, low_ = parts[b % 2][:, :, 1, :], parts[b % 2][:, :, 2, :]
                    gp.wait_ge(s["mid_done"], 2 * b + 2)
                    nc.gpsimd.tensor_tensor(low_[:, 0:2], res[:, 0:2, :], mid[:, 0:2], ALU.subtract)
                    nc.gpsimd.tensor_tensor(low_[0:64, 2], res[0:64, 2, :], mid[0:64, 2],
                                            ALU.subtract).then_inc(s["low_done"], 1)

                step(nc.gpsimd.memset(ident[:, :], 0.0))
                nc.gpsimd.affine_select(out=ident[:, :], in_=ident[:, :], compare_op=ALU.not_equal, fill=1.0,
                                        base=0, pattern=[[-1, P]], channel_multiplier=1).then_inc(s["const_done"], 1)
                nc.gpsimd.memset(V, 1.0).then_inc(s["v_ones"], 1)
                for h in range(2):
                    nc.gpsimd.memset(Q[h][:, :, :, :], 0.0)
                    nc.gpsimd.memset(K[h][:, :, :], 1.0)
                    last = nc.gpsimd.memset(K0[h][:, :, :], 0.0)
                last.then_inc(s["cleared_q"], 1)
                gp.wait_ge(s["const_done"], 1)
                step(nc.gpsimd.tensor_copy(ident_bf[:, :], ident[:, :]))
                step(nc.gpsimd.memset(mask_qk[:, :, :], 0.0))
                step(nc.gpsimd.affine_select(out=mask_qk[:, :, :], in_=mask_qk[:, :, :], compare_op=ALU.is_ge,
                                             fill=NEG, base=0, pattern=[[0, REP], [-1, P]], channel_multiplier=1))
                for b in range(B):
                    low(b)
                step(nc.gpsimd.memset(before_bf[:, :], 1.0))
                step(nc.gpsimd.memset(ones_bf[:, :], 1.0))
                step(nc.gpsimd.memset(earlier[:, :, :], 1.0))
                step(nc.gpsimd.affine_select(out=before_bf[:, :], in_=before_bf[:, :], compare_op=ALU.is_gt,
                                             fill=0.0, base=0, pattern=[[1, P]], channel_multiplier=-1))
                step(nc.gpsimd.affine_select(out=earlier[:, :, :], in_=earlier[:, :, :], compare_op=ALU.is_gt,
                                             fill=0.0, base=0, pattern=[[1, E], [-1, E]], channel_multiplier=0))
                at_ = 0
                for step_, num, cm in ((REGION, E, 0), (P, E, 0), (P, NT, 1), (1, TOPK, 0), (1, TILES, 0),
                                       (P, TILES, 0), (0, 1, 1)):
                    step(nc.gpsimd.iota(counts_i[:, at_:at_ + num], [[step_, num]], 0, cm))
                    at_ += num
                step(nc.gpsimd.tensor_copy(counts[:, :], counts_i[:, :]))

            @block.scalar
            def _(act):
                def deviation(b):
                    act.wait_ge(s["ln_stats"], b + 1)
                    nc.scalar.activation(ln_sd[:, :], ln_mv[:, :, 1], ACT.Sqrt,
                                         bias=eps[:, :]).then_inc(s["ln_sdev"], 1)

                def modulate(b):
                    act.wait_ge(s["tr_done"], b + 1)
                    for c in range(DC):
                        nc.scalar.activation(hT[:, c, :], bank[:, c, :], ACT.Identity, bias=mod[:, SA + c, b:b + 1],
                                             scale=mod[:, CA + c, b:b + 1]).then_inc(s["h_ready"], 1)

                act.wait_ge(s["c_in"], 16)
                nc.scalar.activation(sc_sb, c_sb, ACT.Silu).then_inc(s["silu_c"], 1)
                deviation(0)
                act.wait_ge(s["mod_used"], 2)
                modulate(0)
                deviation(1)
                for b in range(B):
                    mine = parts[b % 2]
                    act.wait_ge(s["qkv_done"], b + 1)
                    if b >= 2:
                        act.wait_ge(q_out[b % 2], 16 * STORES * (b // 2))
                    nc.scalar.activation(mine[:, 0:2, 0, :], bank[:, 2:4, :], ACT.Copy).then_inc(s["qkv_high"], 1)
                    nc.scalar.activation(mine[0:64, 2, 0, :], bank[0:64, 4, :], ACT.Copy).then_inc(s["qkv_high"], 1)
                    if b == 0:
                        act.wait_ge(s["v_ones"], 1)
                    nc.scalar.activation(V[:, b * QT:b * QT + QT, :, 0:HD],
                                         bank[:, 5, 0:QT * 64].rearrange("p (t g d) -> p t g d", t=QT, g=NKV),
                                         ACT.Copy).then_inc(s["v_done"], 1)
                    if b + 1 < B:
                        modulate(b + 1)
                    act.wait_ge(s["res1"], b + 1)
                    nc.scalar.activation(mine[:, 0:2, 1, :], res[:, 0:2, :], ACT.Copy).then_inc(s["mid_done"], 1)
                    nc.scalar.activation(mine[0:64, 2, 1, :], res[0:64, 2, :], ACT.Copy).then_inc(s["mid_done"], 1)
                    if b + 2 < B:
                        deviation(b + 2)

            @block.vector
            def _(dve):
                def gates(b):
                    dve.wait_ge(s["gate_mm"], b + 1)
                    g_ps = bank[:, 6, :].rearrange("p (a n) -> p a n", a=2)
                    link(dve, nc.vector.tensor_scalar(gtmp, g_ps, -1.0, 0.25, ALU.mult, ALU.max))
                    link(dve, nc.vector.tensor_tensor(gtmp, g_ps, gtmp, ALU.max))
                    link(dve, nc.vector.tensor_scalar(gsgn, g_ps, 0.0, 2.0, ALU.is_ge, ALU.mult))
                    nc.vector.scalar_tensor_tensor(out=gate_bc[:, b, 0:2, :], in0=gsgn, scalar=-1.0, in1=gtmp,
                                                   op0=ALU.add, op1=ALU.mult)
                    nc.vector.tensor_copy(gate_bc[:, b, 2, :], bank[:, 7, 0:D])
                    nc.vector.tensor_scalar(gate_bc[:, b, 3, :], bank[:, 7, D:2 * D], 1.0, None,
                                            ALU.add).then_inc(s["gate_used"], 1)
                    dve.wait_ge(s["gate_used"], b + 1)

                def norm(b):
                    dve.wait_ge(x_in[b], 16)
                    layer_norm(dve, b, lambda i: xn[:, i, :], turned=b)

                link(dve, nc.vector.memset(eps[:, :], EPS))
                norm(0)
                dve.wait_ge(s["mod_done"], 1)
                mod_ps = bank[:, 7, 0:2 * DC * B].rearrange("p (m b) -> p m b", b=B)
                nc.vector.tensor_copy(mod[:, SA:SA + DC, :], mod_ps[:, SA:SA + DC, :]).then_inc(s["mod_used"], 1)
                nc.vector.tensor_scalar(mod[:, CA:CA + DC, :], mod_ps[:, CA:CA + DC, :], 1.0, None,
                                        ALU.add).then_inc(s["mod_used"], 1)
                nc.vector.tensor_copy(sc_bc, sc_sb.unsqueeze(3).to_broadcast([P, DC, B, P])).then_inc(s["sc_bcast"], 1)
                norm(1)
                for b in range(B):
                    dve.wait_ge(s["qkv_high"], 2 * b + 2)
                    if b > 0:
                        dve.wait_ge(s["low_done"], b)
                    mine = parts[b % 2]
                    nc.vector.tensor_tensor(res[:, 0:2, :], bank[:, 2:4, :], mine[:, 0:2, 0, :], ALU.subtract)
                    nc.vector.tensor_tensor(res[0:64, 2, :], bank[0:64, 4, :], mine[0:64, 2, 0, :],
                                            ALU.subtract).then_inc(s["res1"], 1)
                    if b + 2 < B:
                        norm(b + 2)
                    gates(b)

            @block.tensor
            def _(pe):
                def turn(b):
                    pe.wait_ge(s["xn_ready"], b + 1)
                    if b > 0:
                        pe.wait_ge(s["h_ready"], DC * b)
                    for c in range(DC):
                        for i in range(QT):
                            last = nc.tensor.transpose(bank[:, c, i * P:i * P + P], xn[:, i, c * P:c * P + P], ident[:, :])
                    last.then_inc(s["tr_done"], 1)

                pe.wait_ge(s["wm_in"], 16)
                pe.wait_ge(s["silu_c"], 1)
                for m in range(2 * DC):
                    for c in range(DC):
                        last = nc.tensor.matmul(bank[:, 7, m * B:m * B + B], wmod_sb[:, c, m * P:m * P + P],
                                                sc_sb[:, c, :], start=(c == 0), stop=(c == DC - 1),
                                                skip_group_check=True)
                last.then_inc(s["mod_done"], 1)
                pe.wait_ge(s["const_done"], 1)
                turn(0)
                pe.wait_ge(s["w_in"], 48)
                for b in range(B):
                    pe.wait_ge(s["h_ready"], DC * b + DC)
                    if b > 0:
                        pe.wait_ge(s["res1"], b)
                        pe.wait_ge(s["v_done"], b)
                    for m in range(2):
                        for c in range(DC):
                            nc.tensor.matmul(bank[:, 2 + m, :], wq_sb[:, c, m * P:m * P + P], hT[:, c, :],
                                             start=(c == 0), stop=(c == DC - 1))
                    for c in range(DC):
                        nc.tensor.matmul(bank[0:64, 4, :], wk_sb[:, c, :], hT[:, c, :],
                                         start=(c == 0), stop=(c == DC - 1))
                    for i in range(QT):
                        for c in range(DC):
                            last = nc.tensor.matmul(bank[:, 5, i * 64:i * 64 + 64], hT[:, c, i * P:i * P + P],
                                                    wv_sb[:, c, :], start=(c == 0), stop=(c == DC - 1),
                                                    skip_group_check=True)
                    last.then_inc(s["qkv_done"], 1)
                    if b + 1 < B:
                        turn(b + 1)
                    if b == 0:
                        pe.wait_ge(s["wg_in"], 16)
                        pe.wait_ge(s["sc_bcast"], 1)
                        pe.wait_ge(s["mod_used"], 2)
                    else:
                        pe.wait_ge(s["gate_used"], b)
                    for a, m in enumerate((GA, GB, SB, CB)):
                        for c in range(DC):
                            last = nc.tensor.matmul(bank[:, 6 + a // 2, a % 2 * D:a % 2 * D + D], sc_bc[:, c, b, :],
                                                    wmod_sb[:, c, m * P:m * P + D], start=(c == 0),
                                                    stop=(c == DC - 1), skip_group_check=True)
                    last.then_inc(s["gate_mm"], 1)

        E_END = [sum(E_UNITS[:q + 1]) for q in range(QT)]
        E_TOT, S_TOT = sum(E_UNITS), sum(S_UNITS)
        S_AT = {(q, g): sum(S_UNITS[:q]) + g * S_UNITS[q] // GH for q in range(QT) for g in range(GH)}
        E_AT = {(q, g): sum(E_UNITS[:q]) + g * E_UNITS[q] // GH for q in range(QT) for g in range(GH)}
        MISC, OBANK = 7, 6
        TURNS, WO_USES = 4, 2

        def misc_base(b, h):
            return 3 if first(b, h) else 3 + (2 * TURNS + WO_USES) * b - (0 if h else WO_USES) + TURNS * h

        def first(b, h):
            return isinstance(b, int) and (b, h) == (0, 0)

        def turn_use(b, h, q):
            return misc_base(b, h) + (0 if q == QT - 1 else q + 1)

        def project_use(b, g):
            return misc_base(b, 0) + TURNS + g - 2

        nm_in = [sem("nm_in_even"), sem("nm_in_odd")]
        y_out = [sem("y_out0"), sem("y_out1")]
        y_in = [sem("y_in0"), sem("y_in1")]
        nm_rows = [nm_row, nm_row2]

        def s_banks(q):
            return {0: 4, 1: 2, 2: 1, 3: 1}[q], (q + 1) * P

        def prev(b, h):
            return (b, 0) if h else (b - 1, 1)

        with nc.Block() as block:
            @block.sync
            def _(sp):
                def load_kv(b, h):
                    load_k(sp, b, h, K, k_in[h])
                    sp.dma_start(Vc[h][:, :, :, :],
                                 V[:, bass.ds(b * QT, QT), h * GH:h * GH + GH, :]).then_inc(k_in[h], 16)

                def put_negm(b, h, q):
                    sp.wait_ge(s["nm_split"], 8 + 16 * (2 * b + h) + 4 * q + 4)
                    sp.nop(nofuse=True)
                    for j in range(PARTS):
                        sp.dma_start(Q[h][PR + j:PR + j + 1, q, :, :],
                                     nm_parts[q % 2][:, j, :]).then_inc(nm_in[q % 2], 16)

                def send_values(b, h):
                    sp.wait_ge(s["o_free"], 1 + 4 * (2 * b + h) + 4)
                    sp.nop(nofuse=True)
                    for g in range(GH):
                        for k in range(2):
                            sp.dma_start(y_parts[h, k, g].rearrange("r d t -> d r t"),
                                         O[h][32 * g + HD * k:32 * g + HD * k + HD, :, :]).then_inc(y_out[h], 16)

                def fetch_values(b, h):
                    sp.wait_ge(s["y_ready"], 2 * b + h + 1)
                    sp.wait_ge(y_out[h], 16 + 128 * b + 128)
                    sp.nop(nofuse=True)
                    for k in range(2):
                        sp.dma_start(Yp[k][:, :], y_parts[h, k].rearrange("g r d t -> (g r d) t")).then_inc(y_in[h], 16)

                def half(b, h, loads=True, nxt=True, back=True):
                    u = 2 * b + h
                    put_negm(b, h, QT - 1)
                    if loads:
                        sp.wait_ge(s["s_ready"], S_TOT * u + S_TOT)
                        sp.nop(nofuse=True)
                        load_k(sp, b + 1, h, K0, k0_in[h])
                    if nxt:
                        if back:
                            sp.wait_ge(s["av_done"], 2 + 4 * u)
                            sp.nop(nofuse=True)
                        load_kv(b + h, 1 - h)
                    if back:
                        send_values(*prev(b, h))
                    for q in range(QT):
                        if q == 1 and back:
                            fetch_values(*prev(b, h))
                        if nxt and q > 0:
                            put_negm(b + h, 1 - h, q - 1)
                        if loads:
                            sp.wait_ge(s["st_ready"], E_TOT * u + E_END[q])
                            sp.nop(nofuse=True)
                            load_q(sp, b + 1, h, q)

                sp.dma_start(Vc[0], V[:, 0:QT, 0:GH, :]).then_inc(k_in[0], 16)
                for i in range(2):
                    sp.wait_ge(q_out[i], 16 * STORES * (B // 2))
                for q in range(QT - 1):
                    put_negm(0, 0, q)
                half(0, 0, back=False)
                with sp.Fori(0, B - 2) as b:
                    half(b, 1)
                    half(b + 1, 0)
                half(B - 2, 1)
                half(B - 1, 0, loads=False)
                half(B - 1, 1, loads=False, nxt=False)
                send_values(B - 1, 1)
                fetch_values(B - 1, 1)

            @block.tensor
            def _(pe):
                def scores_for_max(b, h, q, g, k):
                    u = 2 * b + h
                    if g == 0 and k == 0:
                        pe.wait_ge(q_in[h][q], 16 * b + 16)
                        if q == 0:
                            pe.wait_ge(k0_in[h], 16 * b + 16)
                    heads, n = s_banks(q)
                    unit = S_TOT * u + S_AT[q, g] + k
                    buf = (S_AT[q, g] + k) % 2
                    pe.wait_ge(s["s_free"], unit + 1)
                    for i in range(heads):
                        nc.tensor.matmul(bank[:, buf, i * n:i * n + n],
                                         Q[h][0:KR, q, g * REP + k * heads + i, :], K0[h][0:KR, g, 0:n],
                                         start=(i == 0), stop=False, skip_group_check=True)
                    view = bank[:, buf, 0:heads * n].rearrange("p (i n) -> p i n", i=heads)
                    nc.tensor.matmul(view[:, :, n - P:n], ident_bf[:, :], mask_qk[:, 0:heads, :],
                                     start=False, stop=True, skip_group_check=True).then_inc(s["s_ready"], 1)

                def scores(b, h, q, g, k):
                    u = 2 * b + h
                    if g == 0 and k == 0:
                        pe.wait_ge(nm_in[q % 2], 16 + 48 * (2 * u + q // 2) + 48)
                        if q == 0:
                            pe.wait_ge(k_in[h], 16 * 2 * b + 16 * 2)
                    unit = E_TOT * u + E_AT[q, g] + k
                    buf = 2 + 2 * ((E_AT[q, g] + k) % 2)
                    pe.wait_ge(s["st_free"], unit + 1)
                    for kt in range(2 * k, min(2 * k + 2, q + 1)):
                        last = nc.tensor.matmul(bank[:, buf + kt % 2, :], K[h][0:KR, g, kt * P:(kt + 1) * P],
                                                Q[h][0:KR, q, g * REP:g * REP + REP, :],
                                                start=True, stop=True, skip_group_check=True)
                    last.then_inc(s["st_ready"], 1)

                def weigh_values(b, h, q):
                    u = 2 * b + h
                    pe.wait_ge(s["p_ready"], 16 * u + 4 * q + 4)
                    pe.wait_ge(s["o_free"], 4 * u + q + 1)
                    for kt in range(q + 1):
                        for g in range(GH):
                            last = nc.tensor.matmul(bank[32 * g:32 * g + 32, OBANK, :], Vc[h][:, kt, g, :],
                                                    pool[:, q % 2, g * QT + kt, :], start=(kt == 0), stop=(kt == q),
                                                    skip_group_check=True)
                    last.then_inc(s["av_done"], 1)

                def turn_max(b, h, q, use):
                    u = 2 * b + h
                    pe.wait_ge(s["s_free"], 2 + S_TOT * u + sum(S_UNITS[:q + 1]))
                    pe.wait_ge(s["misc_free"], use + 1)
                    nc.tensor.transpose(bank[0:HH, MISC, 0:P], negm[h][:, q, :], ident[:, :]).then_inc(s["misc_ready"], 1)

                def project(b, w, use):
                    pe.wait_ge(s["y_ready"], 1 + 2 * b + 2)
                    pe.wait_ge(s["misc_free"], use + 1)
                    for i in range(2):
                        t = (2 * w + i) * P
                        for h in range(2):
                            last = nc.tensor.matmul(bank[:, MISC, i * D:i * D + D], Y[h][:, t:t + P], wo_sb[:, h, :],
                                                    start=(h == 0 and i == 0), stop=(h == 1), skip_group_check=True)
                    last.then_inc(s["misc_ready"], 1)

                def half(b, h, nxt=True, back=True):
                    for q in range(QT):
                        for g in range(GH):
                            ne, ns = E_UNITS[q] // GH, (S_UNITS[q] // GH if nxt else 0)
                            for k in range(ne):
                                scores(b, h, q, g, k)
                                for j in range(k * ns // ne, (k + 1) * ns // ne):
                                    scores_for_max(b + h, 1 - h, q, g, j)
                            if g == 1 and q > 0:
                                weigh_values(b, h, q - 1)
                            elif g == 1 and back:
                                weigh_values(*prev(b, h), QT - 1)
                            if g == 2 and q == 0:
                                turn_max(b, h, QT - 1, turn_use(b, h, QT - 1))
                            elif g == 2 and nxt:
                                turn_max(b + h, 1 - h, q - 1, turn_use(b, h, q - 1))
                            if h == 0 and back and q == 3 and g >= 2:
                                project(b - 1, g - 2, project_use(b, g))

                pe.wait_ge(s["wo_in"], 16)
                for q in range(QT):
                    for g in range(GH):
                        for k in range(S_UNITS[q] // GH):
                            scores_for_max(0, 0, q, g, k)
                    if q > 0:
                        turn_max(0, 0, q - 1, q - 1)
                half(0, 0, back=False)
                with pe.Fori(0, B - 1) as b:
                    half(b, 1)
                    half(b + 1, 0)
                half(B - 1, 1, nxt=False)
                weigh_values(B - 1, 1, QT - 1)
                for w in range(2):
                    project(B - 1, w, misc_base(B - 1, 1) + 1 + w)

            @block.scalar
            def _(act):
                def out_of_psum(b, h, q):
                    m = 4 * (2 * b + h) + q
                    act.wait_ge(s["av_done"], 2 + m + 1)
                    if q == 0:
                        act.wait_ge(y_out[h], 128 * b + 16)
                    nc.scalar.activation(O[h][:, :, q * P:q * P + P],
                                         bank[:, OBANK, :].rearrange("p (r t) -> p r t", r=REP),
                                         ACT.Copy).then_inc(s["o_free"], 1)

                def half(b, h, back=True):
                    u = 2 * b + h
                    for q in range(QT):
                        act.wait_ge(s["av_done"], 4 * u + q + 1)
                        for g in range(GH):
                            for k, kt in enumerate(range(0, q + 1, 2)):
                                unit = E_TOT * u + E_AT[q, g] + k
                                buf = 2 + 2 * ((E_AT[q, g] + k) % 2)
                                n = min(2, q + 1 - kt)
                                act.wait_ge(s["st_ready"], unit + 1)
                                nc.scalar.activation(pool[:, q % 2, g * QT + kt:g * QT + kt + n, :],
                                                     bank[:, buf:buf + n, :], ACT.Exp,
                                                     scale=SCALE).then_inc(s["st_free"], 1)
                            if g == 2 and q > 0:
                                out_of_psum(b, h, q - 1)
                            elif g == 2 and back:
                                out_of_psum(*prev(b, h), QT - 1)
                half(0, 0, back=False)
                with act.Fori(0, B - 1) as b:
                    half(b, 1)
                    half(b + 1, 0)
                half(B - 1, 1)
                out_of_psum(B - 1, 1, QT - 1)

            @block.gpsimd
            def _(gp):
                def mask(b, h, q, g):
                    unit = E_TOT * (2 * b + h) + E_AT[q, g] + E_UNITS[q] // GH
                    block_ = pool[:, q % 2, g * QT + q, :].rearrange("p (r t) -> p r t", r=REP)
                    gp.wait_ge(s["st_free"], 2 + unit)
                    gp.nop(nofuse=True)
                    nc.gpsimd.affine_select(out=block_, in_=block_, compare_op=ALU.is_ge, fill=0.0, base=0,
                                            pattern=[[0, REP], [1, P]], channel_multiplier=-1).then_inc(s["p_ready"], 1)

                def split(b, h, q, use):
                    u = 2 * b + h
                    t8 = 8 + 16 * u + 4 * q
                    row, to = nm_rows[q % 2], nm_parts[q % 2]
                    gp.wait_ge(s["misc_free"], 1 + use + 1)
                    gp.wait_ge(nm_in[q % 2], 16 + 48 * (2 * u + q // 2))
                    gp.nop(nofuse=True)
                    nc.gpsimd.tensor_copy(to[:, 0, :], row[:, :]).then_inc(s["nm_split"], 1)
                    gp.wait_ge(s["nm_split"], t8 + 1)
                    nc.gpsimd.tensor_tensor(nm_res[:, :], row[:, :], to[:, 0, :], ALU.subtract).then_inc(s["nm_split"], 1)
                    gp.wait_ge(s["nm_split"], t8 + 2)
                    gp.nop(nofuse=True)
                    nc.gpsimd.tensor_copy(to[:, 1, :], nm_res[:, :]).then_inc(s["nm_split"], 1)
                    gp.wait_ge(s["nm_split"], t8 + 3)
                    nc.gpsimd.tensor_tensor(to[:, 2, :], nm_res[:, :], to[:, 1, :], ALU.subtract).then_inc(s["nm_split"], 1)
                    gp.wait_ge(s["nm_split"], t8 + 4)

                def half(b, h, nxt=True):
                    for q in range(QT):
                        for g in range(GH):
                            mask(b, h, q, g)
                            if g == 2 and q == 0:
                                split(b, h, QT - 1, turn_use(b, h, QT - 1))
                            elif g == 2 and nxt:
                                split(b + h, 1 - h, q - 1, turn_use(b, h, q - 1))
                for q in range(QT - 1):
                    split(0, 0, q, q)
                half(0, 0)
                with gp.Fori(0, B - 1) as b:
                    half(b, 1)
                    half(b + 1, 0)
                half(B - 1, 1, nxt=False)

            @block.vector
            def _(dve):
                for name, n in (("s_free", 2), ("st_free", 2), ("av_done", 2), ("o_free", 1), ("misc_free", 1),
                                ("x2_ready", 1), ("y_ready", 1), ("nm_split", 8)):
                    nc.vector.memset(credit(), 0.0).then_inc(s[name], n)
                for one in (*nm_in, *y_out):
                    nc.vector.memset(credit(), 0.0).then_inc(one, 16)

                def maxima(b, h, q, g):
                    u = 2 * b + h
                    heads, n = s_banks(q)
                    for k in range(REP // heads):
                        unit = S_TOT * u + S_AT[q, g] + k
                        dve.wait_ge(s["s_ready"], unit + 1)
                        at_ = g * REP + k * heads
                        view = bank[:, (S_AT[q, g] + k) % 2, 0:heads * n].rearrange("p (i n) -> p i n", i=heads)
                        nc.vector.tensor_reduce(negm[h][:, q, at_:at_ + heads], view, AX.X, ALU.max,
                                                negate=True).then_inc(s["s_free"], 1)

                def take_max(b, h, q, use):
                    u = 2 * b + h
                    dve.wait_ge(s["misc_ready"], use + 1)
                    dve.wait_ge(s["nm_split"], 16 * u + 4 * q + 4)
                    nc.vector.tensor_copy(nm_rows[q % 2][:, :], bank[0:HH, MISC, 0:P]).then_inc(s["misc_free"], 1)

                def invert(b, h, q):
                    dve.wait_ge(y_in[h], 32 * b + 32)
                    nc.vector.reciprocal(Yp[1][:, q * P:q * P + P], Yp[1][:, q * P:q * P + P]).then_inc(s["inverted"], 1)

                def normalise(b, h):
                    dve.wait_ge(s["inverted"], 4 * (2 * b + h) + 4)
                    nc.vector.tensor_tensor(Y[h][:, :], Yp[0][:, :], Yp[1][:, :], ALU.mult).then_inc(s["y_ready"], 1)

                def residual(b, w, use):
                    dve.wait_ge(s["misc_ready"], use + 1)
                    dve.wait_ge(s["x2_ready"], 2 * b + w + 1)
                    g1 = gate_bc[:, bass.ds(b, 1), 0, :].to_broadcast([P, 2, D])
                    xt = X[:, bass.ds(b * QT + 2 * w, 2), :]
                    nc.vector.tensor_tensor(prod[:, :, :], bank[:, MISC, :].rearrange("p (i d) -> p i d", i=2), g1,
                                            ALU.mult).then_inc(s["misc_free"], 1)
                    dve.wait_ge(s["misc_free"], 1 + use + 1)
                    nc.vector.tensor_tensor(xt, xt, prod[:, :, :], ALU.add).then_inc(s["x2_ready"], 1)

                def half(b, h, nxt=True, back=True):
                    for q in range(QT):
                        for g in range(GH):
                            if nxt:
                                maxima(b + h, 1 - h, q, g)
                            if q == 3 and g < 2 and back:
                                invert(*prev(b, h), 2 * g)
                                invert(*prev(b, h), 2 * g + 1)
                            if q == 3 and g == 2 and back:
                                normalise(*prev(b, h))
                            if g == 2 and q == 0:
                                take_max(b, h, QT - 1, turn_use(b, h, QT - 1))
                            elif g == 2 and nxt:
                                take_max(b + h, 1 - h, q - 1, turn_use(b, h, q - 1))
                            if h == 0 and back and q == 3 and g >= 2:
                                residual(b - 1, g - 2, project_use(b, g))

                for q in range(QT):
                    for g in range(GH):
                        maxima(0, 0, q, g)
                    if q > 0:
                        take_max(0, 0, q - 1, q - 1)
                half(0, 0, back=False)
                with dve.Fori(0, B - 1) as b:
                    half(b, 1)
                    half(b + 1, 0)
                half(B - 1, 1, nxt=False)
                for q in range(QT):
                    invert(B - 1, 1, q)
                normalise(B - 1, 1)
                for w in range(2):
                    residual(B - 1, w, misc_base(B - 1, 1) + 1 + w)

        PLACE = {}
        at_ = 0
        for name, num in (("first", E), ("k128", E), ("token", NT), ("slot", TOPK), ("tile", TILES),
                          ("tile128", TILES), ("partition", 1)):
            PLACE[name] = counts[:, at_:at_ + num]
            at_ += num

        with nc.Block() as block:
            @block.sync
            def _(sp):
                sp.dma_start(gate_sb, gate_t.rearrange("(c p) e -> p c e", p=P)).then_inc(s["gate_in"], 16)
                for c in range(2):
                    sp.dma_start(ws_up[:, :, c, :],
                                 up_t[E:E + 2, c * P:c * P + P, :].rearrange("e p n -> p e n")).then_inc(s["ws_in"], 16)
                sp.dma_start(ws_down[:, :, 0, :],
                             down_t[E:E + 2, 0:P, :].rearrange("e p n -> p e n")).then_inc(s["ws_in"], 16)
                sp.dma_start(ws_down[LO:LO + I1, :, 1, :],
                             down_t[E:E + 2, P:I, :].rearrange("e p n -> p e n")).then_inc(s["ws_in"], 16)
                for c in range(DC):
                    sp.dma_start(w_up[:, :, c, :],
                                 up_t[0:E, c * P:c * P + P, :].rearrange("e p n -> p e n")).then_inc(s["wu_in"], 16)
                sp.dma_start(w_down[0], down_t[0:E, 0:P, :].rearrange("e p n -> p e n")).then_inc(s["wd_in"], 16)
                sp.wait_ge(s["wd_zero"], 1)
                sp.dma_start(w_down[1][0:I1], down_t[0:E, P:I, :].rearrange("e p n -> p e n")).then_inc(s["wd_in"], 16)

            @block.scalar
            def _(act):
                def deviation(b):
                    act.wait_ge(s["ln_stats"], B + b + 1)
                    nc.scalar.activation(ln_sd[:, :], ln_mv[:, :, 1], ACT.Sqrt,
                                         bias=eps[:, :]).then_inc(s["ln_sdev"], 1)

                def out_of_psum(b):
                    act.wait_ge(s["tr_done"], B + b + 1)
                    for c in range(DC):
                        nc.scalar.activation(h2T[:, c, bass.ds(b * T, T)], bank[:, c, :],
                                             ACT.Copy).then_inc(s["h_ready"], 1)
                    act.wait_ge(s["lg_done"], b + 1)
                    nc.scalar.activation(lgT[0:E, :], bank[0:E, 2, :], ACT.Copy).then_inc(s["lg_sb"], 1)
                    act.wait_ge(s["lgt_done"], b + 1)
                    nc.scalar.activation(logit[:, bass.ds(b * QT, QT), :],
                                         bank[:, 3, 0:QT * E].rearrange("p (i e) -> p i e", i=QT),
                                         ACT.Copy).then_inc(s["lg_ready"], 1)
                deviation(0)
                with act.Fori(0, B - 1) as b:
                    deviation(b + 1)
                    out_of_psum(b)
                out_of_psum(B - 1)

            @block.tensor
            def _(pe):
                pe.wait_ge(s["gate_in"], 16)
                for b in range(B):
                    pe.wait_ge(s["h2_ready"], 2 * b + 2)
                    for c in range(DC):
                        for i in range(QT):
                            last = nc.tensor.transpose(bank[:, c, i * P:i * P + P],
                                                       rows[:, b * QT + i, c * P:c * P + P], ident[:, :])
                    last.then_inc(s["tr_done"], 1)
                    pe.wait_ge(s["h_ready"], DC * (B + b) + DC)
                    for c in range(DC):
                        last = nc.tensor.matmul(bank[0:E, 2, :], gate_sb[:, c, :], h2T[:, c, b * T:b * T + T],
                                                start=(c == 0), stop=(c == DC - 1))
                    last.then_inc(s["lg_done"], 1)
                    pe.wait_ge(s["lg_sb"], b + 1)
                    for i in range(QT):
                        last = nc.tensor.transpose(bank[:, 3, i * E:i * E + E], lgT[0:E, i * P:i * P + P],
                                                   ident[0:E, 0:E])
                    last.then_inc(s["lgt_done"], 1)
                    pe.wait_ge(s["lg_ready"], b + 1)

            @block.vector
            def _(dve):
                nc.vector.tensor_copy(rows[:, :, D], PLACE["token"]).then_inc(s["numbered"], 1)
                nc.vector.memset(fill[:, :], 0.0).then_inc(s["numbered"], 1)
                dve.wait_ge(s["numbered"], 2)
                nc.vector.tensor_scalar(fill[:, D:D + 1], PLACE["partition"], float(B * T), None,
                                        ALU.add).then_inc(s["filled"], 1)
                nc.vector.tensor_copy(taken[:, :], PLACE["first"]).then_inc(s["numbered"], 1)
                with dve.Fori(0, B) as b:
                    layer_norm(dve, b, lambda i: rows[:, bass.ds(b * QT + i, 1), 0:D].rearrange("p o d -> p (o d)"), B)

            @block.gpsimd
            def _(gp):
                nc.gpsimd.memset(w_down[1], 0.0).then_inc(s["wd_zero"], 1)
                with gp.Fori(0, B) as b:
                    def modulation(k):
                        return gate_bc[:, bass.ds(b, 1), k, :].to_broadcast([P, QT, D])
                    gp.wait_ge(s["xn_ready"], B + b + 1)
                    gp.nop(nofuse=True)
                    tokens = rows[:, bass.ds(b * QT, QT), 0:D]
                    nc.gpsimd.tensor_tensor(tokens, tokens, modulation(3), ALU.mult).then_inc(s["h2_ready"], 1)
                    gp.wait_ge(s["h2_ready"], 2 * b + 1)
                    gp.nop(nofuse=True)
                    nc.gpsimd.tensor_tensor(tokens, tokens, modulation(2), ALU.add).then_inc(s["h2_ready"], 1)

        ys_out = [s["ys_out0"], s["ys_out1"]]
        with nc.Block() as block:
            @block.sync
            def _(sp):
                sp.wait_ge(s["filled"], 1)
                zeros = fill[:, 0:D].unsqueeze(1).to_broadcast([P, NT + 1, D])
                sp.dma_start(y_sum[1].rearrange("(t p) d -> p t d", p=P), zeros).then_inc(s["y_zero"], 16)
                sp.dma_start(y_sum[0][NT * P:, :], fill[:, 0:D]).then_inc(s["y_zero"], 16)
                sp.dma_start(x_rows[DUMMY:, :], fill[:, :]).then_inc(s["pad_out"], 16)
                for n in range(B):
                    for h in range(2):
                        sp.wait_ge(s["ys_ready"], 2 * n + h + 1)
                        at_ = n * T + 2 * h * P
                        sp.dma_start(y_sum[0][at_:at_ + 2 * P, :].rearrange("(t p) d -> p t d", p=P),
                                     y_shared[:, h]).then_inc(ys_out[h], 16)
                    if n == B - 2:
                        sp.wait_ge(s["run_done"], 1)
                        with sp.Fori(0, E) as e:
                            row = sp.value_load(pad_row[0:1, bass.ds(e, 1)], min_val=0, max_val=DUMMY - P)
                            sp.dma_start(x_rows[bass.ds(row, P), :], fill[:, :]).then_inc(s["pad_out"], 16)

            @block.gpsimd
            def _(gp):
                for m in range(B):
                    gp.wait_ge(s["routed"], m + 1)
                    for i in range(QT):
                        for k in range(TOPK):
                            t = m * QT + i
                            gp.indirect_dma_start(x_rows, bass.IndirectOffsetOnAxis(ap=slots[:, t, k:k + 1], axis=0),
                                                  rows[:, t, :], None).then_inc(s["rows_out"], 16)

            @block.tensor
            def _(pe):
                def up(n, j):
                    v = 2 * n + j
                    if v >= 2:
                        pe.wait_ge(s["sh_a"], v - 1)
                    b0 = 3 * (v % 2)
                    for k, (c0, w, at_) in enumerate(((0, P, 0), (I, P, 0), (P, I1, 0), (I + P, I1, LO))):
                        for c in range(DC):
                            last = nc.tensor.matmul(bank[at_:at_ + w, b0 + min(k, 2), :], ws_up[:, j, c, c0:c0 + w],
                                                    h2T[:, c, n * T:n * T + T], start=(c == 0),
                                                    stop=(c == DC - 1), skip_group_check=True)
                    last.then_inc(s["sh_up"], 1)

                def down(n, h):
                    pe.wait_ge(s["sh_a"], 2 * n + 2)
                    if h == 0 and n > 0:
                        pe.wait_ge(s["ys_ready"], 2 * n - 1)
                    if h == 1 and n < B - 1:
                        pe.wait_ge(s["pos_used"], n + 2)
                    if h == 1 and n == B - 1:
                        pe.wait_ge(s["ys_ready"], 2 * n)
                    for i in range(2):
                        tok = (2 * h + i) * P
                        for j in range(2):
                            nc.tensor.matmul(bank[:, 7 - h, i * D:i * D + D], aT[n % 2][:, j, 0, tok:tok + P],
                                             ws_down[:, j, 0, :], start=(i == 0 and j == 0), stop=False,
                                             skip_group_check=True)
                            last = nc.tensor.matmul(bank[:, 7 - h, i * D:i * D + D],
                                                    aT[n % 2][LO:LO + I1, j, 1, tok:tok + P],
                                                    ws_down[LO:LO + I1, j, 1, :], start=False, stop=(j == 1),
                                                    skip_group_check=True)
                    last.then_inc(s["sh_down"], 1)

                def positions(m):
                    pe.wait_ge(s["sel_ready"], m + 1)
                    if m >= 2:
                        pe.wait_ge(s["ys_ready"], 2 * (m - 2) + 2)
                    flat = sel_bf[:, :, :].rearrange("p t e -> p (t e)")
                    nc.tensor.matmul(bank[:, 6, 0:QT * E], before_bf[:, :], flat, start=True, stop=False,
                                     skip_group_check=True)
                    for i in range(1, QT):
                        nc.tensor.matmul(bank[:, 6, i * E:QT * E], ones_bf[:, :], flat[:, 0:(QT - i) * E],
                                         start=False, stop=(i == QT - 1), skip_group_check=True)
                    for i in range(QT):
                        last = nc.tensor.matmul(bank[:, 6, QT * E:QT * E + E], ones_bf[:, :],
                                                flat[:, i * E:i * E + E], start=False, stop=(i == QT - 1),
                                                skip_group_check=True)
                    last.then_inc(s["pos_done"], 1)

                pe.wait_ge(s["ws_in"], 64)
                positions(0)
                pe.wait_ge(s["pos_used"], 1)
                for m in range(1, B + 1):
                    up(m - 1, 0)
                    up(m - 1, 1)
                    if m < B:
                        positions(m)
                    down(m - 1, 0)
                    down(m - 1, 1)

            @block.scalar
            def _(act):
                def exponential(m):
                    act.wait_ge(s["subtracted"], m + 1)
                    nc.scalar.activation(rt[:, 0], rt[:, 0], ACT.Exp).then_inc(s["exp_l"], 1)

                exponential(0)
                for n in range(B):
                    if n < B - 1:
                        exponential(n + 1)
                    for v in (2 * n, 2 * n + 1):
                        act.wait_ge(s["sh_up"], v + 1)
                        if v >= 2:
                            act.wait_ge(s["sh_a"], v - 1)
                        b0 = 3 * (v % 2)
                        nc.scalar.activation(sg[v % 2][:, 0, :], bank[:, b0, :], ACT.Silu).then_inc(s["sh_silu"], 1)
                        nc.scalar.activation(sg[v % 2][LO:LO + I1, 1, :], bank[0:I1, b0 + 2, :],
                                             ACT.Silu).then_inc(s["sh_silu"], 1)
                    for h in range(2):
                        act.wait_ge(s["sh_down"], 2 * n + h + 1)
                        if n > 0:
                            act.wait_ge(ys_out[h], 16 * n)
                        nc.scalar.activation(y_shared[:, h], bank[:, 7 - h, :].rearrange("p (t d) -> p t d", t=2),
                                             ACT.Copy).then_inc(s["ys_ready"], 1)

            @block.vector
            def _(dve):
                count = [0]

                def step(ins):
                    count[0] += 1
                    ins.then_inc(s["route"], 1)
                    dve.wait_ge(s["route"], count[0])

                def over(a, k):
                    return a.unsqueeze(2).to_broadcast([P, QT, k])

                expd, score, msk, rank, sel, w, pos, tmp = (rt[:, i] for i in range(8))
                mx, total, inv, kept = (few[:, i, 0:QT] for i in range(4))

                def before(v, k, to):
                    mine = v[:, :, 0:k].unsqueeze(3).to_broadcast([P, QT, k, k])
                    other = v[:, :, 0:k].unsqueeze(2).to_broadcast([P, QT, k, k])
                    tri = earlier[:, 0:k, 0:k].unsqueeze(1).to_broadcast([P, QT, k, k])
                    greater, equal = (c.rearrange("p a b -> p (a b)")[:, 0:QT * k * k]
                                      .rearrange("p (t i j) -> p t i j", t=QT, i=k) for c in cmp)
                    step(nc.vector.tensor_tensor(greater, other, mine, ALU.is_gt))
                    step(nc.vector.tensor_tensor(equal, other, mine, ALU.is_equal))
                    step(nc.vector.tensor_tensor(equal, equal, tri, ALU.mult))
                    step(nc.vector.tensor_tensor(greater, greater, equal, ALU.add))
                    step(nc.vector.tensor_reduce(to[:, :, 0:k], greater, AX.X, ALU.add))

                def choose(m):
                    lg = logit[:, m * QT:m * QT + QT, :]
                    step(nc.vector.tensor_reduce(mx, lg, AX.X, ALU.max))
                    nc.vector.tensor_tensor(expd, lg, over(mx, E), ALU.subtract).then_inc(s["subtracted"], 1)
                    dve.wait_ge(s["exp_l"], m + 1)
                    step(nc.vector.tensor_reduce(total, expd, AX.X, ALU.add))
                    step(nc.vector.reciprocal(inv, total))
                    step(nc.vector.tensor_tensor(score, expd, over(inv, E), ALU.mult))
                    by_group = score.rearrange("p t (g e) -> p t g e", g=G)
                    step(nc.vector.tensor_reduce(tmp[:, :, 0:G], by_group, AX.X, ALU.max))
                    before(tmp, G, rank)
                    step(nc.vector.tensor_scalar(tmp[:, :, 0:G], rank[:, :, 0:G], float(TOPG), None, ALU.is_lt))
                    step(nc.vector.tensor_tensor(msk.rearrange("p t (g e) -> p t g e", g=G), by_group,
                                                 tmp[:, :, 0:G].unsqueeze(3).to_broadcast([P, QT, G, E // G]),
                                                 ALU.mult))
                    before(msk, E, rank)
                    if m > 0:
                        dve.wait_ge(s["pos_done"], m)
                    nc.vector.tensor_scalar(sel_bf[:, :, :], rank, float(TOPK), None,
                                            ALU.is_lt).then_inc(s["sel_ready"], 1)
                    step(nc.vector.tensor_scalar(sel, rank, float(TOPK), None, ALU.is_lt))
                    step(nc.vector.tensor_tensor(w, msk, sel, ALU.mult))
                    step(nc.vector.tensor_reduce(kept, w, AX.X, ALU.add))
                    step(nc.vector.tensor_scalar(mx, kept, 1e-20, None, ALU.add))
                    step(nc.vector.reciprocal(inv, mx))
                    step(nc.vector.tensor_tensor(rows[:, m * QT:m * QT + QT, D + 1:ROW], w, over(inv, E), ALU.mult))

                def place(m):
                    dve.wait_ge(s["pos_done"], m + 1)
                    ps = bank[:, 6, 0:QT * E].rearrange("p (t e) -> p t e", t=QT)
                    step(nc.vector.tensor_tensor(pos, ps, taken[:, :].unsqueeze(1).to_broadcast([P, QT, E]), ALU.add))
                    nc.vector.tensor_tensor(taken[:, :], taken[:, :], bank[:, 6, QT * E:QT * E + E],
                                            ALU.add).then_inc(s["pos_used"], 1)
                    dve.wait_ge(s["pos_used"], m + 1)
                    wide = [P, QT, TOPK, E]
                    step(nc.vector.tensor_tensor(big[:, :, :, :], rank.unsqueeze(2).to_broadcast(wide),
                                                 PLACE["slot"].unsqueeze(1).unsqueeze(3).to_broadcast(wide),
                                                 ALU.is_equal))
                    step(nc.vector.tensor_tensor(big[:, :, :, :], big[:, :, :, :], pos.unsqueeze(2).to_broadcast(wide),
                                                 ALU.mult))
                    step(nc.vector.tensor_reduce(slot_f[:, :, :], big[:, :, :, :], AX.X, ALU.add))
                    nc.vector.tensor_copy(slots[:, m * QT:m * QT + QT, :], slot_f[:, :, :]).then_inc(s["routed"], 1)

                def gated(v):
                    dve.wait_ge(s["sh_silu"], 2 * v + 2)
                    n, j, b0 = v // 2, v % 2, 3 * (v % 2)
                    if n >= 2:
                        dve.wait_ge(s["sh_down"], 2 * n - 2)
                    nc.vector.tensor_tensor(aT[n % 2][:, j, 0, :], bank[:, b0 + 1, :], sg[j][:, 0, :], ALU.mult)
                    nc.vector.tensor_tensor(aT[n % 2][LO:LO + I1, j, 1, :], bank[LO:LO + I1, b0 + 2, :],
                                            sg[j][LO:LO + I1, 1, :], ALU.mult).then_inc(s["sh_a"], 1)

                def tables():
                    n, tiles, start, end = (few[:, i, :] for i in range(4, 8))
                    nc.vector.tensor_copy(pad_row[:, :], taken[0:1, :]).then_inc(s["run_done"], 1)
                    step(nc.vector.tensor_tensor(n, taken[:, :], PLACE["first"], ALU.subtract))
                    square = [P, E, E]
                    ee = cmp[0][:, 0:E, :]
                    step(nc.vector.tensor_tensor(ee, n.unsqueeze(2).to_broadcast(square),
                                                 PLACE["k128"].unsqueeze(1).to_broadcast(square), ALU.is_gt))
                    step(nc.vector.tensor_reduce(tiles, ee, AX.X, ALU.add))
                    step(nc.vector.tensor_tensor(ee, earlier[:, :, :], tiles.unsqueeze(1).to_broadcast(square),
                                                 ALU.mult))
                    step(nc.vector.tensor_reduce(start, ee, AX.X, ALU.add))
                    step(nc.vector.tensor_tensor(end, start, tiles, ALU.add))
                    wide = [1, TILES, E]
                    past, weighed = (c[0:1, 0:TILES, :] for c in cmp)
                    step(nc.vector.tensor_tensor(past, PLACE["tile"][0:1].unsqueeze(2).to_broadcast(wide),
                                                 end[0:1].unsqueeze(1).to_broadcast(wide), ALU.is_ge))
                    step(nc.vector.tensor_tensor(weighed, past, tiles[0:1].unsqueeze(1).to_broadcast(wide), ALU.mult))
                    step(nc.vector.tensor_reduce(tab[:, 0, :], past, AX.X, ALU.add))
                    step(nc.vector.tensor_reduce(tab[:, 1, :], weighed, AX.X, ALU.add))
                    step(nc.vector.scalar_tensor_tensor(out=tab[:, 2, :], in0=tab[:, 1, :], scalar=-float(P),
                                                        in1=PLACE["tile128"][0:1], op0=ALU.mult, op1=ALU.add))
                    step(nc.vector.scalar_tensor_tensor(out=tab[:, 1, :], in0=tab[:, 0, :], scalar=float(REGION),
                                                        in1=tab[:, 2, :], op0=ALU.mult, op1=ALU.add))
                    step(nc.vector.tensor_scalar(tile_row[:, :], tab[:, 1, :], float(DUMMY), None, ALU.min))
                    nc.vector.tensor_scalar(tile_expert[:, :], tab[:, 0, :], float(E - 1), None,
                                            ALU.min).then_inc(s["table"], 1)

                dve.wait_ge(s["numbered"], 3)
                choose(0)
                place(0)
                for m in range(1, B + 1):
                    if m < B:
                        choose(m)
                    gated(2 * m - 2)
                    gated(2 * m - 1)
                    if m < B:
                        place(m)
                    if m == B - 1:
                        tables()

        STEPS = 4
        TURNS_ = (TILES - 2) // STEPS
        xt_in = [sem(f"xt_in{i}") for i in range(STEPS)]
        scat = [s["scat0"], s["scat1"]]
        back = [sem(f"y_back{b}") for b in range(B)]
        with nc.Block() as block:
            def over_tiles(eng, one):
                with eng.Fori(0, TURNS_) as turn:
                    for i in range(STEPS):
                        one(STEPS * turn + i, i, True, True)
                for t in range(STEPS * TURNS_, TILES):
                    one(t, t % STEPS, t + 1 < TILES, t + 2 < TILES)

            @block.sync
            def _(sp):
                def load(t, i):
                    sp.nop(nofuse=True)
                    row = sp.value_load(tile_row[0:1, bass.ds(t, 1)], min_val=0, max_val=DUMMY)
                    sp.dma_start(xt[i], x_rows[bass.ds(row, P), :]).then_inc(xt_in[i], 16)

                sp.wait_ge(s["table"], 1)
                sp.wait_ge(s["rows_out"], 16 * NT * TOPK)
                sp.wait_ge(s["pad_out"], 16 * (E + 1))
                for t in range(STEPS):
                    load(t, t)

                def one(t, i, more, far):
                    sp.wait_ge(s["tx_done"], 2 + t + 1)
                    sp.nop(nofuse=True)
                    sp.wait_ge(s["extra"], t + 1)
                    load(t + STEPS, i)
                full = (TILES - STEPS) // STEPS
                with sp.Fori(0, full) as turn:
                    for i in range(STEPS):
                        one(STEPS * turn + i, i, True, True)
                for t in range(STEPS * full, TILES - STEPS):
                    one(t, t % STEPS, True, True)
                for i in range(2):
                    sp.wait_ge(scat[i], 16 * ((TILES + 1 - i) // 2))
                for b in range(B):
                    for i in range(2):
                        sp.dma_start(y_back[:, b, i], y_sum[i][b * T:b * T + T, :].rearrange("(t p) d -> p t d", p=P)
                                     ).then_inc(back[b], 16)
                for b in range(B):
                    sp.wait_ge(s["fin"], 3 * b + 3)
                    sp.dma_start(out[b].rearrange("(t p) d -> p t d", p=P),
                                 X[:, b * QT:b * QT + QT, :]).then_inc(s["out_done"], 16)
                sp.wait_ge(s["out_done"], 16 * B)

            @block.tensor
            def _(pe):
                def turn_rows(t, i):
                    pe.wait_ge(xt_in[i % STEPS], 16 * (t // STEPS) + 16)
                    for c in range(DC):
                        last = nc.tensor.transpose(bank[:, i % 2, c * P:c * P + P],
                                                   xt[i % STEPS][:, c * P:c * P + P], ident[:, :])
                    last.then_inc(s["tx_done"], 1)

                def expert_of(t):
                    return pe.value_load(tile_expert[0:1, bass.ds(t, 1)], min_val=0, max_val=E - 1)

                def up(t, i, e):
                    w = w_up.rearrange("p e c n -> p (e c n)")
                    pe.wait_ge(s["xT_ready"], 2 + t + 1)
                    pe.wait_ge(s["a_ready"], t + 1)
                    for c in range(DC):
                        last = nc.tensor.matmul(bank[:, 2 + i % 2, 0:2 * I], xT[i % 2][:, c, :],
                                                w[:, bass.ds(e * (DC * 2 * I) + c * 2 * I, 2 * I)],
                                                start=(c == 0), stop=(c == DC - 1))
                    last.then_inc(s["up_done"], 1)

                def turn_act(t, i):
                    pe.wait_ge(s["a_ready"], 2 + t + 1)
                    pe.wait_ge(s["aT_ready"], t + 1)
                    nc.tensor.transpose(bank[:, 4 + i % 2, 0:P], act_g[i % 2][:, 0:P], ident[:, :])
                    nc.tensor.transpose(bank[0:I1, 4 + i % 2, P:2 * P], act_g[i % 2][:, P:I],
                                        ident[:, :]).then_inc(s["ta_done"], 1)

                def down(t, i, e):
                    pe.wait_ge(s["aT_ready"], 2 + t + 1)
                    pe.wait_ge(s["yo_ready"], t + 1)
                    for c in range(2):
                        w = w_down[c].rearrange("p e n -> p (e n)")
                        last = nc.tensor.matmul(bank[:, 6 + i % 2, 0:D], actT[i % 2][:, c, :],
                                                w[:, bass.ds(e * D, D)], start=(c == 0), stop=(c == 1))
                    last.then_inc(s["dn_done"], 1)

                pe.wait_ge(s["table"], 1)
                pe.wait_ge(s["wu_in"], 32)
                pe.wait_ge(s["wd_in"], 32)
                pe.wait_ge(s["xT_ready"], 2)
                turn_rows(0, 0)
                turn_rows(1, 1)
                up(0, 0, expert_of(0))

                with pe.Fori(0, TURNS_) as turn:
                    e = None
                    for i in range(STEPS):
                        t = STEPS * turn + i
                        e_next = expert_of(t + 1)
                        turn_act(t, i)
                        up(t + 1, i + 1, e_next)
                        pe.wait_ge(s["xT_ready"], t + 3)
                        pe.wait_ge(xt_in[(i + 2) % STEPS], 16 * turn + 16 * ((i + 2) // STEPS) + 16)
                        j = (i + 2) % STEPS
                        for c in range(DC):
                            last = nc.tensor.transpose(bank[:, j % 2, c * P:c * P + P],
                                                       xt[j][:, c * P:c * P + P], ident[:, :])
                        last.then_inc(s["tx_done"], 1)
                        down(t, i, expert_of(t) if e is None else e)
                        e = e_next
                for t in range(STEPS * TURNS_, TILES):
                    turn_act(t, t % STEPS)
                    if t + 1 < TILES:
                        up(t + 1, (t + 1) % STEPS, expert_of(t + 1))
                    if t + 2 < TILES:
                        pe.wait_ge(s["xT_ready"], t + 3)
                        turn_rows(t + 2, (t + 2) % STEPS)
                    down(t, t % STEPS, expert_of(t))

            @block.scalar
            def _(act):
                def rows_out_of_psum(t, i):
                    act.wait_ge(s["tx_done"], 2 + t + 1)
                    act.wait_ge(s["up_done"], t + 1)
                    nc.scalar.activation(xT[i % 2].rearrange("p c n -> p (c n)"), bank[:, i % 2, 0:DC * P],
                                         ACT.Copy).then_inc(s["xT_ready"], 1)

                def silu(t, i):
                    act.wait_ge(s["up_done"], 2 + t + 1)
                    act.wait_ge(s["ta_done"], t + 1)
                    nc.scalar.activation(act_g[i % 2], bank[:, 2 + i % 2, 0:I], ACT.Silu).then_inc(s["silu_done"], 1)

                def act_out_of_psum(t, i):
                    act.wait_ge(s["ta_done"], 2 + t + 1)
                    act.wait_ge(s["dn_done"], t + 1)
                    nc.scalar.activation(actT[i % 2][:, 0, :], bank[:, 4 + i % 2, 0:P], ACT.Copy)
                    nc.scalar.activation(actT[i % 2][0:I1, 1, :], bank[0:I1, 4 + i % 2, P:2 * P],
                                         ACT.Copy).then_inc(s["aT_ready"], 1)

                act.wait_ge(s["sh_down"], 2 * B)
                act.wait_ge(s["cleared"], 1)
                rows_out_of_psum(0, 0)
                rows_out_of_psum(1, 1)
                silu(0, 0)

                def one(t, i, more, far):
                    act_out_of_psum(t, i)
                    if more:
                        silu(t + 1, i + 1)
                    if far:
                        rows_out_of_psum(t + 2, i + 2)
                over_tiles(act, one)

            @block.vector
            def _(dve):
                for i in range(2):
                    last = nc.vector.memset(actT[i][:, 1, :], 0.0)
                last.then_inc(s["cleared"], 1)
                for name in "tx_done xT_ready up_done silu_done a_ready ta_done aT_ready dn_done yo_ready".split():
                    nc.vector.memset(credit(), 0.0).then_inc(s[name], 2)

                def extras(t, i, ins, done):
                    e = dve.value_load(tile_expert[0:1, bass.ds(t, 1)], min_val=0, max_val=E - 1)
                    dve.wait_ge(xt_in[i % STEPS], ins)
                    if not isinstance(t, int) or t >= STEPS:
                        dve.wait_ge(scat[i % 2], done)
                    nc.vector.tensor_copy(token_no[i % STEPS][:, :], xt[i % STEPS][:, D:D + 1])
                    nc.vector.tensor_copy(weight[i % STEPS][:, :],
                                          xt[i % STEPS][:, bass.ds(e + D + 1, 1)]).then_inc(s["extra"], 1)

                def gated(t, i):
                    dve.wait_ge(s["silu_done"], 2 + t + 1)
                    nc.vector.tensor_tensor(act_g[i % 2], bank[:, 2 + i % 2, I:2 * I], act_g[i % 2],
                                            ALU.mult).then_inc(s["a_ready"], 1)

                def weigh(t, i):
                    dve.wait_ge(s["dn_done"], 2 + t + 1)
                    nc.vector.tensor_scalar(yo[i % STEPS], bank[:, 6 + i % 2, 0:D], weight[i % STEPS][:, :], None,
                                            ALU.mult).then_inc(s["yo_ready"], 1)

                dve.wait_ge(s["table"], 1)
                extras(0, 0, 16, 0)
                extras(1, 1, 16, 0)
                gated(0, 0)

                def turn_of(turn):
                    for i in range(STEPS):
                        t = STEPS * turn + i
                        extras(t + 2, i + 2, 16 * turn + 16 * ((i + 2) // STEPS) + 16,
                               32 * turn + 16 * ((i + 2) // 2) - 16)
                        gated(t + 1, i + 1)
                        weigh(t, i)
                turn_of(0)
                with dve.Fori(1, TURNS_) as turn:
                    turn_of(turn)
                for t in range(STEPS * TURNS_, TILES):
                    if t + 2 < TILES:
                        extras(t + 2, t + 2, 16 * ((t + 2) // STEPS) + 16, 16 * ((t + 2) // 2) - 16)
                    if t + 1 < TILES:
                        gated(t + 1, t + 1)
                    weigh(t, t)

                for b in range(B):
                    x_b = X[:, b * QT:b * QT + QT, :]
                    g2 = gate_bc[:, b, 1, :].unsqueeze(1).to_broadcast([P, QT, D])
                    dve.wait_ge(back[b], 32)
                    nc.vector.tensor_tensor(y_back[:, b, 0], y_back[:, b, 0], y_back[:, b, 1],
                                            ALU.add).then_inc(s["fin"], 1)
                    dve.wait_ge(s["fin"], 3 * b + 1)
                    nc.vector.tensor_tensor(y_back[:, b, 0], y_back[:, b, 0], g2, ALU.mult).then_inc(s["fin"], 1)
                    dve.wait_ge(s["fin"], 3 * b + 2)
                    nc.vector.tensor_tensor(x_b, x_b, y_back[:, b, 0], ALU.add).then_inc(s["fin"], 1)

            @block.gpsimd
            def _(gp):
                def add_rows(t, i, done):
                    gp.wait_ge(s["yo_ready"], 2 + t + 1)
                    if not isinstance(t, int) or t >= 2:
                        gp.wait_ge(scat[i % 2], done)
                    gp.nop(nofuse=True)
                    gp.indirect_dma_start(y_sum[i % 2], bass.IndirectOffsetOnAxis(ap=token_no[i % STEPS][:, :], axis=0),
                                          yo[i % STEPS], None, compute_op=ALU.add).then_inc(scat[i % 2], 16)

                gp.wait_ge(s["y_zero"], 32)
                for h in range(2):
                    gp.wait_ge(ys_out[h], 16 * B)
                for t in range(STEPS):
                    add_rows(t, t, 16 * (t // 2))
                with gp.Fori(1, TURNS_) as turn:
                    for i in range(STEPS):
                        add_rows(STEPS * turn + i, i, 32 * turn + 16 * (i // 2))
                for t in range(STEPS * TURNS_, TILES):
                    add_rows(t, t, 16 * (t // 2))

def kernel(L0_attn_x, L0_attn_wq, L0_attn_wk, L0_attn_wv, L0_attn_wo, L0_ffn_gate_w, L0_ffn_expert_up_w,
           L0_ffn_expert_down_w, L0_ffn_shared_up_w, L0_ffn_shared_down_w, L0_c, L0_wmod):
    import numpy as np
    import concourse.bacc as bacc
    from concourse.bass_utils import run_bass_kernel_spmd

    def cols(w, *dims, order):
        a = np.asarray(w)
        n = a.shape[0]
        return a.reshape(n, *dims).transpose(0, *(1 + i for i in order)).reshape(n, -1)

    a = np.asarray
    wq = cols(L0_attn_wq, 2, HH, HD, order=(0, 2, 1))
    wk = cols(L0_attn_wk, 2, GH, HD, order=(0, 2, 1))
    sh = a(L0_ffn_shared_up_w).reshape(2, 2, I, D).transpose(1, 0, 2, 3).reshape(2, 2 * I, D)
    up = np.concatenate([a(L0_ffn_expert_up_w), sh]).transpose(0, 2, 1)
    sd = a(L0_ffn_shared_down_w).reshape(D, 2, I).transpose(1, 2, 0)
    down = np.concatenate([a(L0_ffn_expert_down_w).transpose(0, 2, 1), sd])
    arrays = {
        "x": a(L0_attn_x), "wq": wq, "wk": wk, "wv": a(L0_attn_wv), "wo": a(L0_attn_wo),
        "gate_t": a(L0_ffn_gate_w).T, "up_t": up, "down_t": down, "c_t": a(L0_c).T, "wmod": a(L0_wmod),
    }
    arrays = {k: np.ascontiguousarray(v) for k, v in arrays.items()}
    nc = bacc.Bacc("TRN2", target_bir_lowering=False, num_devices=1)
    args = [nc.dram_tensor(k, v.shape, mybir.dt.from_np(v.dtype), kind="ExternalInput").ap() for k, v in arrays.items()]
    out = nc.dram_tensor("out", (B, T, D), F32, kind="ExternalOutput").ap()
    adaln_block(nc, *args, out)
    r = run_bass_kernel_spmd(nc, [arrays], core_ids=[0])
    return r.results[0]["out"]
```

```python
from contextlib import ExitStack

import numpy as np

import concourse.bass as bass
from concourse import mybir

P = 128
ALU = mybir.AluOpType
ACT = mybir.ActivationFunctionType
AX = mybir.AxisListType
F32 = mybir.dt.float32
I32 = mybir.dt.int32
U32 = mybir.dt.uint32
BF16 = mybir.dt.bfloat16

B, T, D = 4, 512, 256
NH, NKV, HD = 32, 8, 8
REP = NH // NKV
DC = D // P
QT = T // P
NT = B * QT
GH = NKV // 2
HH = NH // 2
E, I = 16, 176
G, TOPG, TOPK = 4, 2, 4
I1 = I - P
SCHUNKS = (P, P, 2 * I - 2 * P)
PARTS = 3
PR = PARTS * PARTS * HD
KR = 96
EPS = 1e-5
NEG = -1e30
REGION = B * T + P
TILES = B * T * TOPK // P + E - 1
ROW = D + 1 + E
DUMMY = E * REGION
ARENA = 40448
SCALE = float(HD) ** -0.5

S_UNITS = [2, 4, 8, 8]
E_UNITS = [GH * (q + 1) for q in range(QT)]
SA, CA, GA, SB, CB, GB = (DC * n for n in range(6))


def adaln_block(nc, x, wq, wk, wv, wo, gate_t, up_t, down_t, shared_up_t, shared_down_t, c_t, wmod, out):
    q_parts = nc.dram_tensor("q_parts", (B, 2, PARTS, PARTS, HD, HH, T), BF16, kind="Internal").ap()
    k_parts = nc.dram_tensor("k_parts", (B, 2, PARTS, PARTS, HD, GH, T), BF16, kind="Internal").ap()
    x_rows = nc.dram_tensor("x_rows", (DUMMY + P, ROW), F32, kind="Internal").ap()
    y_sum = [nc.dram_tensor(f"y_sum{i}", (B * T + P, D), F32, kind="Internal").ap() for i in range(2)]
    y_parts = nc.dram_tensor("y_parts", (2, 2, GH, REP, HD, T), F32, kind="Internal").ap()

    with ExitStack() as ctx:
        def sb(name, shape, dt=F32):
            return ctx.enter_context(nc.sbuf_tensor(name, shape, dt))

        def sem(name):
            return ctx.enter_context(nc.semaphore(name))

        bank = ctx.enter_context(nc.psum_tensor("bank", [P, 8, 512], F32))

        ident = sb("ident", [P, P])
        ident_bf = sb("ident_bf", [P, P], BF16)
        mask_qk = sb("mask_qk", [P, REP, P], BF16)
        earlier = sb("earlier", [P, E, E], BF16)
        before_bf = sb("before_bf", [P, P], BF16)
        ones_bf = sb("ones_bf", [P, P], BF16)
        counts = sb("counts", [P, 3 * E + TOPK + 2 * TILES + 1])
        eps = sb("eps", [P, 1])
        X = sb("X", [P, NT, D])
        gate_bc = sb("gate_bc", [P, B, 4, D])
        mod = sb("mod", [P, 2 * DC, B])
        wo_sb = sb("wo_sb", [P, 2, D])
        ln_st = sb("ln_st", [P, QT, 6])
        ln_mv = sb("ln_mv", [P, QT, 2])
        ln_sd = sb("ln_sd", [P, QT])
        ln_rs = sb("ln_rs", [P, QT])

        arena = sb("arena", [P, ARENA])

        def region(start):
            place = [start]

            def take(*dims, dt=F32):
                n = int(np.prod(dims))
                words = n // 2 if dt == BF16 else n
                piece = arena[:, place[0]:place[0] + words]
                place[0] += words
                assert place[0] <= arena.shape[1]
                if dt != F32:
                    piece = piece.bitcast(dt)
                names = "abcd"[:len(dims)]
                return piece.rearrange(f"p ({' '.join(names)}) -> p {' '.join(names)}", **dict(zip(names, dims)))
            return take

        take = region(0)
        pool = take(2, 4 * GH, T)
        Q = [take(QT, HH, P, dt=BF16) for s in range(2)]
        K = [take(GH, T, dt=BF16) for s in range(2)]
        K0 = [take(GH, T, dt=BF16) for s in range(2)]
        V = take(NT, NKV, 32)
        Vc = [take(QT, GH, 32) for s in range(2)]
        O = [take(REP, T) for s in range(2)]
        Yp = [take(T) for k in range(2)]
        Y = [take(T) for s in range(2)]
        prod = take(2, D)
        negm = [sb(f"negm{s}", [P, QT, HH]) for s in range(2)]
        nm_row = sb("nm_row", [HH, P])
        nm_row2 = sb("nm_row2", [HH, P])
        nm_res = sb("nm_res", [HH, P])
        nm_parts = [sb(f"nm_parts{i}", [HH, PARTS, P], BF16) for i in range(2)]

        take = region(0)
        wmod_sb = take(DC, 6 * D)
        wq_sb = take(DC, D)
        wk_sb = take(DC, NKV * HD)
        wv_sb = take(DC, NKV * HD)
        c_sb = take(DC, B)
        sc_sb = take(DC, B)
        sc_bc = take(DC, B, P)
        gtmp = take(2, D)
        gsgn = take(2, D)
        hT = take(DC, T)
        res = take(3, T)
        parts = [take(3, PARTS, T, dt=BF16) for i in range(2)]
        xn = take(QT, D)
        counts_i = take(3 * E + TOPK + 2 * TILES + 1).bitcast(I32)

        take = region(0)
        y_back = take(B, 2, QT, D)
        take = region(0)
        w_up = take(E, DC, 2 * I)
        h2T = take(DC, B * T)
        w_down = [take(E, D) for c in range(2)]
        ws_up = take(DC, 4 * I)
        ws_down = take(3, D)
        fill = take(ROW)
        take = region(26624)
        rows = take(NT, ROW)
        cmp = [take(TILES + 1, E, dt=BF16) for i in range(2)]
        y_shared = take(2, 2, D)
        sg = [take(T) for k in range(3)]
        aT = [take(3, T) for i in range(2)]
        tail = region(ARENA - 4096)
        xt = [tail(ROW) for i in range(4)]
        xT = [tail(DC, P) for i in range(2)]
        act_g = [tail(I) for i in range(2)]
        actT = [tail(2, P) for i in range(2)]
        yo = [tail(D) for i in range(4)]

        gate_sb = sb("gate_sb", [P, DC, E])
        norm_st = sb("norm_st", [P, NT, 6])
        norm_mv = sb("norm_mv", [P, NT, 2])
        norm_sd = sb("norm_sd", [P, NT])
        norm_rs = sb("norm_rs", [P, NT])
        logit = sb("logit", [P, NT, E])
        rt = sb("rt", [P, 8, QT, E])
        sel_bf = sb("sel_bf", [P, QT, E], BF16)
        taken = sb("taken", [P, E])
        slot_f = sb("slot_f", [P, QT, TOPK])
        slots = sb("slots", [P, NT, TOPK], U32)
        few = sb("few", [P, 8, E])
        big = sb("big", [P, QT, TOPK, E])
        pad_row = sb("pad_row", [1, E], I32)
        tile_row = sb("tile_row", [1, TILES], I32)
        tile_expert = sb("tile_expert", [1, TILES], I32)
        tab = sb("tab", [1, 3, TILES])
        token_no = [sb(f"token_no{i}", [P, 1], U32) for i in range(4)]
        weight = [sb(f"weight{i}", [P, 1]) for i in range(4)]

        def at(t, i):
            if isinstance(i, int):
                return t[i]
            a, *rest = "abcdefgh"[:len(t.shape) - 1]
            rest = " ".join(rest)
            return t[bass.ds(i, 1)].rearrange(f"o {a} {rest} -> (o {a}) {rest}")

        names = """norm2 y_mm added ws_up_in norm_st norm_mv centred inverse_sd w_in wm_in wg_in cleared_q c_in wo_in
            const_done silu_c sc_bcast mod_done mod_used gate_mm gate_used v_ones ln_stats ln_sdev xn_ready
            tr_done h_ready qkv_done qkv_high v_done res1 mid_done low_done q_out k_in0 k_in1 k0_in0 k0_in1
            s_ready s_free st_ready st_free av_done o_free misc_ready misc_free nm_split y_ready x2_ready
            lg_done lg_ready soft exp_l route chain pchain inverted p_ready numbered gate_in wu_in wd_in wd_zero
            ws_in filled sh_up sh_silu sh_a sh_down ys_ready ys_out0 ys_out1 y_zero subtracted sel_ready
            pos_done pos_used routed run_done table rows_out pad_out cleared tx_done xT_ready up_done silu_done
            a_ready ta_done aT_ready dn_done yo_ready extra scat0 scat1 fin out_done""".split()
        s = {n: sem(n) for n in names}

        credits = sb("credits", [P, 32])
        given = [0]

        def credit():
            given[0] += 1
            return credits[:, given[0]:given[0] + 1]

        chained = [0]

        def link(eng, ins):
            chained[0] += 1
            ins.then_inc(s["chain"], 1)
            eng.wait_ge(s["chain"], chained[0])

        def layer_norm(dve, b, to, turned=0):
            for i in range(QT):
                st = nc.vector.bn_stats(ln_st[:, i, :], X[:, bass.ds(b * QT + i, 1), :].rearrange("p o d -> p (o d)"))
            st.then_inc(s["soft"], 1)
            dve.wait_ge(s["soft"], 3 * b + 1)
            dve.nop(nofuse=True)
            for i in range(QT):
                ag = nc.vector.bn_aggr(ln_mv[:, i, :], ln_st[:, i, :])
            ag.then_inc(s["ln_stats"], 1)
            dve.wait_ge(s["ln_sdev"], b + 1)
            nc.vector.reciprocal(ln_rs[:, :], ln_sd[:, :]).then_inc(s["soft"], 2)
            dve.wait_ge(s["soft"], 3 * b + 3)
            if turned:
                dve.wait_ge(s["tr_done"], turned)
            for i in range(QT):
                last = nc.vector.tensor_scalar(to(i), X[:, bass.ds(b * QT + i, 1), :].rearrange("p o d -> p (o d)"),
                                               ln_mv[:, i, 0:1], ln_rs[:, i:i + 1], ALU.subtract, ALU.mult)
            last.then_inc(s["xn_ready"], 1)

        x_in = [sem(f"x_in{b}") for b in range(B)]
        q_out = [sem(f"q_out{i}") for i in range(2)]
        q_in = [[sem(f"q_in{h}_{q}") for q in range(QT)] for h in range(2)]
        k_in = [s["k_in0"], s["k_in1"]]
        k0_in = [s["k0_in0"], s["k0_in1"]]
        STORES = 4 * PARTS

        def load_q(sp, b, h, q):
            sp.dma_start(Q[h][0:PR, q, :, :],
                         at(q_parts, b)[h].rearrange("j n d h t -> (j n d) h t")[:, :, q * P:q * P + P]
                         ).then_inc(q_in[h][q], 16)

        def load_k(sp, b, h, to, signal):
            sp.dma_start(to[h][0:PR, :, :], at(k_parts, b)[h].rearrange("n j d g t -> (n j d) g t")).then_inc(signal, 16)

        with nc.Block() as block:
            @block.sync
            def _(sp):
                def load_x(b):
                    sp.dma_start(X[:, b * QT:b * QT + QT, :], x[b].rearrange("(t p) d -> p t d", p=P)).then_inc(x_in[b], 16)
                sp.dma_start(c_sb, c_t.rearrange("(c p) b -> p c b", p=P)).then_inc(s["c_in"], 16)
                load_x(0)
                wm = wmod.rearrange("(c p) n -> p c n", p=P)
                sp.dma_start(wmod_sb[:, :, 0:GA * P], wm[:, :, 0:GA * P]).then_inc(s["wm_in"], 16)
                sp.dma_start(wq_sb, wq.rearrange("(c p) n -> p c n", p=P)).then_inc(s["w_in"], 16)
                sp.dma_start(wk_sb, wk.rearrange("(c p) n -> p c n", p=P)).then_inc(s["w_in"], 16)
                sp.dma_start(wv_sb, wv.rearrange("(c p) n -> p c n", p=P)).then_inc(s["w_in"], 16)
                load_x(1)
                sp.dma_start(wmod_sb[:, :, GA * P:], wm[:, :, GA * P:]).then_inc(s["wg_in"], 16)
                load_x(2)
                load_x(3)
                sp.dma_start(wo_sb[:, :, :], wo.rearrange("(s p) n -> p s n", p=P)).then_inc(s["wo_in"], 16)
                sp.dma_start(gate_sb[:, :, :], gate_t.rearrange("(c p) e -> p c e", p=P)).then_inc(s["gate_in"], 16)

                for b in range(B):
                    i = b % 2
                    sp.wait_ge(s["low_done"], b + 1)
                    for h in range(2):
                        for j in range(PARTS):
                            mine = parts[i][:, h, j, :].unsqueeze(1).to_broadcast([P, PARTS, T])
                            sp.dma_start(q_parts[b, h, j].rearrange("n d h t -> (d h) n t"), mine).then_inc(q_out[i], 16)
                        for n in range(PARTS):
                            sp.dma_start(k_parts[b, h, n].rearrange("j d g t -> (d g) j t"),
                                         parts[i][32 * h:32 * h + 32, 2, :, :]).then_inc(q_out[i], 16)
                    if b == 1:
                        sp.wait_ge(q_out[0], 16 * STORES)
                        sp.wait_ge(s["cleared_q"], 1)
                        for q in range(QT):
                            load_q(sp, 0, 0, q)
                            if q == 0:
                                load_k(sp, 0, 0, K0, k0_in[0])
                        load_k(sp, 0, 0, K, k_in[0])
                        load_k(sp, 0, 1, K0, k0_in[1])
                        for q in range(QT):
                            load_q(sp, 0, 1, q)

            @block.gpsimd
            def _(gp):
                n = [0]

                def step(ins):
                    n[0] += 1
                    ins.then_inc(s["pchain"], 1)
                    gp.wait_ge(s["pchain"], n[0])

                def low(b):
                    mid, low_ = parts[b % 2][:, :, 1, :], parts[b % 2][:, :, 2, :]
                    gp.wait_ge(s["mid_done"], 2 * b + 2)
                    nc.gpsimd.tensor_tensor(low_[:, 0:2], res[:, 0:2, :], mid[:, 0:2], ALU.subtract)
                    nc.gpsimd.tensor_tensor(low_[0:64, 2], res[0:64, 2, :], mid[0:64, 2],
                                            ALU.subtract).then_inc(s["low_done"], 1)

                step(nc.gpsimd.memset(ident[:, :], 0.0))
                nc.gpsimd.affine_select(out=ident[:, :], in_=ident[:, :], compare_op=ALU.not_equal, fill=1.0,
                                        base=0, pattern=[[-1, P]], channel_multiplier=1).then_inc(s["const_done"], 1)
                nc.gpsimd.memset(V, 1.0).then_inc(s["v_ones"], 1)
                for h in range(2):
                    nc.gpsimd.memset(Q[h][:, :, :, :], 0.0)
                    nc.gpsimd.memset(K[h][:, :, :], 1.0)
                    last = nc.gpsimd.memset(K0[h][:, :, :], 0.0)
                last.then_inc(s["cleared_q"], 1)
                gp.wait_ge(s["const_done"], 1)
                step(nc.gpsimd.tensor_copy(ident_bf[:, :], ident[:, :]))
                step(nc.gpsimd.memset(mask_qk[:, :, :], 0.0))
                step(nc.gpsimd.affine_select(out=mask_qk[:, :, :], in_=mask_qk[:, :, :], compare_op=ALU.is_ge,
                                             fill=NEG, base=0, pattern=[[0, REP], [-1, P]], channel_multiplier=1))
                for b in range(B):
                    low(b)
                step(nc.gpsimd.memset(before_bf[:, :], 1.0))
                step(nc.gpsimd.memset(ones_bf[:, :], 1.0))
                step(nc.gpsimd.memset(earlier[:, :, :], 1.0))
                step(nc.gpsimd.affine_select(out=before_bf[:, :], in_=before_bf[:, :], compare_op=ALU.is_gt,
                                             fill=0.0, base=0, pattern=[[1, P]], channel_multiplier=-1))
                step(nc.gpsimd.affine_select(out=earlier[:, :, :], in_=earlier[:, :, :], compare_op=ALU.is_gt,
                                             fill=0.0, base=0, pattern=[[1, E], [-1, E]], channel_multiplier=0))
                at_ = 0
                for step_, num, cm in ((REGION, E, 0), (P, E, 0), (P, NT, 1), (1, TOPK, 0), (1, TILES, 0),
                                       (P, TILES, 0), (0, 1, 1)):
                    step(nc.gpsimd.iota(counts_i[:, at_:at_ + num], [[step_, num]], 0, cm))
                    at_ += num
                step(nc.gpsimd.tensor_copy(counts[:, :], counts_i[:, :]))

            @block.scalar
            def _(act):
                def deviation(b):
                    act.wait_ge(s["ln_stats"], b + 1)
                    nc.scalar.activation(ln_sd[:, :], ln_mv[:, :, 1], ACT.Sqrt,
                                         bias=eps[:, :]).then_inc(s["ln_sdev"], 1)

                def modulate(b):
                    act.wait_ge(s["tr_done"], b + 1)
                    for c in range(DC):
                        nc.scalar.activation(hT[:, c, :], bank[:, c, :], ACT.Identity, bias=mod[:, SA + c, b:b + 1],
                                             scale=mod[:, CA + c, b:b + 1]).then_inc(s["h_ready"], 1)

                act.wait_ge(s["c_in"], 16)
                nc.scalar.activation(sc_sb, c_sb, ACT.Silu).then_inc(s["silu_c"], 1)
                deviation(0)
                act.wait_ge(s["mod_used"], 2)
                modulate(0)
                deviation(1)
                for b in range(B):
                    mine = parts[b % 2]
                    act.wait_ge(s["qkv_done"], b + 1)
                    if b >= 2:
                        act.wait_ge(q_out[b % 2], 16 * STORES * (b // 2))
                    nc.scalar.activation(mine[:, 0:2, 0, :], bank[:, 2:4, :], ACT.Copy).then_inc(s["qkv_high"], 1)
                    nc.scalar.activation(mine[0:64, 2, 0, :], bank[0:64, 4, :], ACT.Copy).then_inc(s["qkv_high"], 1)
                    if b == 0:
                        act.wait_ge(s["v_ones"], 1)
                    nc.scalar.activation(V[:, b * QT:b * QT + QT, :, 0:HD],
                                         bank[:, 5, 0:QT * 64].rearrange("p (t g d) -> p t g d", t=QT, g=NKV),
                                         ACT.Copy).then_inc(s["v_done"], 1)
                    if b + 1 < B:
                        modulate(b + 1)
                    act.wait_ge(s["res1"], b + 1)
                    nc.scalar.activation(mine[:, 0:2, 1, :], res[:, 0:2, :], ACT.Copy).then_inc(s["mid_done"], 1)
                    nc.scalar.activation(mine[0:64, 2, 1, :], res[0:64, 2, :], ACT.Copy).then_inc(s["mid_done"], 1)
                    if b + 2 < B:
                        deviation(b + 2)

            @block.vector
            def _(dve):
                def gates(b):
                    dve.wait_ge(s["gate_mm"], b + 1)
                    g_ps = bank[:, 6, :].rearrange("p (a n) -> p a n", a=2)
                    link(dve, nc.vector.tensor_scalar(gtmp, g_ps, -1.0, 0.25, ALU.mult, ALU.max))
                    link(dve, nc.vector.tensor_tensor(gtmp, g_ps, gtmp, ALU.max))
                    link(dve, nc.vector.tensor_scalar(gsgn, g_ps, 0.0, 2.0, ALU.is_ge, ALU.mult))
                    nc.vector.scalar_tensor_tensor(out=gate_bc[:, b, 0:2, :], in0=gsgn, scalar=-1.0, in1=gtmp,
                                                   op0=ALU.add, op1=ALU.mult)
                    nc.vector.tensor_copy(gate_bc[:, b, 2, :], bank[:, 7, 0:D])
                    nc.vector.tensor_scalar(gate_bc[:, b, 3, :], bank[:, 7, D:2 * D], 1.0, None,
                                            ALU.add).then_inc(s["gate_used"], 1)
                    dve.wait_ge(s["gate_used"], b + 1)

                def norm(b):
                    dve.wait_ge(x_in[b], 16)
                    layer_norm(dve, b, lambda i: xn[:, i, :], turned=b)

                link(dve, nc.vector.memset(eps[:, :], EPS))
                norm(0)
                dve.wait_ge(s["mod_done"], 1)
                mod_ps = bank[:, 7, 0:2 * DC * B].rearrange("p (m b) -> p m b", b=B)
                nc.vector.tensor_copy(mod[:, SA:SA + DC, :], mod_ps[:, SA:SA + DC, :]).then_inc(s["mod_used"], 1)
                nc.vector.tensor_scalar(mod[:, CA:CA + DC, :], mod_ps[:, CA:CA + DC, :], 1.0, None,
                                        ALU.add).then_inc(s["mod_used"], 1)
                nc.vector.tensor_copy(sc_bc, sc_sb.unsqueeze(3).to_broadcast([P, DC, B, P])).then_inc(s["sc_bcast"], 1)
                norm(1)
                for b in range(B):
                    dve.wait_ge(s["qkv_high"], 2 * b + 2)
                    if b > 0:
                        dve.wait_ge(s["low_done"], b)
                    mine = parts[b % 2]
                    nc.vector.tensor_tensor(res[:, 0:2, :], bank[:, 2:4, :], mine[:, 0:2, 0, :], ALU.subtract)
                    nc.vector.tensor_tensor(res[0:64, 2, :], bank[0:64, 4, :], mine[0:64, 2, 0, :],
                                            ALU.subtract).then_inc(s["res1"], 1)
                    if b + 2 < B:
                        norm(b + 2)
                    gates(b)

            @block.tensor
            def _(pe):
                def turn(b):
                    pe.wait_ge(s["xn_ready"], b + 1)
                    if b > 0:
                        pe.wait_ge(s["h_ready"], DC * b)
                    for c in range(DC):
                        for i in range(QT):
                            last = nc.tensor.transpose(bank[:, c, i * P:i * P + P], xn[:, i, c * P:c * P + P], ident[:, :])
                    last.then_inc(s["tr_done"], 1)

                pe.wait_ge(s["wm_in"], 16)
                pe.wait_ge(s["silu_c"], 1)
                for m in range(2 * DC):
                    for c in range(DC):
                        last = nc.tensor.matmul(bank[:, 7, m * B:m * B + B], wmod_sb[:, c, m * P:m * P + P],
                                                sc_sb[:, c, :], start=(c == 0), stop=(c == DC - 1),
                                                skip_group_check=True)
                last.then_inc(s["mod_done"], 1)
                pe.wait_ge(s["const_done"], 1)
                turn(0)
                pe.wait_ge(s["w_in"], 48)
                for b in range(B):
                    pe.wait_ge(s["h_ready"], DC * b + DC)
                    if b > 0:
                        pe.wait_ge(s["res1"], b)
                        pe.wait_ge(s["v_done"], b)
                    for m in range(2):
                        for c in range(DC):
                            nc.tensor.matmul(bank[:, 2 + m, :], wq_sb[:, c, m * P:m * P + P], hT[:, c, :],
                                             start=(c == 0), stop=(c == DC - 1))
                    for c in range(DC):
                        nc.tensor.matmul(bank[0:64, 4, :], wk_sb[:, c, :], hT[:, c, :],
                                         start=(c == 0), stop=(c == DC - 1))
                    for i in range(QT):
                        for c in range(DC):
                            last = nc.tensor.matmul(bank[:, 5, i * 64:i * 64 + 64], hT[:, c, i * P:i * P + P],
                                                    wv_sb[:, c, :], start=(c == 0), stop=(c == DC - 1),
                                                    skip_group_check=True)
                    last.then_inc(s["qkv_done"], 1)
                    if b + 1 < B:
                        turn(b + 1)
                    if b == 0:
                        pe.wait_ge(s["wg_in"], 16)
                        pe.wait_ge(s["sc_bcast"], 1)
                        pe.wait_ge(s["mod_used"], 2)
                    else:
                        pe.wait_ge(s["gate_used"], b)
                    for a, m in enumerate((GA, GB, SB, CB)):
                        for c in range(DC):
                            last = nc.tensor.matmul(bank[:, 6 + a // 2, a % 2 * D:a % 2 * D + D], sc_bc[:, c, b, :],
                                                    wmod_sb[:, c, m * P:m * P + D], start=(c == 0),
                                                    stop=(c == DC - 1), skip_group_check=True)
                    last.then_inc(s["gate_mm"], 1)

        E_END = [sum(E_UNITS[:q + 1]) for q in range(QT)]
        E_TOT, S_TOT = sum(E_UNITS), sum(S_UNITS)
        S_AT = {(q, g): sum(S_UNITS[:q]) + (g // 2 if q == 0 else g * S_UNITS[q] // GH) for q in range(QT) for g in range(GH)}
        E_AT = {(q, g): sum(E_UNITS[:q]) + g * E_UNITS[q] // GH for q in range(QT) for g in range(GH)}
        MISC, OBANK = 7, 6
        TURNS, WO_USES = 4, 2

        def misc_base(b, h):
            return 3 if first(b, h) else 3 + (2 * TURNS + WO_USES) * b - (0 if h else WO_USES) + TURNS * h

        def first(b, h):
            return isinstance(b, int) and (b, h) == (0, 0)

        def turn_use(b, h, q):
            return misc_base(b, h) + (0 if q == QT - 1 else q + 1)

        def project_use(b, g):
            return misc_base(b, 0) + TURNS + g - 2

        nm_in = [sem("nm_in_even"), sem("nm_in_odd")]
        y_out = [sem("y_out0"), sem("y_out1")]
        y_in = [sem("y_in0"), sem("y_in1")]
        nm_rows = [nm_row, nm_row2]

        def s_units(q, g):
            return g % 2 if q == 0 else S_UNITS[q] // GH

        def s_heads(q, g, k):
            return (g - 1) * REP if q == 0 else g * REP + 2 * k * s_banks(q)[0]

        def s_banks(q):
            return {0: 4, 1: 2, 2: 1, 3: 1}[q], (q + 1) * P

        def prev(b, h):
            return (b, 0) if h else (b - 1, 1)

        def fetch_values(sp, b, h):
            sp.wait_ge(s["y_ready"], 2 * b + h + 1)
            sp.wait_ge(y_out[h], 16 + 128 * b + 128)
            sp.nop(nofuse=True)
            for k in range(2):
                sp.dma_start(Yp[k][:, :], y_parts[h, k].rearrange("g r d t -> (g r d) t")).then_inc(y_in[h], 16)

        def invert(dve, b, h, q):
            dve.wait_ge(y_in[h], 32 * b + 32)
            nc.vector.reciprocal(Yp[1][:, q * P:q * P + P], Yp[1][:, q * P:q * P + P]).then_inc(s["inverted"], 1)

        def normalise(dve, b, h):
            dve.wait_ge(s["inverted"], 4 * (2 * b + h) + 4)
            nc.vector.tensor_tensor(Y[h][:, :], Yp[0][:, :], Yp[1][:, :], ALU.mult).then_inc(s["y_ready"], 1)

        def turn_banks(b):
            return ((0, 1), 2) if b == 0 else ((3, 4), 5) if b == 1 else ((7, 6), 7)

        def turn(pe, b):
            (k0, k1), _ = turn_banks(b)
            pe.wait_ge(s["norm2"], b + 1)
            if b == B - 1:
                pe.wait_ge(s["ys_ready"], 2)
            for c, k in enumerate((k0, k1)):
                for i in range(QT):
                    last = nc.tensor.transpose(bank[:, k, i * P:i * P + P],
                                               rows[:, b * QT + i, c * P:c * P + P], ident[:, :])
            last.then_inc(s["tr_done"], 1)

        def out_of_psum_turned(act, b):
            act.wait_ge(s["tr_done"], B + b + 1)
            for c, k in enumerate(turn_banks(b)[0]):
                nc.scalar.activation(h2T[:, c, b * T:b * T + T], bank[:, k, :], ACT.Copy).then_inc(s["h_ready"], 1)

        def norm_start(dve, b0, b1):
            for t in range(b0 * QT, b1 * QT):
                last = nc.vector.bn_stats(norm_st[:, t, :], X[:, t, :])
            last.then_inc(s["norm_st"], 1)
            dve.wait_ge(s["norm_st"], 1 + (b0 > 0))
            for t in range(b0 * QT, b1 * QT):
                last = nc.vector.bn_aggr(norm_mv[:, t, :], norm_st[:, t, :])
            last.then_inc(s["norm_mv"], 1)
            dve.wait_ge(s["norm_mv"], 1 + (b0 > 0))
            for t in range(b0 * QT, b1 * QT):
                last = nc.vector.scalar_tensor_tensor(out=rows[:, t, 0:D], in0=X[:, t, :], scalar=norm_mv[:, t, 0:1],
                                                      in1=gate_bc[:, t // QT, 3, :], op0=ALU.subtract, op1=ALU.mult)
            last.then_inc(s["centred"], 1)

        def deviation(act, b0, b1):
            act.wait_ge(s["norm_mv"], 1 + (b0 > 0))
            nc.scalar.activation(norm_sd[:, b0 * QT:b1 * QT], norm_mv[:, b0 * QT:b1 * QT, 1], ACT.Sqrt,
                                 bias=eps[:, :]).then_inc(s["ln_sdev"], 1)

        def norm_end(dve, b0, b1):
            dve.wait_ge(s["ln_sdev"], B + 1 + (b0 > 0))
            nc.vector.reciprocal(norm_rs[:, b0 * QT:b1 * QT], norm_sd[:, b0 * QT:b1 * QT]).then_inc(s["inverse_sd"], 1)
            dve.wait_ge(s["centred"], 1 + (b0 > 0))
            dve.wait_ge(s["inverse_sd"], 1 + (b0 > 0))
            for t in range(b0 * QT, b1 * QT):
                last = nc.vector.scalar_tensor_tensor(out=rows[:, t, 0:D], in0=rows[:, t, 0:D],
                                                      scalar=norm_rs[:, t:t + 1], in1=gate_bc[:, t // QT, 2, :],
                                                      op0=ALU.mult, op1=ALU.add)
                if t % QT == QT - 1:
                    last.then_inc(s["norm2"], 1)

        PLACE = {}
        at_ = 0
        for name, num in (("first", E), ("k128", E), ("token", NT), ("slot", TOPK), ("tile", TILES),
                          ("tile128", TILES), ("partition", 1)):
            PLACE[name] = counts[:, at_:at_ + num]
            at_ += num
        ys_out = [s["ys_out0"], s["ys_out1"]]

        STEPS = 4
        TURNS_ = (TILES - 2) // STEPS
        xt_in = [sem(f"xt_in{i}") for i in range(STEPS)]
        scat = [s["scat0"], s["scat1"]]
        back = [sem(f"y_back{b}") for b in range(B)]
        def over_tiles(eng, one):
            with eng.Fori(0, TURNS_) as trip:
                for i in range(STEPS):
                    one(STEPS * trip + i, i, True, True)
            for t in range(STEPS * TURNS_, TILES):
                one(t, t % STEPS, t + 1 < TILES, t + 2 < TILES)

        with nc.Block() as block:
            @block.sync
            def _(sp):
                def load_kv(b, h):
                    load_k(sp, b, h, K, k_in[h])
                    sp.dma_start(Vc[h][:, :, :, :],
                                 V[:, bass.ds(b * QT, QT), h * GH:h * GH + GH, :]).then_inc(k_in[h], 16)

                def put_negm(b, h, q):
                    sp.wait_ge(s["nm_split"], 8 + 16 * (2 * b + h) + 4 * q + 4)
                    sp.nop(nofuse=True)
                    for j in range(PARTS):
                        sp.dma_start(Q[h][PR + j:PR + j + 1, q, :, :],
                                     nm_parts[q % 2][:, j, :]).then_inc(nm_in[q % 2], 16)

                def send_values(b, h):
                    sp.wait_ge(s["o_free"], 1 + 4 * (2 * b + h) + 4)
                    sp.nop(nofuse=True)
                    for g in range(GH):
                        for k in range(2):
                            sp.dma_start(y_parts[h, k, g].rearrange("r d t -> d r t"),
                                         O[h][32 * g + HD * k:32 * g + HD * k + HD, :, :]).then_inc(y_out[h], 16)

                def half(b, h, loads=True, nxt=True, back=True):
                    u = 2 * b + h
                    put_negm(b, h, QT - 1)
                    if loads:
                        sp.wait_ge(s["s_ready"], S_TOT * u + S_TOT)
                        sp.nop(nofuse=True)
                        load_k(sp, b + 1, h, K0, k0_in[h])
                    if nxt:
                        if back:
                            sp.wait_ge(s["av_done"], 2 + 4 * u)
                            sp.nop(nofuse=True)
                        load_kv(b + h, 1 - h)
                    if back:
                        send_values(*prev(b, h))
                    for q in range(QT):
                        if q == 1 and back:
                            fetch_values(sp, *prev(b, h))
                        if nxt and q > 0:
                            put_negm(b + h, 1 - h, q - 1)
                        if loads:
                            sp.wait_ge(s["st_ready"], E_TOT * u + E_END[q])
                            sp.nop(nofuse=True)
                            load_q(sp, b + 1, h, q)

                sp.dma_start(Vc[0], V[:, 0:QT, 0:GH, :]).then_inc(k_in[0], 16)
                for i in range(2):
                    sp.wait_ge(q_out[i], 16 * STORES * (B // 2))
                for q in range(QT - 1):
                    put_negm(0, 0, q)
                half(0, 0, back=False)
                with sp.Fori(0, B - 2) as b:
                    half(b, 1)
                    half(b + 1, 0)
                half(B - 2, 1)
                half(B - 1, 0, loads=False)
                half(B - 1, 1, loads=False, nxt=False)
                send_values(B - 1, 1)

                sp.wait_ge(s["st_ready"], E_TOT * 2 * B)
                sp.dma_start(ws_up, shared_up_t.rearrange("(c p) n -> p c n", p=P)).then_inc(s["ws_up_in"], 16)
                fetch_values(sp, B - 1, 1)
                for k, w in enumerate(SCHUNKS):
                    sp.dma_start(ws_down[0:w, k, :], shared_down_t[k * P:k * P + w, :]).then_inc(s["ws_in"], 16)
                sp.wait_ge(s["filled"], 1)
                zeros = fill[:, 0:D].unsqueeze(1).to_broadcast([P, NT + 1, D])
                sp.dma_start(y_sum[1].rearrange("(t p) d -> p t d", p=P), zeros).then_inc(s["y_zero"], 16)
                sp.dma_start(y_sum[0][NT * P:, :], fill[:, 0:D]).then_inc(s["y_zero"], 16)
                sp.dma_start(x_rows[DUMMY:, :], fill[:, :]).then_inc(s["pad_out"], 16)
                sp.wait_ge(s["av_done"], 2 + 4 * 2 * B)
                for c in range(DC):
                    sp.dma_start(w_up[:, :, c, :],
                                 up_t[:, c * P:c * P + P, :].rearrange("e p n -> p e n")).then_inc(s["wu_in"], 16)
                sp.dma_start(w_down[0], down_t[:, 0:P, :].rearrange("e p n -> p e n")).then_inc(s["wd_in"], 16)
                sp.wait_ge(s["wd_zero"], 1)
                sp.dma_start(w_down[1][0:I1], down_t[:, P:I, :].rearrange("e p n -> p e n")).then_inc(s["wd_in"], 16)
                sp.wait_ge(s["run_done"], 1)
                with sp.Fori(0, E // 4) as e4:
                    for i in range(4):
                        row = sp.value_load(pad_row[0:1, bass.ds(4 * e4 + i, 1)], min_val=0, max_val=DUMMY - P)
                        sp.dma_start(x_rows[bass.ds(row, P), :], fill[:, :]).then_inc(s["pad_out"], 16)

                sp.wait_ge(s["sh_down"], 2 * B)
                def load(t, i):
                    sp.nop(nofuse=True)
                    row = sp.value_load(tile_row[0:1, bass.ds(t, 1)], min_val=0, max_val=DUMMY)
                    sp.dma_start(xt[i], x_rows[bass.ds(row, P), :]).then_inc(xt_in[i], 16)

                sp.wait_ge(s["table"], 1)
                sp.wait_ge(s["rows_out"], 16 * NT * TOPK)
                sp.wait_ge(s["pad_out"], 16 * (E + 1))
                for t in range(STEPS):
                    load(t, t)

                def one(t, i, more, far):
                    sp.wait_ge(s["tx_done"], 2 + t + 1)
                    sp.nop(nofuse=True)
                    sp.wait_ge(s["extra"], t + 1)
                    load(t + STEPS, i)
                full = (TILES - STEPS) // STEPS
                with sp.Fori(0, full) as trip:
                    for i in range(STEPS):
                        one(STEPS * trip + i, i, True, True)
                for t in range(STEPS * full, TILES - STEPS):
                    one(t, t % STEPS, True, True)
                for i in range(2):
                    sp.wait_ge(scat[i], 16 * ((TILES + 1 - i) // 2))
                for b in range(B):
                    for i in range(2):
                        sp.dma_start(y_back[:, b, i], y_sum[i][b * T:b * T + T, :].rearrange("(t p) d -> p t d", p=P)
                                     ).then_inc(back[b], 16)
                for b in range(B):
                    sp.wait_ge(s["fin"], 3 * b + 3)
                    sp.dma_start(out[b].rearrange("(t p) d -> p t d", p=P),
                                 X[:, b * QT:b * QT + QT, :]).then_inc(s["out_done"], 16)
                sp.wait_ge(s["out_done"], 16 * B)

            @block.tensor
            def _(pe):
                def q_first(q):
                    return 1 if q == 0 else 0

                def scores_for_max(b, h, q, g, k):
                    u = 2 * b + h
                    if g == q_first(q) and k == 0:
                        pe.wait_ge(q_in[h][q], 16 * b + 16)
                        if q == 0:
                            pe.wait_ge(k0_in[h], 16 * b + 16)
                    heads, n = s_banks(q)
                    unit = S_TOT * u + S_AT[q, g] + k
                    buf = 2 * ((S_AT[q, g] + k) % 2)
                    pe.wait_ge(s["s_free"], unit + 1)
                    for j in range(2):
                        for i in range(heads):
                            head = s_heads(q, g, k) + j * heads + i
                            nc.tensor.matmul(bank[:, buf + j, i * n:i * n + n], Q[h][0:KR, q, head, :],
                                             K0[h][0:KR, head // REP, 0:n], start=(i == 0), stop=False,
                                             skip_group_check=True)
                        view = bank[:, buf + j, 0:heads * n].rearrange("p (i n) -> p i n", i=heads)
                        last = nc.tensor.matmul(view[:, :, n - P:n], ident_bf[:, :], mask_qk[:, 0:heads, :],
                                                start=False, stop=True, skip_group_check=True)
                    last.then_inc(s["s_ready"], 1)

                def scores(b, h, q, g, k):
                    u = 2 * b + h
                    if g == 0 and k == 0:
                        pe.wait_ge(nm_in[q % 2], 16 + 48 * (2 * u + q // 2) + 48)
                        if q == 0:
                            pe.wait_ge(k_in[h], 16 * 2 * b + 16 * 2)
                    unit = E_TOT * u + E_AT[q, g] + k
                    buf = 4 + (E_AT[q, g] + k) % 2
                    pe.wait_ge(s["st_free"], unit + 1)
                    nc.tensor.matmul(bank[:, buf, :], K[h][0:KR, g, k * P:(k + 1) * P],
                                     Q[h][0:KR, q, g * REP:g * REP + REP, :], start=True, stop=True,
                                     skip_group_check=True).then_inc(s["st_ready"], 1)

                def weigh_values(b, h, q):
                    u = 2 * b + h
                    pe.wait_ge(s["p_ready"], 16 * u + 4 * q + 4)
                    pe.wait_ge(s["o_free"], 4 * u + q + 1)
                    for kt in range(q + 1):
                        for g in range(GH):
                            last = nc.tensor.matmul(bank[32 * g:32 * g + 32, OBANK, :], Vc[h][:, kt, g, :],
                                                    pool[:, q % 2, g * QT + kt, :], start=(kt == 0), stop=(kt == q),
                                                    skip_group_check=True)
                    last.then_inc(s["av_done"], 1)

                def turn_max(b, h, q, use):
                    u = 2 * b + h
                    pe.wait_ge(s["s_free"], 2 + S_TOT * u + sum(S_UNITS[:q + 1]))
                    pe.wait_ge(s["misc_free"], use + 1)
                    nc.tensor.transpose(bank[0:HH, MISC, 0:P], negm[h][:, q, :], ident[:, :]).then_inc(s["misc_ready"], 1)

                def project(b, w, use):
                    pe.wait_ge(s["y_ready"], 1 + 2 * b + 2)
                    pe.wait_ge(s["misc_free"], use + 1)
                    for i in range(2):
                        t = (2 * w + i) * P
                        for h in range(2):
                            last = nc.tensor.matmul(bank[:, MISC, i * D:i * D + D], Y[h][:, t:t + P], wo_sb[:, h, :],
                                                    start=(h == 0 and i == 0), stop=(h == 1), skip_group_check=True)
                    last.then_inc(s["misc_ready"], 1)

                def half(b, h, nxt=True, back=True):
                    for q in range(QT):
                        for g in range(GH):
                            ne, ns = q + 1, (s_units(q, g) if nxt else 0)
                            for k in range(ne):
                                scores(b, h, q, g, k)
                                for j in range(k * ns // ne, (k + 1) * ns // ne):
                                    scores_for_max(b + h, 1 - h, q, g, j)
                            if g == 1 and q > 0:
                                weigh_values(b, h, q - 1)
                            elif g == 1 and back:
                                weigh_values(*prev(b, h), QT - 1)
                            if g == 2 and q == 0:
                                turn_max(b, h, QT - 1, turn_use(b, h, QT - 1))
                            elif g == 2 and nxt:
                                turn_max(b + h, 1 - h, q - 1, turn_use(b, h, q - 1))
                            if h == 0 and back and q == 3 and g >= 2:
                                project(b - 1, g - 2, project_use(b, g))

                pe.wait_ge(s["wo_in"], 16)
                for q in range(QT):
                    for g in range(GH):
                        for k in range(s_units(q, g)):
                            scores_for_max(0, 0, q, g, k)
                    if q > 0:
                        turn_max(0, 0, q - 1, q - 1)
                half(0, 0, back=False)
                with pe.Fori(0, B - 1) as b:
                    half(b, 1)
                    half(b + 1, 0)
                half(B - 1, 1, nxt=False)
                pe.wait_ge(s["s_free"], 2 + S_TOT * 2 * B)
                turn(pe, 0)
                weigh_values(B - 1, 1, QT - 1)

                pe.wait_ge(s["st_free"], 2 + E_TOT * 2 * B)
                pe.wait_ge(s["o_free"], 1 + 4 * 2 * B)
                pe.wait_ge(s["misc_free"], 1 + misc_base(B - 1, 1) + 1)
                def logits(b):
                    _, k2 = turn_banks(b)
                    pe.wait_ge(s["h_ready"], DC * (B + b) + DC)
                    for i in range(QT):
                        for c in range(DC):
                            t = b * T + i * P
                            last = nc.tensor.matmul(bank[:, k2, i * E:i * E + E], h2T[:, c, t:t + P], gate_sb[:, c, :],
                                                    start=(i == 0 and c == 0), stop=(c == DC - 1),
                                                    skip_group_check=True)
                    last.then_inc(s["lg_done"], 1)

                def shared_up(n, k):
                    v = 3 * n + k
                    if n > 0:
                        pe.wait_ge(s["sh_a"], v - 2)
                    w = SCHUNKS[k]
                    for i in range(2):
                        c0 = i * 2 * I + k * P
                        for c in range(DC):
                            last = nc.tensor.matmul(bank[0:w, 2 * k + i, :], ws_up[:, c, c0:c0 + w],
                                                    h2T[:, c, n * T:n * T + T], start=(c == 0), stop=(c == DC - 1))
                    last.then_inc(s["sh_up"], 1)

                def shared_down(n, h):
                    pe.wait_ge(s["sh_a"], 3 * n + 3)
                    if n > 0:
                        pe.wait_ge(s["ys_ready"], 2 * n - 1 + h)
                    if h == 0:
                        pe.wait_ge(s["lg_ready"], 3 if n == 0 else B)
                    elif n < B - 1:
                        pe.wait_ge(s["pos_used"], n + 2)
                    for i in range(2):
                        tok = (2 * h + i) * P
                        for k, w in enumerate(SCHUNKS):
                            last = nc.tensor.matmul(bank[:, 7 - h, i * D:i * D + D], aT[n % 2][0:w, k, tok:tok + P],
                                                    ws_down[0:w, k, :], start=(i == 0 and k == 0), stop=(k == 2),
                                                    skip_group_check=True)
                    last.then_inc(s["sh_down"], 1)

                def positions(m):
                    pe.wait_ge(s["sel_ready"], m + 1)
                    if m == 1:
                        pe.wait_ge(s["added"], 3)
                    if m > 1:
                        pe.wait_ge(s["ys_ready"], 2 * m - 2)
                    flat = sel_bf[:, :, :].rearrange("p t e -> p (t e)")
                    nc.tensor.matmul(bank[:, 6, 0:QT * E], before_bf[:, :], flat, start=True, stop=False,
                                     skip_group_check=True)
                    for i in range(1, QT):
                        nc.tensor.matmul(bank[:, 6, i * E:QT * E], ones_bf[:, :], flat[:, 0:(QT - i) * E],
                                         start=False, stop=(i == QT - 1), skip_group_check=True)
                    for i in range(QT):
                        last = nc.tensor.matmul(bank[:, 6, QT * E:QT * E + E], ones_bf[:, :],
                                                flat[:, i * E:i * E + E], start=False, stop=(i == QT - 1),
                                                skip_group_check=True)
                    last.then_inc(s["pos_done"], 1)

                def project_last(w):
                    if w == 0:
                        pe.wait_ge(s["y_ready"], 1 + 2 * B)
                    else:
                        pe.wait_ge(s["pos_used"], 1)
                    for i in range(2):
                        t = (2 * w + i) * P
                        for h in range(2):
                            last = nc.tensor.matmul(bank[:, 7 - w, i * D:i * D + D], Y[h][:, t:t + P], wo_sb[:, h, :],
                                                    start=(h == 0 and i == 0), stop=(h == 1), skip_group_check=True)
                    last.then_inc(s["y_mm"], 1)

                pe.wait_ge(s["gate_in"], 16)
                logits(0)
                turn(pe, 1)
                turn(pe, 2)
                logits(1)
                logits(2)
                pe.wait_ge(s["ws_up_in"], 16)
                positions(0)
                for m in range(B):
                    for k in range(3):
                        if m == 0:
                            pe.wait_ge(s["lg_ready"], min(k + 1, 2))
                        shared_up(m, k)
                        if k == 0 and m == B - 1:
                            positions(m)
                    if m == 1:
                        pe.wait_ge(s["lg_ready"], 3)
                        project_last(0)
                        project_last(1)
                    if m == 2:
                        turn(pe, B - 1)
                        logits(B - 1)
                    if m not in (0, B - 1):
                        positions(m)
                    if m > 0:
                        pe.wait_ge(s["ws_in"], 48)
                        shared_down(m - 1, 0)
                        shared_down(m - 1, 1)
                shared_down(B - 1, 0)
                shared_down(B - 1, 1)

                pe.wait_ge(s["sh_a"], 3 * B)
                pe.wait_ge(s["ys_ready"], 2 * B)
                def turn_rows(t, i):
                    pe.wait_ge(xt_in[i % STEPS], 16 * (t // STEPS) + 16)
                    for c in range(DC):
                        last = nc.tensor.transpose(bank[:, i % 2, c * P:c * P + P],
                                                   xt[i % STEPS][:, c * P:c * P + P], ident[:, :])
                    last.then_inc(s["tx_done"], 1)

                def expert_of(t):
                    return pe.value_load(tile_expert[0:1, bass.ds(t, 1)], min_val=0, max_val=E - 1)

                def up(t, i, e):
                    w = w_up.rearrange("p e c n -> p (e c n)")
                    pe.wait_ge(s["xT_ready"], 2 + t + 1)
                    pe.wait_ge(s["a_ready"], t + 1)
                    for c in range(DC):
                        last = nc.tensor.matmul(bank[:, 2 + i % 2, 0:2 * I], xT[i % 2][:, c, :],
                                                w[:, bass.ds(e * (DC * 2 * I) + c * 2 * I, 2 * I)],
                                                start=(c == 0), stop=(c == DC - 1))
                    last.then_inc(s["up_done"], 1)

                def turn_act(t, i):
                    pe.wait_ge(s["a_ready"], 2 + t + 1)
                    pe.wait_ge(s["aT_ready"], t + 1)
                    nc.tensor.transpose(bank[:, 4 + i % 2, 0:P], act_g[i % 2][:, 0:P], ident[:, :])
                    nc.tensor.transpose(bank[0:I1, 4 + i % 2, P:2 * P], act_g[i % 2][:, P:I],
                                        ident[:, :]).then_inc(s["ta_done"], 1)

                def down(t, i, e):
                    pe.wait_ge(s["aT_ready"], 2 + t + 1)
                    pe.wait_ge(s["yo_ready"], t + 1)
                    for c in range(2):
                        w = w_down[c].rearrange("p e n -> p (e n)")
                        last = nc.tensor.matmul(bank[:, 6 + i % 2, 0:D], actT[i % 2][:, c, :],
                                                w[:, bass.ds(e * D, D)], start=(c == 0), stop=(c == 1))
                    last.then_inc(s["dn_done"], 1)

                pe.wait_ge(s["table"], 1)
                pe.wait_ge(s["wu_in"], 32)
                pe.wait_ge(s["wd_in"], 32)
                pe.wait_ge(s["xT_ready"], 2)
                turn_rows(0, 0)
                turn_rows(1, 1)
                up(0, 0, expert_of(0))

                with pe.Fori(0, TURNS_) as trip:
                    e = None
                    for i in range(STEPS):
                        t = STEPS * trip + i
                        e_next = expert_of(t + 1)
                        turn_act(t, i)
                        up(t + 1, i + 1, e_next)
                        pe.wait_ge(s["xT_ready"], t + 3)
                        pe.wait_ge(xt_in[(i + 2) % STEPS], 16 * trip + 16 * ((i + 2) // STEPS) + 16)
                        j = (i + 2) % STEPS
                        for c in range(DC):
                            last = nc.tensor.transpose(bank[:, j % 2, c * P:c * P + P],
                                                       xt[j][:, c * P:c * P + P], ident[:, :])
                        last.then_inc(s["tx_done"], 1)
                        down(t, i, expert_of(t) if e is None else e)
                        e = e_next
                for t in range(STEPS * TURNS_, TILES):
                    turn_act(t, t % STEPS)
                    if t + 1 < TILES:
                        up(t + 1, (t + 1) % STEPS, expert_of(t + 1))
                    if t + 2 < TILES:
                        pe.wait_ge(s["xT_ready"], t + 3)
                        turn_rows(t + 2, (t + 2) % STEPS)
                    down(t, t % STEPS, expert_of(t))

            @block.scalar
            def _(act):
                def out_of_psum(b, h, q):
                    m = 4 * (2 * b + h) + q
                    act.wait_ge(s["av_done"], 2 + m + 1)
                    if q == 0:
                        act.wait_ge(y_out[h], 128 * b + 16)
                    nc.scalar.activation(O[h][:, :, q * P:q * P + P],
                                         bank[:, OBANK, :].rearrange("p (r t) -> p r t", r=REP),
                                         ACT.Copy).then_inc(s["o_free"], 1)

                def half(b, h, back=True, norm=False):
                    u = 2 * b + h
                    for q in range(QT):
                        act.wait_ge(s["av_done"], 4 * u + q + 1)
                        for g in range(GH):
                            for kt in range(q + 1):
                                unit = E_TOT * u + E_AT[q, g] + kt
                                buf = 4 + (E_AT[q, g] + kt) % 2
                                act.wait_ge(s["st_ready"], unit + 1)
                                nc.scalar.activation(pool[:, q % 2, g * QT + kt, :], bank[:, buf, :], ACT.Exp,
                                                     scale=SCALE).then_inc(s["st_free"], 1)
                            if norm and (q, g) == (QT - 1, 0):
                                deviation(act, 0, B - 1)
                            if g == 2 and q > 0:
                                out_of_psum(b, h, q - 1)
                            elif g == 2 and back:
                                out_of_psum(*prev(b, h), QT - 1)
                half(0, 0, back=False)
                with act.Fori(0, B - 1) as b:
                    half(b, 1)
                    half(b + 1, 0)
                half(B - 1, 1, norm=True)
                out_of_psum(B - 1, 1, QT - 1)
                out_of_psum_turned(act, 0)

                def logits_out(b):
                    act.wait_ge(s["lg_done"], b + 1)
                    nc.scalar.activation(logit[:, b * QT:b * QT + QT, :],
                                         bank[:, turn_banks(b)[1], 0:QT * E].rearrange("p (i e) -> p i e", i=QT),
                                         ACT.Copy).then_inc(s["lg_ready"], 1)

                def exponential(m):
                    act.wait_ge(s["subtracted"], m + 1)
                    nc.scalar.activation(rt[:, 0], rt[:, 0], ACT.Exp).then_inc(s["exp_l"], 1)

                def shared_silu(n, k):
                    v = 3 * n + k
                    act.wait_ge(s["sh_up"], v + 1)
                    if n > 0:
                        act.wait_ge(s["sh_a"], v - 2)
                    nc.scalar.activation(sg[k][0:SCHUNKS[k]], bank[0:SCHUNKS[k], 2 * k, :],
                                         ACT.Silu).then_inc(s["sh_silu"], 1)

                def store(n):
                    for h in range(2):
                        act.wait_ge(s["sh_down"], 2 * n + h + 1)
                        if n > 0:
                            act.wait_ge(ys_out[h], 16 * n)
                        nc.scalar.activation(y_shared[:, h], bank[:, 7 - h, :].rearrange("p (t d) -> p t d", t=2),
                                             ACT.Copy).then_inc(s["ys_ready"], 1)
                        act.wait_ge(s["ys_ready"], 2 * n + h + 1)
                        t = n * T + 2 * h * P
                        act.dma_start(y_sum[0][t:t + 2 * P, :].rearrange("(t p) d -> p t d", p=P),
                                      y_shared[:, h]).then_inc(ys_out[h], 16)

                logits_out(0)
                exponential(0)
                act.wait_ge(y_out[0], 16 + 128 * B)
                out_of_psum_turned(act, 1)
                logits_out(1)
                out_of_psum_turned(act, 2)
                logits_out(2)
                for m in range(B):
                    for k in range(3):
                        shared_silu(m, k)
                    if m == 2:
                        out_of_psum_turned(act, B - 1)
                        logits_out(B - 1)
                    if m + 1 < B:
                        exponential(m + 1)
                    if m > 0:
                        store(m - 1)
                    if m == 1:
                        deviation(act, B - 1, B)
                store(B - 1)

                def rows_out_of_psum(t, i):
                    act.wait_ge(s["tx_done"], 2 + t + 1)
                    act.wait_ge(s["up_done"], t + 1)
                    nc.scalar.activation(xT[i % 2].rearrange("p c n -> p (c n)"), bank[:, i % 2, 0:DC * P],
                                         ACT.Copy).then_inc(s["xT_ready"], 1)

                def silu(t, i):
                    act.wait_ge(s["up_done"], 2 + t + 1)
                    act.wait_ge(s["ta_done"], t + 1)
                    nc.scalar.activation(act_g[i % 2], bank[:, 2 + i % 2, 0:I], ACT.Silu).then_inc(s["silu_done"], 1)

                def act_out_of_psum(t, i):
                    act.wait_ge(s["ta_done"], 2 + t + 1)
                    act.wait_ge(s["dn_done"], t + 1)
                    nc.scalar.activation(actT[i % 2][:, 0, :], bank[:, 4 + i % 2, 0:P], ACT.Copy)
                    nc.scalar.activation(actT[i % 2][0:I1, 1, :], bank[0:I1, 4 + i % 2, P:2 * P],
                                         ACT.Copy).then_inc(s["aT_ready"], 1)

                act.wait_ge(s["sh_down"], 2 * B)
                act.wait_ge(s["cleared"], 1)
                rows_out_of_psum(0, 0)
                rows_out_of_psum(1, 1)
                silu(0, 0)

                def one(t, i, more, far):
                    act_out_of_psum(t, i)
                    if more:
                        silu(t + 1, i + 1)
                    if far:
                        rows_out_of_psum(t + 2, i + 2)
                over_tiles(act, one)

            @block.gpsimd
            def _(gp):
                def mask(b, h, q, g):
                    unit = E_TOT * (2 * b + h) + E_AT[q, g] + E_UNITS[q] // GH
                    block_ = pool[:, q % 2, g * QT + q, :].rearrange("p (r t) -> p r t", r=REP)
                    gp.wait_ge(s["st_free"], 2 + unit)
                    gp.nop(nofuse=True)
                    nc.gpsimd.affine_select(out=block_, in_=block_, compare_op=ALU.is_ge, fill=0.0, base=0,
                                            pattern=[[0, REP], [1, P]], channel_multiplier=-1).then_inc(s["p_ready"], 1)

                def split(b, h, q, use):
                    u = 2 * b + h
                    t8 = 8 + 16 * u + 4 * q
                    row, to = nm_rows[q % 2], nm_parts[q % 2]
                    gp.wait_ge(s["misc_free"], 1 + use + 1)
                    gp.wait_ge(nm_in[q % 2], 16 + 48 * (2 * u + q // 2))
                    gp.nop(nofuse=True)
                    nc.gpsimd.tensor_copy(to[:, 0, :], row[:, :]).then_inc(s["nm_split"], 1)
                    gp.wait_ge(s["nm_split"], t8 + 1)
                    nc.gpsimd.tensor_tensor(nm_res[:, :], row[:, :], to[:, 0, :], ALU.subtract).then_inc(s["nm_split"], 1)
                    gp.wait_ge(s["nm_split"], t8 + 2)
                    gp.nop(nofuse=True)
                    nc.gpsimd.tensor_copy(to[:, 1, :], nm_res[:, :]).then_inc(s["nm_split"], 1)
                    gp.wait_ge(s["nm_split"], t8 + 3)
                    nc.gpsimd.tensor_tensor(to[:, 2, :], nm_res[:, :], to[:, 1, :], ALU.subtract).then_inc(s["nm_split"], 1)
                    gp.wait_ge(s["nm_split"], t8 + 4)

                def half(b, h, nxt=True):
                    for q in range(QT):
                        for g in range(GH):
                            mask(b, h, q, g)
                            if g == 2 and q == 0:
                                split(b, h, QT - 1, turn_use(b, h, QT - 1))
                            elif g == 2 and nxt:
                                split(b + h, 1 - h, q - 1, turn_use(b, h, q - 1))
                for q in range(QT - 1):
                    split(0, 0, q, q)
                half(0, 0)
                with gp.Fori(0, B - 1) as b:
                    half(b, 1)
                    half(b + 1, 0)
                half(B - 1, 1, nxt=False)

                gp.wait_ge(s["st_ready"], E_TOT * 2 * B)
                gp.wait_ge(k_in[1], 32 * B)
                nc.gpsimd.memset(fill[:, :], 0.0).then_inc(s["numbered"], 1)
                gp.wait_ge(s["numbered"], 1)
                nc.gpsimd.tensor_scalar(fill[:, D:D + 1], PLACE["partition"], float(B * T), None,
                                        ALU.add).then_inc(s["filled"], 1)
                nc.gpsimd.tensor_copy(rows[:, :, D], PLACE["token"]).then_inc(s["numbered"], 1)
                nc.gpsimd.tensor_copy(taken[:, :], PLACE["first"]).then_inc(s["numbered"], 1)
                nc.gpsimd.memset(w_down[1], 0.0).then_inc(s["wd_zero"], 1)
                gp.wait_ge(s["numbered"], 3)
                for m in range(B):
                    gp.wait_ge(s["routed"], m + 1)
                    for i in range(QT):
                        for k in range(TOPK):
                            t = m * QT + i
                            gp.indirect_dma_start(x_rows, bass.IndirectOffsetOnAxis(ap=slots[:, t, k:k + 1], axis=0),
                                                  rows[:, t, :], None).then_inc(s["rows_out"], 16)

                def add_rows(t, i, done):
                    gp.wait_ge(s["yo_ready"], 2 + t + 1)
                    if not isinstance(t, int) or t >= 2:
                        gp.wait_ge(scat[i % 2], done)
                    gp.nop(nofuse=True)
                    gp.indirect_dma_start(y_sum[i % 2], bass.IndirectOffsetOnAxis(ap=token_no[i % STEPS][:, :], axis=0),
                                          yo[i % STEPS], None, compute_op=ALU.add).then_inc(scat[i % 2], 16)

                gp.wait_ge(s["y_zero"], 32)
                for h in range(2):
                    gp.wait_ge(ys_out[h], 16 * B)
                for t in range(STEPS):
                    add_rows(t, t, 16 * (t // 2))
                with gp.Fori(1, TURNS_) as trip:
                    for i in range(STEPS):
                        add_rows(STEPS * trip + i, i, 32 * trip + 16 * (i // 2))
                for t in range(STEPS * TURNS_, TILES):
                    add_rows(t, t, 16 * (t // 2))

            @block.vector
            def _(dve):
                for name, n in (("s_free", 2), ("st_free", 2), ("av_done", 2), ("o_free", 1), ("misc_free", 1),
                                ("x2_ready", 1), ("y_ready", 1), ("nm_split", 8)):
                    nc.vector.memset(credit(), 0.0).then_inc(s[name], n)
                for one in (*nm_in, *y_out):
                    nc.vector.memset(credit(), 0.0).then_inc(one, 16)

                def maxima(b, h, q, g):
                    u = 2 * b + h
                    heads, n = s_banks(q)
                    for k in range(s_units(q, g)):
                        unit = S_TOT * u + S_AT[q, g] + k
                        dve.wait_ge(s["s_ready"], unit + 1)
                        buf = 2 * ((S_AT[q, g] + k) % 2)
                        view = bank[:, buf:buf + 2, 0:heads * n].rearrange("p j (i n) -> p j i n", i=heads)
                        head = s_heads(q, g, k)
                        to = negm[h][:, q, head:head + 2 * heads].rearrange("p (j i) -> p j i", j=2)
                        nc.vector.tensor_reduce(to, view, AX.X, ALU.max, negate=True).then_inc(s["s_free"], 1)

                def take_max(b, h, q, use):
                    u = 2 * b + h
                    dve.wait_ge(s["misc_ready"], use + 1)
                    dve.wait_ge(s["nm_split"], 16 * u + 4 * q + 4)
                    nc.vector.tensor_copy(nm_rows[q % 2][:, :], bank[0:HH, MISC, 0:P]).then_inc(s["misc_free"], 1)

                def residual(b, w, use):
                    dve.wait_ge(s["misc_ready"], use + 1)
                    dve.wait_ge(s["x2_ready"], 2 * b + w + 1)
                    g1 = gate_bc[:, bass.ds(b, 1), 0, :].to_broadcast([P, 2, D])
                    xt = X[:, bass.ds(b * QT + 2 * w, 2), :]
                    nc.vector.tensor_tensor(prod[:, :, :], bank[:, MISC, :].rearrange("p (i d) -> p i d", i=2), g1,
                                            ALU.mult).then_inc(s["misc_free"], 1)
                    dve.wait_ge(s["misc_free"], 1 + use + 1)
                    nc.vector.tensor_tensor(xt, xt, prod[:, :, :], ALU.add).then_inc(s["x2_ready"], 1)

                def half(b, h, nxt=True, back=True):
                    for q in range(QT):
                        for g in range(GH):
                            if nxt:
                                maxima(b + h, 1 - h, q, g)
                            if q == 3 and g < 2 and back:
                                invert(dve, *prev(b, h), 2 * g)
                                invert(dve, *prev(b, h), 2 * g + 1)
                            if q == 3 and g == 2 and back:
                                normalise(dve, *prev(b, h))
                            if g == 2 and q == 0:
                                take_max(b, h, QT - 1, turn_use(b, h, QT - 1))
                            elif g == 2 and nxt:
                                take_max(b + h, 1 - h, q - 1, turn_use(b, h, q - 1))
                            if h == 0 and back and q == 3 and g >= 2:
                                residual(b - 1, g - 2, project_use(b, g))

                for q in range(QT):
                    for g in range(GH):
                        maxima(0, 0, q, g)
                    if q > 0:
                        take_max(0, 0, q - 1, q - 1)
                half(0, 0, back=False)
                with dve.Fori(0, B - 1) as b:
                    half(b, 1)
                    half(b + 1, 0)
                half(B - 1, 1, nxt=False)
                dve.wait_ge(k_in[1], 32 * B)
                norm_start(dve, 0, B - 1)
                norm_end(dve, 0, B - 1)

                count = [0]

                def step(ins):
                    count[0] += 1
                    ins.then_inc(s["route"], 1)
                    dve.wait_ge(s["route"], count[0])

                def over(a, k):
                    return a.unsqueeze(2).to_broadcast([P, QT, k])

                expd, score, msk, rank, sel, w, pos, tmp = (rt[:, i] for i in range(8))
                mx, total, inv, kept = (few[:, i, 0:QT] for i in range(4))

                def before(v, k, to):
                    mine = v[:, :, 0:k].unsqueeze(3).to_broadcast([P, QT, k, k])
                    other = v[:, :, 0:k].unsqueeze(2).to_broadcast([P, QT, k, k])
                    tri = earlier[:, 0:k, 0:k].unsqueeze(1).to_broadcast([P, QT, k, k])
                    greater, equal = (c.rearrange("p a b -> p (a b)")[:, 0:QT * k * k]
                                      .rearrange("p (t i j) -> p t i j", t=QT, i=k) for c in cmp)
                    step(nc.vector.tensor_tensor(greater, other, mine, ALU.is_gt))
                    step(nc.vector.tensor_tensor(equal, other, mine, ALU.is_equal))
                    step(nc.vector.tensor_tensor(equal, equal, tri, ALU.mult))
                    step(nc.vector.tensor_tensor(greater, greater, equal, ALU.add))
                    step(nc.vector.tensor_reduce(to[:, :, 0:k], greater, AX.X, ALU.add))

                def begin(m):
                    dve.wait_ge(s["lg_ready"], m + 1)
                    lg = logit[:, m * QT:m * QT + QT, :]
                    step(nc.vector.tensor_reduce(mx, lg, AX.X, ALU.max))
                    nc.vector.tensor_tensor(expd, lg, over(mx, E), ALU.subtract).then_inc(s["subtracted"], 1)

                def choose(m):
                    dve.wait_ge(s["exp_l"], m + 1)
                    step(nc.vector.tensor_reduce(total, expd, AX.X, ALU.add))
                    step(nc.vector.reciprocal(inv, total))
                    step(nc.vector.tensor_tensor(score, expd, over(inv, E), ALU.mult))
                    by_group = score.rearrange("p t (g e) -> p t g e", g=G)
                    step(nc.vector.tensor_reduce(tmp[:, :, 0:G], by_group, AX.X, ALU.max))
                    before(tmp, G, rank)
                    step(nc.vector.tensor_scalar(tmp[:, :, 0:G], rank[:, :, 0:G], float(TOPG), None, ALU.is_lt))
                    step(nc.vector.tensor_tensor(msk.rearrange("p t (g e) -> p t g e", g=G), by_group,
                                                 tmp[:, :, 0:G].unsqueeze(3).to_broadcast([P, QT, G, E // G]),
                                                 ALU.mult))
                    before(msk, E, rank)
                    if m > 0:
                        dve.wait_ge(s["pos_done"], m)
                    nc.vector.tensor_scalar(sel_bf[:, :, :], rank, float(TOPK), None,
                                            ALU.is_lt).then_inc(s["sel_ready"], 1)
                    step(nc.vector.tensor_scalar(sel, rank, float(TOPK), None, ALU.is_lt))
                    step(nc.vector.tensor_tensor(w, msk, sel, ALU.mult))
                    step(nc.vector.tensor_reduce(kept, w, AX.X, ALU.add))
                    step(nc.vector.tensor_scalar(mx, kept, 1e-20, None, ALU.add))
                    step(nc.vector.reciprocal(inv, mx))
                    step(nc.vector.tensor_tensor(rows[:, m * QT:m * QT + QT, D + 1:ROW], w, over(inv, E), ALU.mult))

                def place(m):
                    dve.wait_ge(s["pos_done"], m + 1)
                    ps = bank[:, 6, 0:QT * E].rearrange("p (t e) -> p t e", t=QT)
                    step(nc.vector.tensor_tensor(pos, ps, taken[:, :].unsqueeze(1).to_broadcast([P, QT, E]), ALU.add))
                    nc.vector.tensor_tensor(taken[:, :], taken[:, :], bank[:, 6, QT * E:QT * E + E],
                                            ALU.add).then_inc(s["pos_used"], 1)
                    dve.wait_ge(s["pos_used"], m + 1)
                    if m == B - 1:
                        nc.vector.tensor_copy(pad_row[:, :], taken[0:1, :]).then_inc(s["run_done"], 1)
                    wide = [P, QT, TOPK, E]
                    step(nc.vector.tensor_tensor(big[:, :, :, :], rank.unsqueeze(2).to_broadcast(wide),
                                                 PLACE["slot"].unsqueeze(1).unsqueeze(3).to_broadcast(wide),
                                                 ALU.is_equal))
                    step(nc.vector.tensor_tensor(big[:, :, :, :], big[:, :, :, :], pos.unsqueeze(2).to_broadcast(wide),
                                                 ALU.mult))
                    step(nc.vector.tensor_reduce(slot_f[:, :, :], big[:, :, :, :], AX.X, ALU.add))
                    nc.vector.tensor_copy(slots[:, m * QT:m * QT + QT, :], slot_f[:, :, :]).then_inc(s["routed"], 1)

                def last_residual(w):
                    dve.wait_ge(s["y_mm"], w + 1)
                    g1 = gate_bc[:, B - 1, 0, :].unsqueeze(1).to_broadcast([P, 2, D])
                    t = (B - 1) * QT + 2 * w
                    nc.vector.tensor_tensor(prod[:, :, :], bank[:, 7 - w, :].rearrange("p (i d) -> p i d", i=2), g1,
                                            ALU.mult).then_inc(s["added"], 1)
                    dve.wait_ge(s["added"], 2 * w + 1)
                    nc.vector.tensor_tensor(X[:, t:t + 2, :], X[:, t:t + 2, :], prod[:, :, :],
                                            ALU.add).then_inc(s["added"], 1)
                    dve.wait_ge(s["added"], 2 * w + 2)

                def shared_gated(n):
                    for k, w in enumerate(SCHUNKS):
                        dve.wait_ge(s["sh_silu"], 3 * n + k + 1)
                        if n >= 2:
                            dve.wait_ge(s["sh_down"], 2 * n - 2)
                        nc.vector.tensor_tensor(aT[n % 2][0:w, k, :], bank[0:w, 2 * k + 1, :], sg[k][0:w],
                                                ALU.mult).then_inc(s["sh_a"], 1)

                def tables():
                    n, tiles, start, end = (few[:, i, :] for i in range(4, 8))
                    step(nc.vector.tensor_tensor(n, taken[:, :], PLACE["first"], ALU.subtract))
                    square = [P, E, E]
                    ee = cmp[0][:, 0:E, :]
                    step(nc.vector.tensor_tensor(ee, n.unsqueeze(2).to_broadcast(square),
                                                 PLACE["k128"].unsqueeze(1).to_broadcast(square), ALU.is_gt))
                    step(nc.vector.tensor_reduce(tiles, ee, AX.X, ALU.add))
                    step(nc.vector.tensor_tensor(ee, earlier[:, :, :], tiles.unsqueeze(1).to_broadcast(square),
                                                 ALU.mult))
                    step(nc.vector.tensor_reduce(start, ee, AX.X, ALU.add))
                    step(nc.vector.tensor_tensor(end, start, tiles, ALU.add))
                    wide = [1, TILES, E]
                    past, weighed = (c[0:1, 0:TILES, :] for c in cmp)
                    step(nc.vector.tensor_tensor(past, PLACE["tile"][0:1].unsqueeze(2).to_broadcast(wide),
                                                 end[0:1].unsqueeze(1).to_broadcast(wide), ALU.is_ge))
                    step(nc.vector.tensor_tensor(weighed, past, tiles[0:1].unsqueeze(1).to_broadcast(wide), ALU.mult))
                    step(nc.vector.tensor_reduce(tab[:, 0, :], past, AX.X, ALU.add))
                    step(nc.vector.tensor_reduce(tab[:, 1, :], weighed, AX.X, ALU.add))
                    step(nc.vector.scalar_tensor_tensor(out=tab[:, 2, :], in0=tab[:, 1, :], scalar=-float(P),
                                                        in1=PLACE["tile128"][0:1], op0=ALU.mult, op1=ALU.add))
                    step(nc.vector.scalar_tensor_tensor(out=tab[:, 1, :], in0=tab[:, 0, :], scalar=float(REGION),
                                                        in1=tab[:, 2, :], op0=ALU.mult, op1=ALU.add))
                    step(nc.vector.tensor_scalar(tile_row[:, :], tab[:, 1, :], float(DUMMY), None, ALU.min))
                    nc.vector.tensor_scalar(tile_expert[:, :], tab[:, 0, :], float(E - 1), None,
                                            ALU.min).then_inc(s["table"], 1)

                dve.wait_ge(s["numbered"], 3)
                begin(0)
                for m in range(B):
                    choose(m)
                    if m == 1:
                        last_residual(0)
                        last_residual(1)
                    place(m)
                    if m + 1 < B:
                        begin(m + 1)
                    if m == 0:
                        dve.wait_ge(y_in[1], 32 * B)
                        for q in range(QT):
                            invert(dve, B - 1, 1, q)
                        normalise(dve, B - 1, 1)
                    shared_gated(m)
                    if m == 1:
                        norm_start(dve, B - 1, B)
                        norm_end(dve, B - 1, B)
                tables()

                dve.wait_ge(s["sh_down"], 2 * B)
                for i in range(2):
                    last = nc.vector.memset(actT[i][:, 1, :], 0.0)
                last.then_inc(s["cleared"], 1)
                for name in "tx_done xT_ready up_done silu_done a_ready ta_done aT_ready dn_done yo_ready".split():
                    nc.vector.memset(credit(), 0.0).then_inc(s[name], 2)

                def extras(t, i, ins, done):
                    e = dve.value_load(tile_expert[0:1, bass.ds(t, 1)], min_val=0, max_val=E - 1)
                    dve.wait_ge(xt_in[i % STEPS], ins)
                    if not isinstance(t, int) or t >= STEPS:
                        dve.wait_ge(scat[i % 2], done)
                    nc.vector.tensor_copy(token_no[i % STEPS][:, :], xt[i % STEPS][:, D:D + 1])
                    nc.vector.tensor_copy(weight[i % STEPS][:, :],
                                          xt[i % STEPS][:, bass.ds(e + D + 1, 1)]).then_inc(s["extra"], 1)

                def gated(t, i):
                    dve.wait_ge(s["silu_done"], 2 + t + 1)
                    nc.vector.tensor_tensor(act_g[i % 2], bank[:, 2 + i % 2, I:2 * I], act_g[i % 2],
                                            ALU.mult).then_inc(s["a_ready"], 1)

                def weigh(t, i):
                    dve.wait_ge(s["dn_done"], 2 + t + 1)
                    nc.vector.tensor_scalar(yo[i % STEPS], bank[:, 6 + i % 2, 0:D], weight[i % STEPS][:, :], None,
                                            ALU.mult).then_inc(s["yo_ready"], 1)

                dve.wait_ge(s["table"], 1)
                extras(0, 0, 16, 0)
                extras(1, 1, 16, 0)
                gated(0, 0)

                def turn_of(trip):
                    for i in range(STEPS):
                        t = STEPS * trip + i
                        extras(t + 2, i + 2, 16 * trip + 16 * ((i + 2) // STEPS) + 16,
                               32 * trip + 16 * ((i + 2) // 2) - 16)
                        gated(t + 1, i + 1)
                        weigh(t, i)
                turn_of(0)
                with dve.Fori(1, TURNS_) as trip:
                    turn_of(trip)
                for t in range(STEPS * TURNS_, TILES):
                    if t + 2 < TILES:
                        extras(t + 2, t + 2, 16 * ((t + 2) // STEPS) + 16, 16 * ((t + 2) // 2) - 16)
                    if t + 1 < TILES:
                        gated(t + 1, t + 1)
                    weigh(t, t)

                for b in range(B):
                    x_b = X[:, b * QT:b * QT + QT, :]
                    g2 = gate_bc[:, b, 1, :].unsqueeze(1).to_broadcast([P, QT, D])
                    dve.wait_ge(back[b], 32)
                    nc.vector.tensor_tensor(y_back[:, b, 0], y_back[:, b, 0], y_back[:, b, 1],
                                            ALU.add).then_inc(s["fin"], 1)
                    dve.wait_ge(s["fin"], 3 * b + 1)
                    nc.vector.tensor_tensor(y_back[:, b, 0], y_back[:, b, 0], g2, ALU.mult).then_inc(s["fin"], 1)
                    dve.wait_ge(s["fin"], 3 * b + 2)
                    nc.vector.tensor_tensor(x_b, x_b, y_back[:, b, 0], ALU.add).then_inc(s["fin"], 1)


def kernel(L0_attn_x, L0_attn_wq, L0_attn_wk, L0_attn_wv, L0_attn_wo, L0_ffn_gate_w, L0_ffn_expert_up_w,
           L0_ffn_expert_down_w, L0_ffn_shared_up_w, L0_ffn_shared_down_w, L0_c, L0_wmod):
    import numpy as np
    import concourse.bacc as bacc
    from concourse.bass_utils import run_bass_kernel_spmd

    def cols(w, *dims, order):
        a = np.asarray(w)
        n = a.shape[0]
        return a.reshape(n, *dims).transpose(0, *(1 + i for i in order)).reshape(n, -1)

    a = np.asarray
    wq = cols(L0_attn_wq, 2, HH, HD, order=(0, 2, 1))
    wk = cols(L0_attn_wk, 2, GH, HD, order=(0, 2, 1))
    arrays = {
        "x": a(L0_attn_x), "wq": wq, "wk": wk, "wv": a(L0_attn_wv), "wo": a(L0_attn_wo),
        "gate_t": a(L0_ffn_gate_w).T, "up_t": a(L0_ffn_expert_up_w).transpose(0, 2, 1),
        "down_t": a(L0_ffn_expert_down_w).transpose(0, 2, 1), "shared_up_t": a(L0_ffn_shared_up_w).T,
        "shared_down_t": a(L0_ffn_shared_down_w).T, "c_t": a(L0_c).T, "wmod": a(L0_wmod),
    }
    arrays = {k: np.ascontiguousarray(v) for k, v in arrays.items()}
    nc = bacc.Bacc("TRN2", target_bir_lowering=False, num_devices=1)
    args = [nc.dram_tensor(k, v.shape, mybir.dt.from_np(v.dtype), kind="ExternalInput").ap() for k, v in arrays.items()]
    out = nc.dram_tensor("out", (B, T, D), F32, kind="ExternalOutput").ap()
    adaln_block(nc, *args, out)
    r = run_bass_kernel_spmd(nc, [arrays], core_ids=[0])
    return r.results[0]["out"]
```
